# Optimizing a Trainium2 kernel written in Bass

```python
import numpy as np
import jax
import jax.numpy as jnp

def _softmax(x, axis=-1):
    return jax.nn.softmax(x, axis=axis)

def _gelu(x):
    return jax.nn.gelu(x, approximate=True)

def _silu(x):
    return jax.nn.silu(x)

def _sigmoid(x):
    return jax.nn.sigmoid(x)

def _layernorm(x, axis=-1, eps=1e-05):
    m = jnp.mean(x, axis=axis, keepdims=True)
    v = jnp.var(x, axis=axis, keepdims=True)
    return (x - m) / jnp.sqrt(v + eps)

def _scatter_add(tgt, idx, src, axis=0):
    return tgt.at[idx].add(src)

def _segment_sum(src, seg, n):
    return jax.ops.segment_sum(src, seg, n)
kernel_name = 'mk_seq_preln_d1_jaxref_r4_531247'

def setup_inputs(seed: int=0):
    np.random.seed(seed)
    _w = jnp.asarray

    def _L0_attn_setup():
        import jax, jax.numpy as jnp
        import numpy as np
        D_MODEL = 256
        NHEAD = 16
        HEAD_DIM = D_MODEL // NHEAD
        key = jax.random.key(seed)
        ks = jax.random.split(key, 5)
        s = 1.0 / np.sqrt(D_MODEL)
        x = jax.random.normal(ks[0], (4, 512, D_MODEL), dtype=jnp.float32)
        W_qkv = jax.random.uniform(ks[1], (D_MODEL, 3 * D_MODEL), jnp.float32, -s, s)
        b_qkv = jax.random.uniform(ks[2], (3 * D_MODEL,), jnp.float32, -s, s)
        W_out = jax.random.uniform(ks[3], (D_MODEL, D_MODEL), jnp.float32, -s, s)
        b_out = jax.random.uniform(ks[4], (D_MODEL,), jnp.float32, -s, s)
        return {'x': x, 'W_qkv': W_qkv, 'b_qkv': b_qkv, 'W_out': W_out, 'b_out': b_out}
    _L0_attn_in = _L0_attn_setup()

    def _L0_ffn_setup():
        import jax, jax.numpy as jnp
        import numpy as np
        B, L, D, H, E, TOP_K = (4, 512, 256, 1024, 8, 2)
        LN_EPS = 1e-05
        key = jax.random.key(seed)
        ks = jax.random.split(key, 8)
        x = jax.random.normal(ks[0], (B, L, D), dtype=jnp.float32)
        gate_w = jax.random.normal(ks[1], (D, E), dtype=jnp.float32) / np.sqrt(D)
        w1 = jax.random.normal(ks[2], (E, D, H), dtype=jnp.float32) / np.sqrt(D)
        b1 = jnp.zeros((E, H), dtype=jnp.float32)
        w2 = jax.random.normal(ks[3], (E, H, D), dtype=jnp.float32) / np.sqrt(H)
        b2 = jnp.zeros((E, D), dtype=jnp.float32)
        gamma = jnp.ones((D,), dtype=jnp.float32)
        beta = jnp.zeros((D,), dtype=jnp.float32)
        return {'x': x, 'gate_w': gate_w, 'w1': w1, 'b1': b1, 'w2': w2, 'b2': b2, 'gamma': gamma, 'beta': beta}
    _L0_ffn_in = _L0_ffn_setup()
    _d = {'L0_attn_x': _L0_attn_in['x'], 'L0_attn_W_qkv': _L0_attn_in['W_qkv'], 'L0_attn_b_qkv': _L0_attn_in['b_qkv'], 'L0_attn_W_out': _L0_attn_in['W_out'], 'L0_attn_b_out': _L0_attn_in['b_out'], 'L0_ffn_gate_w': _L0_ffn_in['gate_w'], 'L0_ffn_w1': _L0_ffn_in['w1'], 'L0_ffn_b1': _L0_ffn_in['b1'], 'L0_ffn_w2': _L0_ffn_in['w2'], 'L0_ffn_b2': _L0_ffn_in['b2'], 'L0_ffn_gamma': _L0_ffn_in['gamma'], 'L0_ffn_beta': _L0_ffn_in['beta']}
    _x0 = _d['L0_attn_x']
    _d['L0_attn_x'] = jax.random.normal(jax.random.fold_in(jax.random.key(seed), 1), (8, 512, 256), dtype=_x0.dtype)
    del _x0
    return _d

def reference(L0_attn_x, L0_attn_W_qkv, L0_attn_b_qkv, L0_attn_W_out, L0_attn_b_out, L0_ffn_gate_w, L0_ffn_w1, L0_ffn_b1, L0_ffn_w2, L0_ffn_b2, L0_ffn_gamma, L0_ffn_beta):

    def _L0_attn_ref(x, W_qkv, b_qkv, W_out, b_out):
        import jax, jax.numpy as jnp
        import numpy as np
        D_MODEL = 256
        NHEAD = 16
        HEAD_DIM = D_MODEL // NHEAD
        B, S, _ = x.shape
        scale = HEAD_DIM ** (-0.5)
        qkv = x @ W_qkv + b_qkv
        qkv = qkv.reshape(B, S, 3, NHEAD, HEAD_DIM)
        q = qkv[:, :, 0].transpose(0, 2, 1, 3)
        k = qkv[:, :, 1].transpose(0, 2, 1, 3)
        v = qkv[:, :, 2].transpose(0, 2, 1, 3)
        scores = jnp.einsum('bhqd,bhkd->bhqk', q, k) * scale
        causal = jnp.triu(jnp.ones((S, S), dtype=bool), k=1)
        scores = jnp.where(causal[None, None], -jnp.inf, scores)
        attn = jax.nn.softmax(scores, axis=-1)
        out = jnp.einsum('bhqk,bhkd->bhqd', attn, v)
        out = out.transpose(0, 2, 1, 3).reshape(B, S, D_MODEL)
        return out @ W_out + b_out

    def _L0_ffn_ref(x, gate_w, w1, b1, w2, b2, gamma, beta):
        import jax, jax.numpy as jnp
        import numpy as np
        B, L, D, H, E, TOP_K = (4, 512, 256, 1024, 8, 2)
        LN_EPS = 1e-05
        residual = x
        mu = jnp.mean(x, axis=-1, keepdims=True)
        var = jnp.mean(jnp.square(x - mu), axis=-1, keepdims=True)
        xn = (x - mu) * jax.lax.rsqrt(var + LN_EPS) * gamma + beta
        probs = jax.nn.softmax(jnp.einsum('bld,de->ble', xn, gate_w), axis=-1)
        w, idx = jax.lax.top_k(probs, TOP_K)
        w = w / jnp.sum(w, axis=-1, keepdims=True)
        cw = jnp.sum(w[..., None] * jax.nn.one_hot(idx, E, dtype=x.dtype), axis=2)
        h = jax.nn.gelu(jnp.einsum('bld,edh->eblh', xn, w1) + b1[:, None, None, :], approximate=False)
        out_e = jnp.einsum('eblh,ehd->ebld', h, w2) + b2[:, None, None, :]
        output = jnp.einsum('ble,ebld->bld', cw, out_e)
        return output + residual
    x = L0_attn_x
    x = x + _L0_attn_ref(_layernorm(x, axis=-1), L0_attn_W_qkv, L0_attn_b_qkv, L0_attn_W_out, L0_attn_b_out)
    x = x + _L0_ffn_ref(_layernorm(x, axis=-1), L0_ffn_gate_w, L0_ffn_w1, L0_ffn_b1, L0_ffn_w2, L0_ffn_b2, L0_ffn_gamma, L0_ffn_beta)
    return x

_drawn_inputs = setup_inputs


def setup_inputs(seed=0):
    import zlib

    import numpy as np

    out = dict(_drawn_inputs(seed))
    spreads = {'L0_ffn_b1': (0.0, 0.314),
     'L0_ffn_b2': (0.0, 0.1),
     'L0_ffn_gamma': (1.0, 0.2),
     'L0_ffn_beta': (0.0, 0.1)}
    factors = {}
    for name, (base, spread) in spreads.items():
        noise = np.random.default_rng([zlib.crc32(name.encode()), seed]).standard_normal(out[name].shape)
        drawn = base * np.exp(spread * noise) if base else spread * noise
        out[name] = jnp.asarray(drawn.astype(out[name].dtype))
    for name, factor in factors.items():
        out[name] = (out[name] * factor).astype(out[name].dtype)
    return out
```

```python
import math
from contextlib import ExitStack

import concourse.bass as bass
import concourse.mybir as mybir

ALU = mybir.AluOpType
ACT = mybir.ActivationFunctionType
AX = mybir.AxisListType
F32 = mybir.dt.float32
F16 = mybir.dt.float16
BF16 = mybir.dt.bfloat16
I32 = mybir.dt.int32

P = 128
NEG = -1.0e30
EPS = 1e-5


class Signal:

    def __init__(self, sem):
        self.sem, self.count = sem, 0

    def after(self, step):
        self.count += step
        return self, self.count


class Lane:

    def __init__(self, signals):
        self.items, self.signals, self.seen = [], signals, {}

    def do(self, emit, name=None):
        if name is None:
            self.items.append(emit)
            return None
        mark = self.signals(name).after(1)
        self.items.append(lambda e: emit(e).then_inc(mark[0].sem, 1))
        return mark

    def dma(self, out, in_, name, **how):
        mark = self.signals(name).after(16)
        self.items.append(lambda e: e.dma_start(out, in_, **how).then_inc(mark[0].sem, 16))
        return mark

    def indirect(self, name, *what, **how):
        mark = self.signals(name).after(16)
        self.items.append(lambda e: e.indirect_dma_start(*what, **how).then_inc(mark[0].sem, 16))
        return mark

    def wait(self, *marks):
        for mark in marks:
            if mark is None or self.seen.get(mark[0], 0) >= mark[1]:
                continue
            self.seen[mark[0]] = mark[1]
            self.items.append(lambda e, mark=mark: e.wait_ge(mark[0].sem, mark[1]))

    def play(self, engine):
        for item in self.items:
            item(engine)


class Ring:

    def __init__(self, buffers):
        self.buffers, self.free, self.next = buffers, [()] * len(buffers), 0

    def take(self, lane):
        n = self.next % len(self.buffers)
        self.next += 1
        lane.wait(*self.free[n])
        return n, self.buffers[n]

    def give(self, n, *marks):
        self.free[n] = marks


def build(nc, t, debug=None):
    B, T, D = t["L0_attn_x"].shape
    E, _, F = t["L0_ffn_w1"].shape
    HD = 16
    H = D // HD
    SCALE = HD ** -0.5
    KC = D // P
    FC = F // P
    TT = T // P
    NT = B * TT
    N = B * T
    HG = 4
    NG = H // HG
    TOPK = 2
    TILE = 256
    TC = TILE // P
    TILES = N * TOPK // TILE + E - 1
    SC = TILES * TC
    ROW = D + E
    Q_PARTS = (0, 1, 0, 2, 1, 0)
    K_PARTS = (0, 0, 1, 0, 1, 2)
    STACK = len(Q_PARTS) * HD
    MAXROWS = 3
    EW = 2 * KC * F

    ctx = ExitStack()
    with ctx:
        pool = {}

        def signals(name):
            if name not in pool:
                pool[name] = Signal(ctx.enter_context(nc.semaphore(name)))
            return pool[name]

        PE, ACTE, DVE, POOL, SP = (Lane(signals) for _ in range(5))
        LANES = (PE, ACTE, DVE, POOL, SP)

        def dram(name, shape, dt):
            return nc.dram_tensor(name, shape, dt).ap()

        qk_dram = dram("qk_parts", (2, 3, B, D, T), BF16)
        v_dram = dram("v_rows", (B, T, D), F32)
        rows_dram = dram("token_rows", (N + P, ROW), F32)
        acc_dram = dram("result_rows", (N + P, D), F32)

        weights = ctx.enter_context(nc.sbuf_tensor("weights", [P, E * EW], F32))
        WORDS = 20400
        arena = ctx.enter_context(nc.sbuf_tensor("arena", [P, WORDS], F32))
        banks = ctx.enter_context(nc.psum_tensor("banks", [P, 8, 512], F32))

        class Area:

            def __init__(self, base, start, end):
                self.base, self.at, self.end = base, start, end

            def take(self, words, dt=F32, **dims):
                a, self.at = self.at, self.at + words
                assert self.at <= self.end, (self.at, self.end)
                v = self.base[:, a:a + words]
                if dt != F32:
                    v = v.bitcast(dt)
                if dims:
                    names = list(dims)
                    v = v.rearrange(f"p ({' '.join(names)}) -> p {' '.join(names)}",
                                    **{k: dims[k] for k in names[1:]})
                return v

        keep = Area(arena, 0, 3000)
        ident = keep.take(P)
        ident_b = keep.take(P // 2, BF16)
        mask_b = keep.take(P // 2, BF16)
        upper_b = keep.take(P // 2, BF16)
        ones_b = keep.take(P // 2, BF16)
        iota_row = keep.take(P)
        iota_part = keep.take(1)
        prefer = keep.take(E)
        gamma = keep.take(D)
        beta = keep.take(D)
        b_out = keep.take(D)
        w_out = keep.take(KC * D, k=KC, n=D)
        gate_w = keep.take(KC * E, k=KC, e=E)
        choice = keep.take(NT * TOPK * E, i=NT, k=TOPK, e=E)
        b1_sb = keep.take(E * FC, e=E, c=FC)
        stat = keep.take(64)
        hot = keep.take(TILES * E, j=TILES, e=E)
        tile_of = keep.take(TILES, I32)
        slot_token = keep.take(SC, I32)

        HEAD = keep.at
        c_zero = POOL.do(lambda e: e.memset(arena[:, 0:2 * P], 0.0), "const")
        c_ones = POOL.do(lambda e: e.memset(ones_b, 1.0), "const")
        c_upper = POOL.do(lambda e: e.memset(upper_b, 1.0), "const")
        POOL.wait(c_zero, c_ones, c_upper)
        POOL.do(lambda e: e.affine_select(out=ident, in_=ident, compare_op=ALU.not_equal, fill=1.0,
                                          base=0, pattern=[[-1, P]], channel_multiplier=1), "const")
        POOL.do(lambda e: e.affine_select(out=ident_b, in_=ident_b, compare_op=ALU.not_equal, fill=1.0,
                                          base=0, pattern=[[-1, P]], channel_multiplier=1), "const")
        POOL.do(lambda e: e.affine_select(out=mask_b, in_=mask_b, compare_op=ALU.is_ge, fill=NEG,
                                          base=0, pattern=[[-1, P]], channel_multiplier=1), "const")
        POOL.do(lambda e: e.affine_select(out=upper_b, in_=upper_b, compare_op=ALU.is_gt, fill=0.0,
                                          base=0, pattern=[[1, P]], channel_multiplier=-1), "const")
        POOL.do(lambda e: e.iota(b_out[:, 0:P].bitcast(I32), [[1, P]], base=0, channel_multiplier=0), "const")
        POOL.do(lambda e: e.iota(b_out[:, P:P + 1].bitcast(I32), [[0, 1]], base=0, channel_multiplier=1), "const")
        consts_pool = POOL.do(lambda e: e.iota(b_out[:, P + 1:P + 1 + E].bitcast(I32), [[-1, E]], base=E,
                                               channel_multiplier=0), "const")
        DVE.wait(consts_pool)
        DVE.do(lambda e: e.tensor_copy(iota_row, b_out[:, 0:P].bitcast(I32)), "numbers")
        DVE.do(lambda e: e.tensor_copy(iota_part, b_out[:, P:P + 1].bitcast(I32)), "numbers")
        numbers = DVE.do(lambda e: e.tensor_copy(prefer, b_out[:, P + 1:P + 1 + E].bitcast(I32)), "numbers")

        def rows_of(vector):
            return vector.partition_broadcast(P)

        def rsqrt(var, scratch, name):
            s, y, u = scratch
            m = DVE.do(lambda e: e.tensor_scalar(s, var, EPS, None, ALU.add), name)
            DVE.wait(m)
            m = DVE.do(lambda e: e.tensor_scalar(y.bitcast(I32), s.bitcast(I32), 1, None,
                                                 ALU.logical_shift_right), name)
            DVE.wait(m)
            m = DVE.do(lambda e: e.tensor_scalar(y.bitcast(I32), y.bitcast(I32), -1.0, float(0x5F3759DF),
                                                 ALU.mult, ALU.add), name)
            for _ in range(4):
                DVE.wait(m)
                m = DVE.do(lambda e: e.scalar_tensor_tensor(u, y, -0.5, y, ALU.mult, ALU.mult), name)
                DVE.wait(m)
                m = DVE.do(lambda e: e.tensor_tensor(u, u, s, ALU.mult), name)
                DVE.wait(m)
                m = DVE.do(lambda e: e.scalar_tensor_tensor(y, u, 1.5, y, ALU.add, ALU.mult), name)
            return m

        a1 = Area(arena, HEAD, WORDS)
        x_in = [a1.take(TT * D, t=TT, d=D) for _ in range(2)]
        x_norm = [a1.take(TT * D, t=TT, d=D) for _ in range(2)]
        x_T = [a1.take(KC * T, k=KC, t=T) for _ in range(2)]
        w_qkv = a1.take(KC * 3 * D, k=KC, n=3 * D)
        b_qk = a1.take(2 * KC)
        b_v = a1.take(D)
        qk_32 = [a1.take(T) for _ in range(2)]
        qk_rest = [a1.take(T) for _ in range(2)]
        qk_part = [a1.take(3 * T // 2, BF16, s=3, t=T) for _ in range(3)]
        v_out = [a1.take(TT * D, t=TT, d=D) for _ in range(2)]
        moments_1 = a1.take(TT * 6, t=TT, s=6)
        mean_var_1 = a1.take(TT * 2, t=TT, s=2)
        newton_1 = [a1.take(TT) for _ in range(3)]

        ring_T = Ring([banks[:, n, :] for n in range(2)])
        ring_qk = Ring([banks[:, n, :] for n in range(2, 5)])
        ring_v = Ring([banks[:, n, :] for n in range(5, 7)])

        x_free = [None, None]
        norm_free = [None, None]
        xT_free = [None, None]
        part_free = [None] * 3
        v_free = [None, None]
        x_loaded, x_ready, xT_ready = {}, {}, {}
        stored_qk, stored_v = {}, {}

        wqkv_loaded = None

        def load_x(b):
            SP.wait(x_free[b % 2])
            x_loaded[b] = SP.dma(x_in[b % 2], t["L0_attn_x"][b].rearrange("(t p) d -> p t d", p=P), f"x_in{b % 2}")

        load_x(0)
        SP.dma(w_qkv, t["L0_attn_W_qkv"].rearrange("(k p) n -> p k n", p=P), "w_qkv")
        bias = t["L0_attn_b_qkv"]
        SP.dma(b_qk, bias[0:2 * D].rearrange("(c p) -> p c", p=P), "w_qkv", allow_slow_non_contiguous=True)
        wqkv_loaded = SP.dma(b_v, rows_of(bias[2 * D:3 * D]), "w_qkv")
        load_x(1)
        SP.wait(numbers)
        SP.dma(gamma, rows_of(t["L0_ffn_gamma"]), "vectors")
        SP.dma(beta, rows_of(t["L0_ffn_beta"]), "vectors")
        SP.dma(b_out, rows_of(t["L0_attn_b_out"]), "vectors")
        SP.dma(w_out, t["L0_attn_W_out"].rearrange("(k p) n -> p k n", p=P), "vectors")
        SP.dma(gate_w, t["L0_ffn_gate_w"].rearrange("(k p) e -> p k e", p=P), "vectors")
        vectors = SP.dma(b1_sb, t["L0_ffn_b1"].rearrange("e (c p) -> p e c", p=P), "vectors",
                         allow_slow_non_contiguous=True)

        DVE.wait(wqkv_loaded)
        bias_scaled = DVE.do(lambda e: e.tensor_scalar(b_qk[:, 0:KC], b_qk[:, 0:KC], SCALE, None, ALU.mult), "bias")

        def normalise(b):
            src, dst = x_in[b % 2], x_norm[b % 2]
            DVE.wait(x_loaded[b], norm_free[b % 2])
            for tt in range(TT):
                m = DVE.do(lambda e, tt=tt: e.bn_stats(moments_1[:, tt, :], src[:, tt, :]), "norm")
            DVE.wait(m)
            for tt in range(TT):
                m = DVE.do(lambda e, tt=tt: e.bn_aggr(mean_var_1[:, tt, :], moments_1[:, tt, :]), "norm")
            DVE.wait(m)
            DVE.wait(rsqrt(mean_var_1[:, :, 1], newton_1, "norm"))
            for tt in range(TT):
                m = DVE.do(lambda e, tt=tt: e.tensor_scalar(dst[:, tt, :], src[:, tt, :], mean_var_1[:, tt, 0:1],
                                                            newton_1[1][:, tt:tt + 1], ALU.subtract, ALU.mult), "norm")
            x_free[b % 2] = x_ready[b] = m

        def turn(b):
            PE.wait(x_ready[b], consts_pool)
            ACTE.wait(xT_free[b % 2])
            src, dst = x_norm[b % 2], x_T[b % 2]
            for k in range(KC):
                n, bank = ring_T.take(PE)
                for tt in range(TT):
                    m = PE.do(lambda e, k=k, tt=tt, bank=bank: e.transpose(
                        bank[:, tt * P:(tt + 1) * P], src[:, tt, k * P:(k + 1) * P], ident), "turned" if tt == TT - 1 else None)
                ACTE.wait(m)
                out = ACTE.do(lambda e, k=k, bank=bank: e.copy(dst[:, k, :], bank), "xT")
                ring_T.give(n, out)
            norm_free[b % 2] = m
            xT_ready[b] = out

        chunk = 0

        def project(b):
            nonlocal chunk
            src = x_T[b % 2]
            PE.wait(xT_ready[b], wqkv_loaded)
            ACTE.wait(bias_scaled)
            for c in range(2 * KC):
                n, bank = ring_qk.take(PE)
                for k in range(KC):
                    m = PE.do(lambda e, k=k, c=c, bank=bank: e.matmul(
                        bank, w_qkv[:, k, c * P:(c + 1) * P], src[:, k, :], start=(k == 0), stop=(k == KC - 1)),
                        "qk" if k == KC - 1 else None)
                i, j = chunk % 2, chunk % 3
                chunk += 1
                full, rest, part = qk_32[i], qk_rest[i], qk_part[j]
                ACTE.wait(m, parts_done.get(chunk - 2), part_free[j])
                got = ACTE.do(lambda e, c=c, bank=bank, full=full: e.activation(
                    full, bank, ACT.Identity, bias=b_qk[:, c:c + 1], scale=SCALE if c < KC else 1.0), "qk_32")
                ring_qk.give(n, got)
                ACTE.wait(got)
                high = ACTE.do(lambda e, full=full, part=part: e.copy(part[:, 0, :], full), "qk_high")
                DVE.wait(high, lows_done.get(chunk - 2))
                m = DVE.do(lambda e, full=full, rest=rest, part=part: e.tensor_tensor(
                    rest, full, part[:, 0, :], ALU.subtract), "qk_rest")
                parts_done[chunk] = m
                DVE.wait(m)
                mid = DVE.do(lambda e, rest=rest, part=part: e.tensor_copy(part[:, 1, :], rest), "qk_mid")
                POOL.wait(mid)
                low = POOL.do(lambda e, rest=rest, part=part: e.tensor_tensor(
                    part[:, 2, :], rest, part[:, 1, :], ALU.subtract), "qk_low")
                lows_done[chunk] = low
                SP.wait(low)
                which, rows = c // KC, slice((c % KC) * P, (c % KC + 1) * P)
                part_free[j] = SP.dma(qk_dram[which, :, b, rows, :].rearrange("s p t -> p s t"), part, f"qk_store{j}")
                stored_qk[b, c] = part_free[j]
            for half in range(2):
                n, bank = ring_v.take(PE)
                for s in range(2):
                    tt = half * 2 + s
                    for k in range(KC):
                        m = PE.do(lambda e, k=k, tt=tt, s=s, bank=bank: e.matmul(
                            bank[:, s * D:(s + 1) * D], src[:, k, tt * P:(tt + 1) * P], w_qkv[:, k, 2 * D:3 * D],
                            start=(k == 0), stop=(k == KC - 1)), "v" if (s, k) == (1, KC - 1) else None)
                DVE.wait(m, v_free[b % 2])
                got = DVE.do(lambda e, half=half, bank=bank: e.tensor_tensor(
                    v_out[b % 2][:, 2 * half:2 * half + 2, :], bank.rearrange("p (s d) -> p s d", s=2),
                    b_v.unsqueeze(1).broadcast_to([P, 2, D]), ALU.add), "v_add")
                ring_v.give(n, got)
            xT_free[b % 2] = m
            SP.wait(got)
            v_free[b % 2] = stored_v[b] = SP.dma(v_dram[b].rearrange("(t p) d -> p t d", p=P), v_out[b % 2], f"v_store{b % 2}")

        parts_done, lows_done = {}, {}

        w_sb = weights[:, :].rearrange("p (e w) -> p e w", e=E)

        def load_expert(e_):
            for m, name in ((0, "L0_ffn_w1"), (1, "L0_ffn_w2")):
                c = KC if m == 0 else FC
                mark = SP.dma(w_sb[:, e_, m * EW // 2:(m + 1) * EW // 2].rearrange("p (c n) -> p c n", c=c),
                              t[name][e_].rearrange("(c p) n -> p c n", p=P), f"w_in{e_}")
            return mark

        w_loaded = {}
        tops = a1.take(2 * E, m=2, e=E)

        def magnitudes(e_):
            DVE.wait(w_loaded[e_])
            for m in range(2):
                mark = DVE.do(lambda e, m=m: e.tensor_reduce(
                    tops[:, m, e_:e_ + 1], w_sb[:, e_, m * EW // 2:(m + 1) * EW // 2], AX.X, ALU.max,
                    apply_absolute_value=True), "tops")
            return mark

        normalise(0)
        turn(0)
        for b in range(B):
            if b + 1 < B:
                normalise(b + 1)
                turn(b + 1)
            if b + 2 < B:
                load_x(b + 2)
            w_loaded[b] = load_expert(b)
            project(b)
            tops_done = magnitudes(b)

        S_TOP, S_SCALE, S_TMP, S_UNDO = stat[:, 0:8], stat[:, 8:12], stat[:, 16:24], stat[:, 24:28]
        DVE.wait(vectors, tops_done)
        m = DVE.do(lambda e: e.tensor_reduce(S_TMP[:, 0:2], tops, AX.X, ALU.max), "scale")
        DVE.do(lambda e: e.tensor_reduce(S_TMP[:, 2:3], gamma, AX.X, ALU.max, apply_absolute_value=True), "scale")
        DVE.do(lambda e: e.tensor_reduce(S_TMP[:, 3:4], beta, AX.X, ALU.max, apply_absolute_value=True), "scale")
        m = DVE.do(lambda e: e.tensor_reduce(S_TMP[:, 4:5], b1_sb, AX.XY, ALU.max, apply_absolute_value=True), "scale")
        POOL.wait(m)
        m = POOL.do(lambda e: e.partition_all_reduce(S_TOP[:, 0:5], S_TMP[:, 0:5], P, bass.bass_isa.ReduceOp.max), "scale_all")
        DVE.wait(m)
        root = math.ceil(math.sqrt(D))
        m = DVE.do(lambda e: e.scalar_tensor_tensor(S_TOP[:, 2:3], S_TOP[:, 2:3], float(root), S_TOP[:, 3:4],
                                                    ALU.mult, ALU.add), "scale")
        DVE.wait(m)
        m = DVE.do(lambda e: e.scalar_tensor_tensor(S_TOP[:, 3:4], S_TOP[:, 2:3], float(D), S_TOP[:, 0:1],
                                                    ALU.mult, ALU.mult), "scale")
        DVE.wait(m)
        m = DVE.do(lambda e: e.tensor_tensor(S_TOP[:, 3:4], S_TOP[:, 3:4], S_TOP[:, 4:5], ALU.add), "scale")
        DVE.wait(m)
        m = DVE.do(lambda e: e.tensor_scalar(S_TMP[:, 0:4].bitcast(I32), S_TOP[:, 0:4].bitcast(I32), 23, None,
                                             ALU.logical_shift_right), "scale")
        DVE.wait(m)
        m = DVE.do(lambda e: e.tensor_scalar(S_TMP[:, 0:4].bitcast(I32), S_TMP[:, 0:4].bitcast(I32), 80.0, 200.0,
                                             ALU.max, ALU.min), "scale")
        DVE.wait(m)
        m = DVE.do(lambda e: e.tensor_scalar(S_TMP[:, 4:8].bitcast(I32), S_TMP[:, 0:4].bitcast(I32), -1.0,
                                             float(127 * 2 + 14), ALU.mult, ALU.add), "scale")
        m2 = DVE.do(lambda e: e.tensor_scalar(S_TMP[:, 0:4].bitcast(I32), S_TMP[:, 0:4].bitcast(I32), -14.0, None,
                                              ALU.add), "scale")
        DVE.wait(m, m2)
        DVE.do(lambda e: e.tensor_scalar(S_SCALE.bitcast(I32), S_TMP[:, 4:8].bitcast(I32), 23, None,
                                         ALU.logical_shift_left), "scale")
        m = DVE.do(lambda e: e.tensor_scalar(S_UNDO.bitcast(I32), S_TMP[:, 0:4].bitcast(I32), 23, None,
                                             ALU.logical_shift_left), "scale")
        DVE.wait(m)
        UNDO_1, UNDO_2 = stat[:, 28:29], stat[:, 29:30]
        DVE.do(lambda e: e.tensor_tensor(UNDO_1, S_UNDO[:, 0:1], S_UNDO[:, 2:3], ALU.mult), "scale")
        scales = DVE.do(lambda e: e.tensor_tensor(UNDO_2, S_UNDO[:, 1:2], S_UNDO[:, 3:4], ALU.mult), "scale")
        SCALE_W = [S_SCALE[:, 0:1], S_SCALE[:, 1:2]]
        SCALE_X, SCALE_H = S_SCALE[:, 2:3], S_SCALE[:, 3:4]

        every_lane = []

        def meet():
            marks = [(s, s.count) for s in pool.values() if s.count]
            for lane in LANES:
                lane.wait(*marks)
        meet()
        a2 = Area(arena, HEAD, WORDS)
        LATE = 2
        lent = Area(weights, (E - LATE) * EW, E * EW)
        q_st = [a2.take(HG * T // 2, BF16, h=HG, t=T) for _ in range(4)]
        k_st = [a2.take(HG * T // 2, BF16, h=HG, t=T) for _ in range(4)]
        v_in = [a2.take(TT * HG * HD, t=TT, n=HG * HD) for _ in range(2)]
        v_one = [a2.take(TT * HG * 2 * HD, t=TT, h=HG, d=2 * HD) for _ in range(2)]
        PT_AT, PT_LEN = (0, 640, 1024, 512), TT * (TT + 1) // 2 * P
        p_T = lent.take(6 * PT_LEN, h=6, c=PT_LEN)
        o_T = a2.take(T)
        o_rows = a2.take(TT * D, t=TT, d=D)
        turned = a2.take(KC * T, k=KC, t=T)
        x2 = a2.take(TT * D, t=TT, d=D)
        z = a2.take(TT * D, t=TT, d=D)
        rows = a2.take(TT * ROW, t=TT, d=ROW)
        b2_pad = [(lent if tt < 2 else a2).take(D) for tt in range(TT)]
        w_high, w_low = a2.take(EW // 8, F16), a2.take(EW // 8, F16)
        top = [a2.take(HG * TT, h=HG, t=TT) for _ in range(2)]
        top_rest = a2.take(HG * TT, h=HG, t=TT)
        top_part = a2.take(MAXROWS * HG * TT // 2, BF16, s=MAXROWS, h=HG, t=TT)
        top_T = a2.take(P // 2, BF16)
        recip = a2.take(TT * HG, t=TT, h=HG)
        moments = a2.take(TT * 6, t=TT, s=6)
        mean_var = a2.take(TT * 2, t=TT, s=2)
        newton = [a2.take(TT) for _ in range(3)]
        rstd = a2.take(TT)
        logit = a2.take(TT * E, t=TT, e=E)
        g1, g2 = a2.take(TT * E, t=TT, e=E), a2.take(TT * E, t=TT, e=E)
        col = [a2.take(TT) for _ in range(6)]
        cw_pad = a2.take(TT * 32, t=TT, e=32)
        cw_T = a2.take(P)

        ring_s = Ring([banks[:, n, :] for n in range(2)])
        ring_p = Ring([banks[:, 2 + 2 * n:4 + 2 * n, :] for n in range(2)])
        ring_c = Ring([banks[:, 6, :]])
        ring_o = Ring([banks[:, 7, :]])

        for s in range(4):
            ones_set = DVE.do(lambda e, s=s: e.memset(k_st[s][STACK:P, :, :], 1.0), "ones_set")
        for s in range(2):
            POOL.do(lambda e, s=s: e.memset(v_one[s][:, :, :, HD:2 * HD], 1.0), "set")
        for tt in range(TT):
            POOL.do(lambda e, tt=tt: e.memset(b2_pad[tt], 0.0), "set")
        is_set = POOL.do(lambda e: e.memset(cw_pad, 0.0), "set")
        SP.wait(is_set)
        for tt in range(TT):
            b2_loaded = SP.dma(b2_pad[tt][32 * tt:32 * tt + E, :], t["L0_ffn_b2"], "b2_in")
        m = DVE.do(lambda e: e.memset(rows[:, :, :], 0.0), "spare")
        SP.wait(m)
        spare_rows = SP.dma(rows_dram[N:N + P, :], rows[:, 0, :], "spare_rows")
        SP.wait(spare_rows)
        spare_acc = SP.dma(acc_dram[N:N + P, :], rows[:, 0, 0:D], "spare_acc")

        UNITS = B * NG
        PAIRS = UNITS * HG // 2
        qk_loaded, v_loaded, top_loaded, v_ready = {}, {}, {}, {}
        st_free, vin_free, vone_free = [None] * 4, [None] * 2, [None] * 2
        pair_free = [()] * 3
        pair_ready = {}
        o_turned = [None]

        def load_unit(u):
            b, g = divmod(u, NG)
            s = u % 4
            own = slice(g * HG * HD, (g + 1) * HG * HD)
            SP.wait(st_free[s])
            for stack, which, parts in ((q_st[s], 0, Q_PARTS), (k_st[s], 1, K_PARTS)):
                for n, part in enumerate(parts):
                    m = SP.dma(stack[n * HD:(n + 1) * HD, :, :],
                               qk_dram[which, part, b, own, :].rearrange("(h d) t -> d h t", d=HD), f"qk_in{s}")
            qk_loaded[u] = m

        def load_v(u):
            b, g = divmod(u, NG)
            own = slice(g * HG * HD, (g + 1) * HG * HD)
            SP.wait(vin_free[u % 2])
            v_loaded[u] = SP.dma(v_in[u % 2], v_dram[b].rearrange("(t p) d -> p t d", p=P)[:, :, own], f"v_in{u % 2}")
            POOL.wait(v_loaded[u], vone_free[u % 2])
            v_ready[u] = vin_free[u % 2] = POOL.do(lambda e, s=u % 2: e.tensor_copy(
                v_one[s][:, :, :, 0:HD], v_in[s].rearrange("p t (h d) -> p t h d", h=HG)), "v_spread")

        def maxima(u, h):
            q, k, out = q_st[u % 4], k_st[u % 4], top[u % 2]
            if h == 0:
                PE.wait(qk_loaded[u])
                DVE.wait(top_split.get(u - 2))

            def block(bank, at, h, qt):
                keys = (qt + 1) * P
                PE.do(lambda e: e.matmul(bank[:, at:at + keys], q[0:STACK, h, qt * P:qt * P + P],
                                         k[0:STACK, h, 0:keys], start=True, stop=False))
                return PE.do(lambda e: e.matmul(bank[:, at + keys - P:at + keys], ident_b, mask_b,
                                                start=False, stop=True), "scores")

            def reduce(out_, in_, mark):
                DVE.wait(mark)
                return DVE.do(lambda e: e.tensor_reduce(out_, in_, AX.X, ALU.max, negate=True), "maxima")

            n, bank = ring_s.take(PE)
            m = block(bank, 0, h, 3)
            ring_s.give(n, reduce(out[:, h, 3:4], bank, m))
            n, bank = ring_s.take(PE)
            block(bank, 0, h, 0)
            m = block(bank, P, h, 2)
            reduce(out[:, h, 0:1], bank[:, 0:P], m)
            ring_s.give(n, reduce(out[:, h, 2:3], bank[:, P:T], m))
            if h % 2:
                n, bank = ring_s.take(PE)
                block(bank, 0, h - 1, 1)
                m = block(bank, 2 * P, h, 1)
                got = reduce(out[:, h - 1:h + 1, 1], bank.rearrange("p (h k) -> p h k", h=2), m)
                ring_s.give(n, got)
                top_done[u] = got

        top_done, top_split = {}, {}

        def place_maxima(u):
            src = top[u % 2]
            DVE.wait(top_done[u], top_turned.get(u - 1))
            m = DVE.do(lambda e: e.tensor_copy(top_part[:, 0], src), "top")
            DVE.wait(m)
            m = DVE.do(lambda e: e.tensor_tensor(top_rest, src, top_part[:, 0], ALU.subtract), "top")
            top_split[u] = m
            DVE.wait(m)
            m = DVE.do(lambda e: e.tensor_copy(top_part[:, 1], top_rest), "top")
            DVE.wait(m)
            m = DVE.do(lambda e: e.tensor_tensor(top_part[:, 2], top_rest, top_part[:, 1], ALU.subtract), "top")
            PE.wait(m)
            n, bank = ring_s.take(PE)
            rows_ = MAXROWS * HG * TT
            m = PE.do(lambda e: e.transpose(bank.bitcast(BF16)[0:rows_, 0:P],
                                            top_part.rearrange("p s h t -> p (s h t)"), ident_b), "top_turned")
            top_turned[u] = m
            DVE.wait(m, top_loaded.get(u - 1))
            m = DVE.do(lambda e: e.tensor_copy(top_T[0:rows_, :], bank.bitcast(BF16)[0:rows_, 0:P]), "top")
            ring_s.give(n, m)
            SP.wait(m)
            for s in range(MAXROWS):
                m = SP.dma(q_st[u % 4][STACK + s:STACK + s + 1, :, :].rearrange("o h (t c) -> o (h t) c", c=P),
                           top_T[s * HG * TT:(s + 1) * HG * TT, :], "top_in")
            top_loaded[u] = m

        top_turned = {}

        def exponentials(u, h, pair):
            q, k = q_st[u % 4], k_st[u % 4]
            ROWS = STACK + MAXROWS
            if h == 0:
                PE.wait(top_loaded[u], ones_set)

            def block(out_, kt, name=None):
                return PE.do(lambda e: e.matmul(out_, k[0:ROWS, h, kt * P:kt * P + P], q[0:ROWS, h, kt * P:T],
                                                start=True, stop=True), name)

            slot = 2 * (pair % 3) + h % 2
            if h % 2 == 0:
                ACTE.wait(*pair_free[pair % 3])
                held_c[:] = ring_c.take(PE)
            nc_, bank_c = held_c
            n, two = ring_p.take(PE)
            block(two[:, 0, :], 0)
            block(two[:, 1, 0:P], 3)
            m = block(two[:, 1, P:T], 1, "scores_T")
            ACTE.wait(m)
            m = ACTE.do(lambda e: e.activation(p_T[:, slot, 0:2 * T], two.rearrange("p b c -> p (b c)"), ACT.Exp), "exp")
            ring_p.give(n, m)
            m = block(bank_c[:, 2 * P * (h % 2):2 * P * (h % 2 + 1)], 2, "scores_T")
            if h % 2:
                st_free[u % 4] = m
                ACTE.wait(m)
                m = ACTE.do(lambda e: e.activation(p_T[:, slot - 1:slot + 1, 2 * T:PT_LEN],
                                                   bank_c.rearrange("p (h c) -> p h c", h=2), ACT.Exp), "exp")
                ring_c.give(nc_, m)
                POOL.wait(m)
                both = p_T[:, slot - 1:slot + 1, :]
                for area, pattern in ((both[:, :, 0:P], [[0, 2], [1, P]]),
                                      (both[:, :, T:T + 2 * P], [[0, 2], [0, 2], [1, P]]),
                                      (both[:, :, 2 * T:2 * T + P], [[0, 2], [1, P]])):
                    m = POOL.do(lambda e, area=area, pattern=pattern: e.affine_select(
                        out=area, in_=area, compare_op=ALU.is_ge, fill=0.0, base=0, pattern=pattern,
                        channel_multiplier=-1), "masked")
                pair_ready[pair] = m

        held_c = [None, None]

        def weigh(u):
            b, g = divmod(u, NG)
            vv = v_one[u % 2]
            n, bank = ring_o.take(PE)
            PE.wait(v_ready[u], pair_ready[2 * u], pair_ready[2 * u + 1])
            for kt in range(TT):
                for h in range(HG):
                    slot = 2 * ((2 * u + h // 2) % 3) + h % 2
                    a, w = PT_AT[kt], T - kt * P
                    m = PE.do(lambda e, h=h, kt=kt, slot=slot, a=a, w=w: e.matmul(
                        bank[32 * h:32 * h + 32, kt * P:T], vv[:, kt, h, :], p_T[:, slot, a:a + w],
                        start=(kt == 0), stop=(kt == TT - 1), tile_position=(0, 32 * h)),
                        "weighed" if (kt, h) == (TT - 1, HG - 1) else None)
            vone_free[u % 2] = m
            for pair in (2 * u, 2 * u + 1):
                pair_free[pair % 3] = (m,)
            ACTE.wait(m, o_turned[0])
            m = ACTE.do(lambda e: e.copy(o_T, bank), "o_T")
            ring_o.give(n, m)
            return m

        def divide(u, copied):
            b, g = divmod(u, NG)
            PE.wait(copied)
            n, bank = ring_s.take(PE)
            for qt in range(TT):
                m = PE.do(lambda e, qt=qt: e.transpose(bank[:, qt * P:qt * P + P], o_T[:, qt * P:qt * P + P], ident),
                          "o_turned" if qt == TT - 1 else None)
            o_turned[0] = m
            sums = bank.rearrange("p (t h d) -> p t h d", t=TT, h=HG)
            DVE.wait(m, o_rows_free[0], recip_free[0])
            m = DVE.do(lambda e: e.reciprocal(recip, sums[:, :, :, HD]), "divide")
            DVE.wait(m)
            m = DVE.do(lambda e: e.tensor_tensor(
                o_rows[:, :, g * HG * HD:(g + 1) * HG * HD].rearrange("p t (h d) -> p t h d", h=HG),
                sums[:, :, :, 0:HD], recip.unsqueeze(3).broadcast_to([P, TT, HG, HD]), ALU.mult), "divide")
            recip_free[0] = m
            ring_s.give(n, m)
            return m

        o_rows_free, recip_free = [None], [None]
        x_again, x2_free = {}, [None]
        rows_free, turned_free = [spare_acc], [None]

        def load_again(b):
            SP.wait(x2_free[0])
            x_again[b] = SP.dma(x2, t["L0_attn_x"][b].rearrange("(t p) d -> p t d", p=P), "x_again")

        def over_tiles(vec):
            return vec.unsqueeze(1).broadcast_to([P, TT, vec.shape[1]])

        def column(c, n):
            return c.unsqueeze(2).broadcast_to([P, TT, n])

        def turn_rows(src, ready, name):
            PE.wait(ready)
            ACTE.wait(turned_free[0])
            for k in range(KC):
                n, bank = ring_s.take(PE)
                for tt in range(TT):
                    m = PE.do(lambda e, k=k, tt=tt, bank=bank: e.transpose(
                        bank[:, tt * P:(tt + 1) * P], src[:, tt, k * P:(k + 1) * P], ident), name if tt == TT - 1 else None)
                ACTE.wait(m)
                out = ACTE.do(lambda e, k=k, bank=bank: e.copy(turned[:, k, :], bank), "turned")
                ring_s.give(n, out)
            return m, out

        def finish_1(b, ready):
            POOL.wait(x_again[b])
            with_bias = POOL.do(lambda e: e.tensor_tensor(x2, x2, over_tiles(b_out), ALU.add), "with_bias")
            o_rows_free[0], out = turn_rows(o_rows, ready, "rows_turned")
            PE.wait(out)
            for half in range(2):
                n, bank = ring_s.take(PE)
                for s in range(2):
                    tt = 2 * half + s
                    for k in range(KC):
                        m = PE.do(lambda e, k=k, tt=tt, s=s, bank=bank: e.matmul(
                            bank[:, s * D:(s + 1) * D], turned[:, k, tt * P:(tt + 1) * P], w_out[:, k, :],
                            start=(k == 0), stop=(k == KC - 1)), "w_out" if (s, k) == (1, KC - 1) else None)
                DVE.wait(m, with_bias)
                got = DVE.do(lambda e, half=half, bank=bank: e.tensor_tensor(
                    x2[:, 2 * half:2 * half + 2, :], bank.rearrange("p (s d) -> p s d", s=2),
                    x2[:, 2 * half:2 * half + 2, :], ALU.add), "x2")
                ring_s.give(n, got)
            turned_free[0] = m
            DVE.wait(got)
            for tt in range(TT):
                m = DVE.do(lambda e, tt=tt: e.bn_stats(moments[:, tt, :], x2[:, tt, :]), "norms")
            DVE.wait(m)
            for tt in range(TT):
                m = DVE.do(lambda e, tt=tt: e.bn_aggr(mean_var[:, tt, :], moments[:, tt, :]), "norms")
            DVE.wait(m)
            DVE.wait(rsqrt(mean_var[:, :, 1], newton, "norms"))
            m = DVE.do(lambda e: e.tensor_copy(rstd, newton[1]), "norms")
            DVE.wait(m, z_free[0])
            for tt in range(TT):
                z_done = DVE.do(lambda e, tt=tt: e.tensor_scalar(
                    z[:, tt, :], x2[:, tt, :], mean_var[:, tt, 0:1], rstd[:, tt:tt + 1], ALU.subtract, ALU.mult), "z")
            m = DVE.do(lambda e: e.tensor_tensor(col[0], mean_var[:, :, 1], rstd, ALU.mult), "norms")
            DVE.wait(m)
            m = DVE.do(lambda e: e.tensor_tensor(col[0], col[0], rstd, ALU.mult), "norms")
            DVE.wait(m)
            DVE.wait(rsqrt(col[0], newton, "norms"))
            DVE.wait(z_done, *rows_free)
            for tt in range(TT):
                m = DVE.do(lambda e, tt=tt: e.scalar_tensor_tensor(
                    rows[:, tt, 0:D], z[:, tt, :], newton[1][:, tt:tt + 1], gamma, ALU.mult, ALU.mult), "norms")
            POOL.wait(m)
            normed = POOL.do(lambda e: e.tensor_tensor(rows[:, :, 0:D], rows[:, :, 0:D], over_tiles(beta), ALU.add), "beta")
            m = POOL.do(lambda e: e.tensor_tensor(z, z, x2, ALU.add), "residual")
            x2_free[0] = m
            return normed, m

        z_free = [None]

        def finish_2(b, normed, residual):
            tiles = slice(b * TT, (b + 1) * TT)
            _, out = turn_rows(rows, normed, "gate_turned")
            PE.wait(out)
            n, bank = ring_s.take(PE)
            for tt in range(TT):
                for k in range(KC):
                    m = PE.do(lambda e, k=k, tt=tt, bank=bank: e.matmul(
                        bank[:, tt * E:(tt + 1) * E], turned[:, k, tt * P:(tt + 1) * P], gate_w[:, k, :],
                        start=(k == 0), stop=(k == KC - 1)), "gate" if (tt, k) == (TT - 1, KC - 1) else None)
            turned_free[0] = m
            DVE.wait(m)
            m = DVE.do(lambda e, bank=bank: e.tensor_copy(logit, bank[:, 0:TT * E].rearrange("p (t e) -> p t e", t=TT)), "choose")
            ring_s.give(n, m)
            step = [m]

            def then(emit):
                DVE.wait(step[0])
                step[0] = DVE.do(emit, "choose")

            first, second, order, gap, one, w1 = col
            pick1, pick2 = choice[:, tiles, 0, :], choice[:, tiles, 1, :]
            for top_, src, pick in ((first, logit, pick1), (second, g2, pick2)):
                then(lambda e, top_=top_, src=src: e.tensor_reduce(top_, src, AX.X, ALU.max))
                then(lambda e, top_=top_, src=src: e.tensor_tensor(g1, src, column(top_, E), ALU.is_ge))
                then(lambda e: e.tensor_tensor(g1, g1, over_tiles(prefer), ALU.mult))
                then(lambda e: e.tensor_reduce(order, g1, AX.X, ALU.max))
                then(lambda e, pick=pick: e.tensor_tensor(pick, g1, column(order, E), ALU.is_equal))
                if pick is pick1:
                    then(lambda e: e.scalar_tensor_tensor(g2, pick1, -3.0e38, logit, ALU.mult, ALU.add))
            then(lambda e: e.tensor_tensor(gap, second, first, ALU.subtract))
            ACTE.wait(step[0])
            m = ACTE.do(lambda e: e.activation(gap, gap, ACT.Exp), "gate_exp")
            step[0] = m
            then(lambda e: e.tensor_scalar(one, gap, 1.0, None, ALU.add))
            then(lambda e: e.reciprocal(w1, one))
            then(lambda e: e.tensor_tensor(gap, gap, w1, ALU.mult))
            then(lambda e: e.tensor_tensor(g1, pick1, column(w1, E), ALU.mult))
            then(lambda e: e.tensor_tensor(g2, pick2, column(gap, E), ALU.mult))
            DVE.wait(cw_free[0])
            then(lambda e: e.tensor_tensor(rows[:, :, D:ROW], g1, g2, ALU.add))
            then(lambda e: e.tensor_tensor(cw_pad[:, :, 0:E], g1, g2, ALU.add))
            SP.wait(step[0], normed)
            m = SP.dma(rows_dram[b * T:(b + 1) * T, :].rearrange("(t p) d -> p t d", p=P), rows, "rows_out")
            rows_free[:] = [m, out]
            PE.wait(step[0])
            n, bank = ring_s.take(PE)
            m = PE.do(lambda e, bank=bank: e.transpose(bank[:, 0:P], cw_pad.rearrange("p t e -> p (t e)"), ident), "cw_turned")
            cw_free[0] = m
            ACTE.wait(m)
            m = ACTE.do(lambda e, bank=bank: e.copy(cw_T, bank[:, 0:P]), "cw_T")
            ring_s.give(n, m)
            PE.wait(m, b2_loaded)
            DVE.wait(residual)
            for half in range(2):
                n, bank = ring_s.take(PE)
                for s in range(2):
                    m = PE.do(lambda e, s=s, bank=bank, tt=2 * half + s: e.matmul(
                        bank[:, s * D:(s + 1) * D], cw_T, b2_pad[tt], start=True, stop=True), "b2")
                DVE.wait(m)
                got = DVE.do(lambda e, half=half, bank=bank: e.tensor_tensor(
                    z[:, 2 * half:2 * half + 2, :], bank.rearrange("p (s d) -> p s d", s=2),
                    z[:, 2 * half:2 * half + 2, :], ALU.add), "base")
                ring_s.give(n, got)
            SP.wait(got)
            z_free[0] = SP.dma(acc_dram[b * T:(b + 1) * T, :].rearrange("(t p) d -> p t d", p=P), z, "acc_out")

        cw_free = [None]

        HALF = EW // 4
        w_16 = weights[:, :].bitcast(F16).rearrange("p (e m k s w) -> p e m k s w", e=E, m=2, k=2, s=2)
        split_free = [None, None]
        w_split = {}

        def split_weights(e_, m_, k_, high, low):
            src = w_sb[:, e_, m_ * EW // 2 + k_ * HALF:m_ * EW // 2 + (k_ + 1) * HALF]
            ACTE.wait(scales, *split_free)
            m = ACTE.do(lambda e: e.activation(src, src, ACT.Copy, scale=SCALE_W[m_]), "w_scaled")
            ACTE.wait(m)
            m = ACTE.do(lambda e: e.copy(high, src), "w_high")
            POOL.wait(m)
            m = POOL.do(lambda e: e.tensor_tensor(low, src, high, ALU.subtract), "w_low")
            DVE.wait(m)
            DVE.do(lambda e: e.tensor_copy(w_16[:, e_, m_, k_, 0, :], high), "w_split")
            m = DVE.do(lambda e: e.tensor_copy(w_16[:, e_, m_, k_, 1, :], low), "w_split")
            split_free[:] = [m, m]
            w_split[e_, m_, k_] = m

        splits = [(e_, m_, k_) for e_ in range(E - LATE) for m_ in range(2) for k_ in range(2)]

        for u in range(3):
            load_unit(u)
        load_again(0)
        for u in range(2):
            for h in range(HG):
                maxima(u, h)
            place_maxima(u)
        pending = None
        for i in range(UNITS + 2):
            if i < UNITS:
                load_v(i)
            if i + 3 < UNITS:
                load_unit(i + 3)
            for h in range(HG):
                if i + 2 < UNITS:
                    maxima(i + 2, h)
                if i < UNITS:
                    exponentials(i, h, 2 * i + h // 2)
                if h == 0:
                    if 1 < i + 1 < UNITS:
                        place_maxima(i + 1)
                    if 0 < i <= UNITS:
                        copied = weigh(i - 1)
                if h == 1 and 0 < i <= UNITS:
                    divided = divide(i - 1, copied)
                if h == 2 and pending:
                    finish_2(*pending)
                    pending = None
                if h == 2 and 0 < i <= UNITS and i % NG == 0:
                    b = i // NG - 1
                    pending = (b, *finish_1(b, divided))
                    if b + 1 < B:
                        load_again(b + 1)
                if h == 3 and i < len(splits):
                    split_weights(*splits[i], w_high, w_low)
        meet()
        for e_ in range(E - LATE, E):
            w_loaded[e_] = load_expert(e_)
        a3 = Area(arena, HEAD, WORDS)
        NE = NT * E
        chosen = a3.take(NE // 2, BF16)
        totals = a3.take(NE, i=NT, e=E)
        before = a3.take(NE, i=NT, e=E)
        ones_i = a3.take(NT)
        counts = a3.take(E)
        tiles_e, ends = a3.take(E), a3.take(E)
        base = a3.take(E)
        by_choice = a3.take(NT * TOPK * E, i=NT, k=TOPK, e=E)
        slot = a3.take(NT * TOPK)
        slot_row, slot_col = a3.take(NT * TOPK), a3.take(NT * TOPK)
        slot_int = a3.take(NT * TOPK, I32)
        in_row = a3.take(NT * TOPK * P // 2, BF16, n=NT * TOPK, q=P)
        in_col = a3.take(NT * TOPK * SC, BF16, n=NT * TOPK, v=2, c=SC)
        ended = a3.take(TILES * E, j=TILES, e=E)
        tile_f = a3.take(TILES)
        found = a3.take(2 * SC, v=2, c=SC)
        real = a3.take(SC)
        spare = a3.take(1)
        temp = Area(arena, a3.at, WORDS)
        w_high_late, w_low_late = temp.take(EW // 8, F16), temp.take(EW // 8, F16)

        step = [None]

        def then3(emit):
            DVE.wait(step[0])
            step[0] = DVE.do(emit, "route")

        then3(lambda e: e.tensor_tensor(chosen.rearrange("p (i e) -> p i e", i=NT), choice[:, :, 0, :], choice[:, :, 1, :], ALU.add))
        then3(lambda e: e.memset(ones_i, 1.0))
        PE.wait(step[0])
        PE.do(lambda e: e.matmul(banks[:, 0, 0:NE], upper_b, chosen, start=True, stop=True))
        m = PE.do(lambda e: e.matmul(banks[:, 1, 0:NE], ones_b, chosen, start=True, stop=True), "counted")
        DVE.wait(m)
        tile_pairs = banks[:, 1, 0:NE].rearrange("p (i e) -> p i e", i=NT)
        for e_ in range(E):
            then3(lambda e, e_=e_: e.tensor_tensor_scan(totals[:, :, e_], ones_i, tile_pairs[:, :, e_], 0.0, ALU.mult, ALU.add))
        then3(lambda e: e.tensor_copy(counts, totals[:, NT - 1, :]))
        then3(lambda e: e.tensor_tensor(totals, totals, tile_pairs, ALU.subtract))
        then3(lambda e: e.tensor_tensor(before, totals, banks[:, 0, 0:NE].rearrange("p (i e) -> p i e", i=NT), ALU.add))
        then3(lambda e: e.tensor_scalar(base.bitcast(I32), counts, float(TILE - 1), None, ALU.add))
        then3(lambda e: e.tensor_scalar(base.bitcast(I32), base.bitcast(I32), TILE.bit_length() - 1, None, ALU.logical_shift_right))
        then3(lambda e: e.tensor_copy(tiles_e, base.bitcast(I32)))
        then3(lambda e: e.tensor_tensor_scan(ends, ones_i[:, 0:E], tiles_e, 0.0, ALU.mult, ALU.add))
        then3(lambda e: e.tensor_tensor(base, ends, tiles_e, ALU.subtract))
        then3(lambda e: e.tensor_scalar(base, base, float(TILE), None, ALU.mult))
        then3(lambda e: e.tensor_tensor(before, before, base.unsqueeze(1).broadcast_to([P, NT, E]), ALU.add))
        then3(lambda e: e.tensor_tensor(by_choice[:, :, 0, :], choice[:, :, 0, :], before, ALU.mult))
        then3(lambda e: e.tensor_tensor(by_choice[:, :, 1, :], choice[:, :, 1, :], before, ALU.mult))
        then3(lambda e: e.tensor_reduce(slot, by_choice.rearrange("p i k e -> p (i k) e"), AX.X, ALU.add))
        then3(lambda e: e.tensor_copy(slot_int, slot))
        then3(lambda e: e.tensor_scalar(slot_int, slot_int, 7, None, ALU.logical_shift_right))
        then3(lambda e: e.tensor_copy(slot_col, slot_int))
        then3(lambda e: e.scalar_tensor_tensor(slot_row, slot_col, float(-P), slot, ALU.mult, ALU.add))
        DVE.wait(step[0])
        for n in range(NT * TOPK):
            DVE.do(lambda e, n=n: e.tensor_scalar(in_row[:, n, :], iota_row, slot_row[:, n:n + 1], None, ALU.is_equal), "in_col")
            DVE.do(lambda e, n=n: e.tensor_scalar(in_col[:, n, 0, :], iota_row[:, 0:SC], slot_col[:, n:n + 1],
                                                  float(n // TOPK + 1), ALU.is_equal, ALU.mult), "in_col")
            col_ready = DVE.do(lambda e, n=n: e.tensor_scalar(in_col[:, n, 1, :], iota_row[:, 0:SC], slot_col[:, n:n + 1],
                                                              iota_part, ALU.is_equal, ALU.mult), "in_col")
            PE.wait(col_ready)
            m = PE.do(lambda e, n=n: e.matmul(banks[:, 2, 0:2 * SC], in_row[:, n, :], in_col[:, n].rearrange("p v c -> p (v c)"),
                                              start=(n == 0), stop=(n == NT * TOPK - 1)), "table" if n == NT * TOPK - 1 else None)
        then3(lambda e: e.tensor_tensor(ended, iota_row[:, 0:TILES].unsqueeze(2).broadcast_to([P, TILES, E]),
                                        ends.unsqueeze(1).broadcast_to([P, TILES, E]), ALU.is_ge))
        then3(lambda e: e.tensor_reduce(tile_f, ended, AX.X, ALU.add))
        then3(lambda e: e.tensor_scalar(tile_f, tile_f, float(E - 1), None, ALU.min))
        then3(lambda e: e.tensor_copy(tile_of, tile_f))
        tiles_known = step[0]
        then3(lambda e: e.tensor_tensor(hot, iota_row[:, 0:E].unsqueeze(1).broadcast_to([P, TILES, E]),
                                        tile_f.unsqueeze(2).broadcast_to([P, TILES, E]), ALU.is_equal))
        then3(lambda e: e.tensor_scalar(hot, hot, UNDO_2, None, ALU.mult))
        DVE.wait(m)
        then3(lambda e: e.tensor_copy(found, banks[:, 2, 0:2 * SC].rearrange("p (v c) -> p v c", v=2)))
        then3(lambda e: e.tensor_scalar(real, found[:, 0, :], 0.0, None, ALU.is_gt))
        then3(lambda e: e.scalar_tensor_tensor(found[:, 1, :], found[:, 0, :], float(P), found[:, 1, :], ALU.mult, ALU.add))
        then3(lambda e: e.tensor_scalar(spare, iota_part, float(N + P), None, ALU.add))
        then3(lambda e: e.tensor_scalar(found[:, 1, :], found[:, 1, :], spare, None, ALU.subtract))
        then3(lambda e: e.tensor_tensor(found[:, 1, :], found[:, 1, :], real, ALU.mult))
        then3(lambda e: e.tensor_scalar(spare, iota_part, float(N), None, ALU.add))
        then3(lambda e: e.tensor_scalar(found[:, 1, :], found[:, 1, :], spare, None, ALU.add))
        then3(lambda e: e.tensor_copy(slot_token, found[:, 1, :]))
        table_ready = step[0]

        split_free[:] = [None, None]
        for e_ in range(E - LATE, E):
            for m_ in range(2):
                for k_ in range(2):
                    ACTE.wait(w_loaded[e_])
                    split_weights(e_, m_, k_, w_high_late, w_low_late)

        meet()
        a4 = Area(arena, HEAD, WORDS)
        gathered = [a4.take(TC * ROW, c=TC, d=ROW) for _ in range(3)]
        xt_high = [a4.take(KC * TILE // 2, F16, k=KC, s=TILE) for _ in range(2)]
        xt_low = [a4.take(KC * TILE // 2, F16, k=KC, s=TILE) for _ in range(2)]
        w1_now = [a4.take(EW // 2, F16, k=KC, s=2, w=F) for _ in range(2)]
        w2_now = [a4.take(EW // 2, F16, k=2, s=2, c=FC // 2, n=D) for _ in range(2)]
        b1_now = [a4.take(FC) for _ in range(2)]
        h_32 = [a4.take(2 * TILE, c=2, s=TILE) for _ in range(2)]
        h_high = [a4.take(FC * TILE // 2, F16, c=FC, s=TILE) for _ in range(1)]
        h_low = [a4.take(FC * TILE // 2, F16, c=FC, s=TILE) for _ in range(1)]
        y = [a4.take(TC * D, c=TC, d=D) for _ in range(2)]
        share = a4.take(TC * E, c=TC, e=E)
        weight = [a4.take(TC) for _ in range(2)]
        ring_x = Ring([banks[:, 0, :]])
        ring_h = Ring([banks[:, n, :] for n in range(1, 6)])
        ring_y = Ring([banks[:, n, :] for n in range(6, 8)])

        gathered_free = [()] * 3
        gather_done, x_split, staged_1, staged_2, staged_b = {}, {}, {}, {}, {}
        xt_free, w1_free, w2_free, b1_free, y_free = [None] * 2, [None] * 2, [None] * 2, [None] * 2, [None] * 2
        h32_free, h_free = [None] * 2, [None]
        h_ready, added, weight_ready = {}, {}, {}
        h_count = 0

        def gather(j):
            s = j % 3
            POOL.wait(*gathered_free[s])
            for c in range(TC):
                gather_done[j] = POOL.indirect(f"gathered{s}", gathered[s][:, c, :], None, rows_dram[:, :],
                                               bass.IndirectOffsetOnAxis(slot_token[:, TC * j + c:TC * j + c + 1], 0))

        def stage_expert(j):
            s = j % 2
            DVE.wait(w1_free[s], w2_free[s], b1_free[s])

            box = []
            DVE.do(lambda e: box.append(e.value_load(tile_of[0:1, j:j + 1], min_val=0, max_val=E - 1)))
            flat = weights[:, :].bitcast(F16)
            staged_1[j] = DVE.do(lambda e: e.tensor_copy(w1_now[s].rearrange("p k s w -> p (k s w)"),
                                                         flat[:, bass.ds(box[0] * (2 * EW), EW)]), "staged")
            staged_b[j] = DVE.do(lambda e: e.tensor_copy(b1_now[s], b1_sb.rearrange("p e c -> p (e c)")[:, bass.ds(box[0] * FC, FC)]), "staged")
            staged_2[j] = DVE.do(lambda e: e.tensor_copy(w2_now[s].rearrange("p k s c n -> p (k s c n)"),
                                                         flat[:, bass.ds(box[0] * (2 * EW) + EW, EW)]), "staged")

        def turn_tokens(j):
            g = gathered[j % 3]
            PE.wait(gather_done[j])
            n, bank = ring_x.take(PE)
            for k in range(KC):
                for c in range(TC):
                    m = PE.do(lambda e, k=k, c=c: e.transpose(bank[:, k * TILE + c * P:k * TILE + (c + 1) * P],
                                                              g[:, c, k * P:(k + 1) * P], ident), "x_turned")
            turned_mark = m
            s = j % 2
            both = bank.rearrange("p (k s) -> p k s", k=KC)
            ACTE.wait(m, xt_free[s])
            m = ACTE.do(lambda e: e.activation(xt_high[s], both, ACT.Copy, scale=SCALE_X), "xt_high")
            DVE.wait(m)
            x_split[j] = DVE.do(lambda e: e.scalar_tensor_tensor(xt_low[s], both, SCALE_X, xt_high[s], ALU.mult, ALU.subtract), "xt_low")
            ring_x.give(n, x_split[j])
            DVE.wait(gather_done[j], y_weighted.get(j - 2))
            m = DVE.do(lambda e: e.tensor_tensor(share, g[:, :, D:ROW], hot[:, j:j + 1, :].broadcast_to([P, TC, E]), ALU.mult), "share")
            DVE.wait(m)
            weight_ready[j] = DVE.do(lambda e: e.tensor_reduce(weight[s], share, AX.X, ALU.add), "share")
            gathered_free[j % 3] = (turned_mark, m)

        y_weighted = {}

        def hidden(j):
            nonlocal h_count
            s = j % 2
            w1, xh, xl = w1_now[s], xt_high[s], xt_low[s]
            PE.wait(staged_1[j], x_split[j])
            for c2 in range(FC // 2):
                n, bank = ring_h.take(PE)
                for c in range(2):
                    f = (2 * c2 + c) * P
                    terms = [(k, wp, xp) for k in range(KC) for wp, xp in ((0, xh), (0, xl), (1, xh))]
                    for i, (k, wp, xp) in enumerate(terms):
                        m = PE.do(lambda e, k=k, wp=wp, xp=xp, f=f, c=c, i=i, bank=bank: e.matmul(
                            bank[:, c * TILE:(c + 1) * TILE], w1[:, k, wp, f:f + P], xp[:, k, :],
                            start=(i == 0), stop=(i == len(terms) - 1)), "hidden" if i == len(terms) - 1 else None)
                r = h_count % 2
                h_count += 1
                ACTE.wait(m, h32_free[r], staged_b[j])
                for c in range(2):
                    m2 = ACTE.do(lambda e, c=c, c2=c2, r=r, bank=bank: e.activation(
                        h_32[r][:, c, :], bank[:, c * TILE:(c + 1) * TILE], ACT.Gelu,
                        bias=b1_now[s][:, 2 * c2 + c:2 * c2 + c + 1], scale=UNDO_1), "gelu")
                ring_h.give(n, m2)
                DVE.wait(m2, h_free[0])
                m3 = DVE.do(lambda e, c2=c2, r=r: e.tensor_scalar(h_high[0][:, 2 * c2:2 * c2 + 2, :], h_32[r], SCALE_H, None,
                                                                  ALU.mult), "h_high")
                DVE.wait(m3)
                h_ready[j, c2] = h32_free[r] = DVE.do(lambda e, c2=c2, r=r: e.scalar_tensor_tensor(
                    h_low[0][:, 2 * c2:2 * c2 + 2, :], h_32[r], SCALE_H, h_high[0][:, 2 * c2:2 * c2 + 2, :], ALU.mult, ALU.subtract), "h_low")
            w1_free[s] = xt_free[s] = m
            b1_free[s] = m2

        def expert_out(j):
            s = j % 2
            w2 = w2_now[s]
            n, bank = ring_y.take(PE)
            PE.wait(staged_2[j])
            for c in range(TC):
                for f in range(FC):
                    PE.wait(h_ready[j, f // 2])
                    for i, (hp, wp) in enumerate(((h_high[0], 0), (h_high[0], 1), (h_low[0], 0))):
                        last = (f, i) == (FC - 1, 2)
                        m = PE.do(lambda e, f=f, c=c, i=i, hp=hp, wp=wp, last=last: e.matmul(
                            bank[:, c * D:(c + 1) * D], hp[:, f, c * P:(c + 1) * P],
                            w2[:, f // (FC // 2), wp, f % (FC // 2), :], start=(f == 0 and i == 0), stop=last),
                            "expert_out" if last else None)
            h_free[0] = w2_free[s] = m
            DVE.wait(m, y_free[s], weight_ready[j])
            for c in range(TC):
                m = DVE.do(lambda e, c=c: e.tensor_scalar(y[s][:, c, :], bank[:, c * D:(c + 1) * D], weight[s][:, c:c + 1], None,
                                                          ALU.mult), "y")
            ring_y.give(n, m)
            y_weighted[j] = m
            POOL.wait(m, added.get(j - 1))
            for c in range(TC):
                if c:
                    POOL.wait(added[j])
                added[j] = POOL.indirect("added", acc_dram[:, :], bass.IndirectOffsetOnAxis(slot_token[:, TC * j + c:TC * j + c + 1], 0),
                                         y[s][:, c, :], None, compute_op=ALU.add)
            y_free[s] = added[j]

        for j in range(2):
            gather(j)
        stage_expert(0)
        turn_tokens(0)
        hidden(0)
        for j in range(TILES):
            if j + 2 < TILES:
                gather(j + 2)
            if j + 1 < TILES:
                stage_expert(j + 1)
                turn_tokens(j + 1)
            expert_out(j)
            if j + 1 < TILES:
                hidden(j + 1)

        SP.wait(added[TILES - 1])
        done = SP.dma(t["out"].rearrange("b t d -> (b t) d"), acc_dram[0:N, :], "out")
        SP.wait(done)
        block = ctx.enter_context(nc.Block())
        for lane, where in zip(LANES, (block.tensor, block.scalar, block.vector, block.gpsimd, block.sync)):
            where(lambda engine, lane=lane: lane.play(engine))


_INS = ["L0_attn_x", "L0_attn_W_qkv", "L0_attn_b_qkv", "L0_attn_W_out", "L0_attn_b_out", "L0_ffn_gate_w",
        "L0_ffn_w1", "L0_ffn_b1", "L0_ffn_w2", "L0_ffn_b2", "L0_ffn_gamma", "L0_ffn_beta"]


def kernel(**inputs):
    import numpy as np
    from concourse import bacc
    from concourse.bass_utils import run_bass_kernel_spmd

    nc = bacc.Bacc("TRN2", target_bir_lowering=False, num_devices=1)
    arrays, tensors = {}, {}
    for name in _INS:
        a = np.ascontiguousarray(inputs[name])
        arrays[f"in_{name}"] = a
        tensors[name] = nc.dram_tensor(f"in_{name}", a.shape, mybir.dt.from_np(a.dtype), kind="ExternalInput").ap()
    shape = inputs["L0_attn_x"].shape
    tensors["out"] = nc.dram_tensor("out", shape, F32, kind="ExternalOutput").ap()
    build(nc, tensors)
    got = run_bass_kernel_spmd(nc, [arrays], core_ids=[0])
    return got.results[0]["out"]
```

```python
import math
from contextlib import ExitStack

import concourse.bass as bass
import concourse.mybir as mybir

ALU = mybir.AluOpType
ACT = mybir.ActivationFunctionType
AX = mybir.AxisListType
F32 = mybir.dt.float32
F16 = mybir.dt.float16
BF16 = mybir.dt.bfloat16
I32 = mybir.dt.int32

P = 128
NEG = -1.0e30
EPS = 1e-5


class Signal:

    def __init__(self, sem):
        self.sem, self.count = sem, 0

    def after(self, step):
        self.count += step
        return self, self.count


class Lane:

    def __init__(self, signals):
        self.items, self.signals, self.seen = [], signals, {}

    def do(self, emit, name=None):
        if name is None:
            self.items.append(emit)
            return None
        mark = self.signals(name).after(1)
        self.items.append(lambda e: emit(e).then_inc(mark[0].sem, 1))
        return mark

    def dma(self, out, in_, name, **how):
        mark = self.signals(name).after(16)
        self.items.append(lambda e: e.dma_start(out, in_, **how).then_inc(mark[0].sem, 16))
        return mark

    def indirect(self, name, *what, **how):
        mark = self.signals(name).after(16)
        self.items.append(lambda e: e.indirect_dma_start(*what, **how).then_inc(mark[0].sem, 16))
        return mark

    def wait(self, *marks):
        for mark in marks:
            if mark is None or self.seen.get(mark[0], 0) >= mark[1]:
                continue
            self.seen[mark[0]] = mark[1]
            self.items.append(lambda e, mark=mark: e.wait_ge(mark[0].sem, mark[1]))

    def play(self, engine):
        for item in self.items:
            item(engine)


class Ring:

    def __init__(self, buffers, free=()):
        self.buffers, self.free, self.next = buffers, [free] * len(buffers), 0

    def take(self, lane):
        n = self.next % len(self.buffers)
        self.next += 1
        assert self.free[n] is not None
        lane.wait(*self.free[n])
        self.free[n] = None
        return n, self.buffers[n]

    def give(self, n, *marks):
        self.free[n] = marks


def whole(steps):
    while True:
        try:
            next(steps)
        except StopIteration as end:
            return end.value


def build(nc, t, debug=None):
    B, T, D = t["L0_attn_x"].shape
    E, _, F = t["L0_ffn_w1"].shape
    HD = 16
    H = D // HD
    SCALE = HD ** -0.5
    KC = D // P
    FC = F // P
    TT = T // P
    NT = B * TT
    N = B * T
    HG = 4
    NG = H // HG
    TOPK = 2
    TILE = 256
    TC = TILE // P
    TILES = N * TOPK // TILE + E - 1
    SC = TILES * TC
    ROW = D + E
    Q_PARTS = (0, 1, 0, 2, 1, 0)
    K_PARTS = (0, 0, 1, 0, 1, 2)
    STACK = len(Q_PARTS) * HD
    MAXROWS = 3
    EW = 2 * KC * F

    ctx = ExitStack()
    with ctx:
        pool = {}

        def signals(name):
            if name not in pool:
                pool[name] = Signal(ctx.enter_context(nc.semaphore(name)))
            return pool[name]

        PE, ACTE, DVE, POOL, SP = (Lane(signals) for _ in range(5))
        LANES = (PE, ACTE, DVE, POOL, SP)

        def dram(name, shape, dt):
            return nc.dram_tensor(name, shape, dt).ap()

        qk_dram = dram("qk_parts", (2, 3, B, D, T), BF16)
        v_dram = dram("v_rows", (B, T, 2 * D), F32)
        rows_dram = dram("token_rows", (N + P, ROW), F32)
        acc_dram = dram("result_rows", (N + P, D), F32)

        weights = ctx.enter_context(nc.sbuf_tensor("weights", [P, E * EW], F32))
        WORDS = 20440
        arena = ctx.enter_context(nc.sbuf_tensor("arena", [P, WORDS], F32))
        banks = ctx.enter_context(nc.psum_tensor("banks", [P, 8, 512], F32))

        class Area:

            def __init__(self, base, start, end):
                self.base, self.at, self.end = base, start, end

            def take(self, words, dt=F32, **dims):
                a, self.at = self.at, self.at + words
                assert self.at <= self.end, (self.at, self.end)
                v = self.base[:, a:a + words]
                if dt != F32:
                    v = v.bitcast(dt)
                if dims:
                    names = list(dims)
                    v = v.rearrange(f"p ({' '.join(names)}) -> p {' '.join(names)}",
                                    **{k: dims[k] for k in names[1:]})
                return v

        keep = Area(arena, 0, 3000)
        ident = keep.take(P)
        ident_b = keep.take(P // 2, BF16)
        mask_b = keep.take(P // 2, BF16)
        upper_b = keep.take(P // 2, BF16)
        ones_b = keep.take(P // 2, BF16)
        iota_row = keep.take(P)
        iota_part = keep.take(1)
        prefer = keep.take(E)
        gamma = keep.take(D)
        beta = keep.take(D)
        b_out = keep.take(D)
        w_out = keep.take(KC * D, k=KC, n=D)
        gate_w = keep.take(KC * E, k=KC, e=E)
        choice = keep.take(NT * TOPK * E, i=NT, k=TOPK, e=E)
        b1_sb = keep.take(E * FC, e=E, c=FC)
        stat = keep.take(64)
        tops = keep.take(2 * E, m=2, e=E)
        hot = keep.take(TILES * E, j=TILES, e=E)
        tile_of = keep.take(TILES, I32)
        slot_token = keep.take(SC, I32)

        HEAD = keep.at
        c_zero = POOL.do(lambda e: e.memset(arena[:, 0:2 * P], 0.0), "const")
        c_ones = POOL.do(lambda e: e.memset(ones_b, 1.0), "const")
        c_upper = POOL.do(lambda e: e.memset(upper_b, 1.0), "const")
        POOL.wait(c_zero, c_ones, c_upper)
        POOL.do(lambda e: e.affine_select(out=ident, in_=ident, compare_op=ALU.not_equal, fill=1.0,
                                          base=0, pattern=[[-1, P]], channel_multiplier=1), "const")
        POOL.do(lambda e: e.affine_select(out=ident_b, in_=ident_b, compare_op=ALU.not_equal, fill=1.0,
                                          base=0, pattern=[[-1, P]], channel_multiplier=1), "const")
        POOL.do(lambda e: e.affine_select(out=mask_b, in_=mask_b, compare_op=ALU.is_ge, fill=NEG,
                                          base=0, pattern=[[-1, P]], channel_multiplier=1), "const")
        POOL.do(lambda e: e.affine_select(out=upper_b, in_=upper_b, compare_op=ALU.is_gt, fill=0.0,
                                          base=0, pattern=[[1, P]], channel_multiplier=-1), "const")
        POOL.do(lambda e: e.iota(b_out[:, 0:P].bitcast(I32), [[1, P]], base=0, channel_multiplier=0), "const")
        POOL.do(lambda e: e.iota(b_out[:, P:P + 1].bitcast(I32), [[0, 1]], base=0, channel_multiplier=1), "const")
        consts_pool = POOL.do(lambda e: e.iota(b_out[:, P + 1:P + 1 + E].bitcast(I32), [[-1, E]], base=E,
                                               channel_multiplier=0), "const")
        DVE.wait(consts_pool)
        DVE.do(lambda e: e.tensor_copy(iota_row, b_out[:, 0:P].bitcast(I32)), "numbers")
        DVE.do(lambda e: e.tensor_copy(iota_part, b_out[:, P:P + 1].bitcast(I32)), "numbers")
        numbers = DVE.do(lambda e: e.tensor_copy(prefer, b_out[:, P + 1:P + 1 + E].bitcast(I32)), "numbers")

        def rows_of(vector):
            return vector.partition_broadcast(P)

        def rsqrt(ready, scratch, name):
            s, y, u = scratch
            DVE.wait(ready)
            m = DVE.do(lambda e: e.tensor_scalar(y.bitcast(I32), s.bitcast(I32), 1, None,
                                                 ALU.logical_shift_right), name)
            yield
            DVE.wait(m)
            m = DVE.do(lambda e: e.tensor_scalar(y.bitcast(I32), y.bitcast(I32), -1.0, float(0x5F3759DF),
                                                 ALU.mult, ALU.add), name)
            for _ in range(3):
                yield
                DVE.wait(m)
                m = DVE.do(lambda e: e.scalar_tensor_tensor(u, y, -0.5, y, ALU.mult, ALU.mult), name)
                yield
                DVE.wait(m)
                m = DVE.do(lambda e: e.tensor_tensor(u, u, s, ALU.mult), name)
                yield
                DVE.wait(m)
                m = DVE.do(lambda e: e.scalar_tensor_tensor(y, u, 1.5, y, ALU.add, ALU.mult), name)
            return m

        stored_qk, stored_v = {}, {}
        LATE = 2
        a2 = Area(arena, HEAD, WORDS)
        lent = Area(weights, (E - LATE) * EW, E * EW)
        q_st = [a2.take(HG * T // 2, BF16, h=HG, t=T) for _ in range(4)]
        k_st = [a2.take(HG * T // 2, BF16, h=HG, t=T) for _ in range(4)]
        v_one = [a2.take(TT * HG * 2 * HD, t=TT, h=HG, d=2 * HD) for _ in range(2)]
        PT_AT, PT_LEN = (0, 640, 1024, 512), TT * (TT + 1) // 2 * P
        p_T = lent.take(6 * PT_LEN, h=6, c=PT_LEN)
        o_T = a2.take(T)
        o_rows = a2.take(TT * D, t=TT, d=D)
        turned = a2.take(KC * T, k=KC, t=T)
        x2 = a2.take(TT * D, t=TT, d=D)
        z = a2.take(TT * D, t=TT, d=D)
        rows = a2.take(TT * ROW, t=TT, d=ROW)
        b2_pad = [a2.take(D) for tt in range(TT)]
        w_high, w_low = a2.take(EW // 8, F16), a2.take(EW // 8, F16)
        top = [a2.take(HG * TT, h=HG, t=TT) for _ in range(2)]
        top_rest = a2.take(HG * TT, h=HG, t=TT)
        top_part = a2.take(MAXROWS * HG * TT // 2, BF16, s=MAXROWS, h=HG, t=TT)
        top_T = a2.take(P // 2, BF16)
        recip = a2.take(TT * HG, t=TT, h=HG)
        moments = a2.take(TT * 6, t=TT, s=6)
        mean_var = a2.take(TT * 2, t=TT, s=2)
        newton = [a2.take(2 * TT, n=2, t=TT) for _ in range(3)]
        shift, rstd_z = a2.take(TT), a2.take(TT)
        logit = a2.take(TT * E, t=TT, e=E)
        g1, g2 = a2.take(TT * E, t=TT, e=E), a2.take(TT * E, t=TT, e=E)
        col = [a2.take(TT) for _ in range(6)]
        cw_pad = a2.take(TT * 32, t=TT, e=32)
        cw_T = a2.take(P)

        UNITS = B * NG
        PAIRS = UNITS * HG // 2
        qk_loaded, top_loaded, v_ready = {}, {}, {}
        st_free, vone_free = [None] * 4, [None] * 2
        pair_free = [()] * 3
        pair_ready = {}
        o_turned = [None]

        def load_unit(u):
            b, g = divmod(u, NG)
            s = u % 4
            own = slice(g * HG * HD, (g + 1) * HG * HD)
            SP.wait(st_free[s], stored_qk[b, g // 2], stored_qk[b, KC + g // 2])
            for stack, which, parts in ((q_st[s], 0, Q_PARTS), (k_st[s], 1, K_PARTS)):
                for n, part in enumerate(parts):
                    m = SP.dma(stack[n * HD:(n + 1) * HD, :, :],
                               qk_dram[which, part, b, own, :].rearrange("(h d) t -> d h t", d=HD), f"qk_in{s}")
            qk_loaded[u] = m

        ring_s = Ring([banks[:, n, :] for n in range(4)])
        def maxima(u, h):
            q, k, out = q_st[u % 4], k_st[u % 4], top[u % 2]
            if h == 0:
                PE.wait(qk_loaded[u])
                DVE.wait(top_split.get(u - 2))

            def block(bank, at, h, qt):
                keys = (qt + 1) * P
                PE.do(lambda e: e.matmul(bank[:, at:at + keys], q[0:STACK, h, qt * P:qt * P + P],
                                         k[0:STACK, h, 0:keys], start=True, stop=False))
                return PE.do(lambda e: e.matmul(bank[:, at + keys - P:at + keys], ident_b, mask_b,
                                                start=False, stop=True), "scores")

            def reduce(out_, in_, mark):
                DVE.wait(mark)
                return DVE.do(lambda e: e.tensor_reduce(out_, in_, AX.X, ALU.max, negate=True), "maxima")

            n, bank = ring_s.take(PE)
            m = block(bank, 0, h, 3)
            ring_s.give(n, reduce(out[:, h, 3:4], bank, m))
            yield
            n, bank = ring_s.take(PE)
            block(bank, 0, h, 0)
            m = block(bank, P, h, 2)
            reduce(out[:, h, 0:1], bank[:, 0:P], m)
            ring_s.give(n, reduce(out[:, h, 2:3], bank[:, P:T], m))
            yield
            if h % 2:
                n, bank = ring_s.take(PE)
                block(bank, 0, h - 1, 1)
                m = block(bank, 2 * P, h, 1)
                got = reduce(out[:, h - 1:h + 1, 1], bank.rearrange("p (h k) -> p h k", h=2), m)
                ring_s.give(n, got)
                top_done[u] = got
                yield

        top_done, top_split = {}, {}

        def rest(steps):
            for _ in range(steps):
                yield

        def place_maxima(u):
            src = top[u % 2]
            DVE.wait(top_done[u], top_turned.get(u - 1))
            m = DVE.do(lambda e: e.tensor_copy(top_part[:, 0], src), "top")
            yield
            DVE.wait(m)
            m = DVE.do(lambda e: e.tensor_tensor(top_rest, src, top_part[:, 0], ALU.subtract), "top")
            yield
            DVE.wait(m)
            m = DVE.do(lambda e: e.tensor_copy(top_part[:, 1], top_rest), "top")
            yield
            DVE.wait(m)
            top_split[u] = DVE.do(lambda e: e.tensor_tensor(top_part[:, 2], top_rest, top_part[:, 1], ALU.subtract), "top")
            yield from rest(REST_TOP)
            PE.wait(top_split[u])
            n, bank = ring_s.take(PE)
            rows_ = MAXROWS * HG * TT
            m = PE.do(lambda e: e.transpose(bank.bitcast(BF16)[0:rows_, 0:P],
                                            top_part.rearrange("p s h t -> p (s h t)"), ident_b), "top_turned")
            top_turned[u] = m
            ACTE.wait(m, top_loaded.get(u - 1))
            m = ACTE.do(lambda e: e.copy(top_T[0:rows_, :], bank.bitcast(BF16)[0:rows_, 0:P]), "top_T")
            ring_s.give(n, m)
            SP.wait(m)
            for s in range(MAXROWS):
                m = SP.dma(q_st[u % 4][STACK + s:STACK + s + 1, :, :].rearrange("o h (t c) -> o (h t) c", c=P),
                           top_T[s * HG * TT:(s + 1) * HG * TT, :], "top_in")
            top_loaded[u] = m

        top_turned = {}
        REST_TOP, REST_SPLIT, REST_BETA, REST_TURN, REST_P = 7, 12, 10, 0, 0

        def open_attention():
            for u in range(2):
                for h in range(HG):
                    yield from maxima(u, h)
            yield from place_maxima(0)

        MIDDLE = range(2, E - LATE)
        a1 = Area(weights, MIDDLE.start * EW, MIDDLE.stop * EW)
        x_in = [a1.take(TT * D, t=TT, d=D) for _ in range(2)]
        x_norm = [a1.take(TT * D, t=TT, d=D) for _ in range(2)]
        x_T = [a1.take(KC * T, k=KC, t=T) for _ in range(2)]
        w_qkv = a1.take(KC * 3 * D, k=KC, n=3 * D)
        b_qk = a1.take(2 * KC)
        b_v = a1.take(D)
        qk_32 = [a1.take(T) for _ in range(2)]
        qk_rest = [a1.take(T) for _ in range(2)]
        qk_part = [a1.take(3 * T // 2, BF16, s=3, t=T) for _ in range(4)]
        v_out = [a1.take(TT * H * 2 * HD, t=TT, h=H, d=2 * HD) for _ in range(1)]
        moments_1 = a1.take(TT * 6, t=TT, s=6)
        mean_var_1 = a1.take(TT * 2, t=TT, s=2)
        newton_1 = [a1.take(TT) for _ in range(3)]

        ring_T = ring_v = Ring([banks[:, 4, :], banks[:, 7, :]])
        ring_qk = Ring([banks[:, n, :] for n in range(5, 7)])

        x_free = [None, None]
        norm_free = [None, None]
        xT_free = [None, None]
        part_free = [None] * 4
        v_free = [None]
        x_loaded, x_ready, xT_ready = {}, {}, {}

        wqkv_loaded = None

        def load_x(b):
            ACTE.wait(x_free[b % 2])
            x_loaded[b] = ACTE.dma(x_in[b % 2], t["L0_attn_x"][b].rearrange("(t p) d -> p t d", p=P), f"x_in{b % 2}")

        load_x(0)
        SP.dma(w_qkv, t["L0_attn_W_qkv"].rearrange("(k p) n -> p k n", p=P), "w_qkv")
        bias = t["L0_attn_b_qkv"]
        SP.dma(b_qk, bias[0:2 * D].rearrange("(c p) -> p c", p=P), "w_qkv", allow_slow_non_contiguous=True)
        wqkv_loaded = SP.dma(b_v, rows_of(bias[2 * D:3 * D]), "w_qkv")
        load_x(1)
        SP.wait(numbers)
        SP.dma(gamma, rows_of(t["L0_ffn_gamma"]), "vectors")
        SP.dma(beta, rows_of(t["L0_ffn_beta"]), "vectors")
        SP.dma(b_out, rows_of(t["L0_attn_b_out"]), "vectors")
        SP.dma(w_out, t["L0_attn_W_out"].rearrange("(k p) n -> p k n", p=P), "vectors")
        SP.dma(gate_w, t["L0_ffn_gate_w"].rearrange("(k p) e -> p k e", p=P), "vectors")
        vectors = SP.dma(b1_sb, t["L0_ffn_b1"].rearrange("e (c p) -> p e c", p=P), "vectors",
                         allow_slow_non_contiguous=True)


        def normalise(b):
            src, dst = x_in[b % 2], x_norm[b % 2]
            DVE.wait(x_loaded[b], norm_free[b % 2])
            for tt in range(TT):
                m = DVE.do(lambda e, tt=tt: e.bn_stats(moments_1[:, tt, :], src[:, tt, :]), "norm")
                yield
            DVE.wait(m)
            for tt in range(TT):
                m = DVE.do(lambda e, tt=tt: e.bn_aggr(mean_var_1[:, tt, :], moments_1[:, tt, :]), "norm")
            yield
            DVE.wait(m)
            m = DVE.do(lambda e: e.tensor_scalar(newton_1[0], mean_var_1[:, :, 1], EPS, None, ALU.add), "norm")
            yield
            m = yield from rsqrt(m, newton_1, "norm")
            yield
            DVE.wait(m)
            for tt in range(TT):
                m = DVE.do(lambda e, tt=tt: e.tensor_scalar(dst[:, tt, :], src[:, tt, :], mean_var_1[:, tt, 0:1],
                                                            newton_1[1][:, tt:tt + 1], ALU.subtract, ALU.mult), "norm")
                yield
            x_free[b % 2] = x_ready[b] = m

        def turn(b):
            PE.wait(x_ready[b], consts_pool)
            ACTE.wait(xT_free[b % 2])
            src, dst = x_norm[b % 2], x_T[b % 2]
            for k in range(KC):
                n, bank = ring_T.take(PE)
                for tt in range(TT):
                    m = PE.do(lambda e, k=k, tt=tt, bank=bank: e.transpose(
                        bank[:, tt * P:(tt + 1) * P], src[:, tt, k * P:(k + 1) * P], ident), "turned" if tt == TT - 1 else None)
                ACTE.wait(m)
                out = ACTE.do(lambda e, k=k, bank=bank: e.copy(dst[:, k, :], bank), "xT")
                ring_T.give(n, out)
            norm_free[b % 2] = m
            xT_ready[b] = out

        chunk = 0

        def project(b):
            nonlocal chunk
            following = normalise(b + 1) if b + 1 < B else iter(())
            src = x_T[b % 2]
            PE.wait(xT_ready[b], wqkv_loaded)
            ACTE.wait(bias_scaled)
            for c in range(2 * KC):
                n, bank = ring_qk.take(PE)
                for k in range(KC):
                    m = PE.do(lambda e, k=k, c=c, bank=bank: e.matmul(
                        bank, w_qkv[:, k, c * P:(c + 1) * P], src[:, k, :], start=(k == 0), stop=(k == KC - 1)),
                        "qk" if k == KC - 1 else None)
                i, j = chunk % 2, chunk % 4
                chunk += 1
                full, rest, part = qk_32[i], qk_rest[i], qk_part[j]
                ACTE.wait(m, parts_done.get(chunk - 2), part_free[j])
                got = ACTE.do(lambda e, c=c, bank=bank, full=full: e.activation(
                    full, bank, ACT.Identity, bias=b_qk[:, c:c + 1], scale=SCALE if c < KC else 1.0), "qk_32")
                ring_qk.give(n, got)
                last["qk_32"] = got
                ACTE.wait(got)
                high = ACTE.do(lambda e, full=full, part=part: e.copy(part[:, 0, :], full), "qk_high")
                for _ in range(STEPS_A_CHUNK):
                    next(following, None)
                    next(opening, None)
                DVE.wait(high, lows_done.get(chunk - 2))
                m = DVE.do(lambda e, full=full, rest=rest, part=part: e.tensor_tensor(
                    rest, full, part[:, 0, :], ALU.subtract), "qk_rest")
                parts_done[chunk] = m
                DVE.wait(m)
                mid = DVE.do(lambda e, rest=rest, part=part: e.tensor_copy(part[:, 1, :], rest), "qk_mid")
                POOL.wait(mid)
                low = POOL.do(lambda e, rest=rest, part=part: e.tensor_tensor(
                    part[:, 2, :], rest, part[:, 1, :], ALU.subtract), "qk_low")
                lows_done[chunk] = last["qk_low"] = low
                SP.wait(low)
                which, rows = c // KC, slice((c % KC) * P, (c % KC + 1) * P)
                part_free[j] = SP.dma(qk_dram[which, :, b, rows, :].rearrange("s p t -> p s t"), part, f"qk_store{j}")
                stored_qk[b, c] = part_free[j]
            for half in range(2):
                n, bank = ring_v.take(PE)
                for s in range(2):
                    tt = half * 2 + s
                    for k in range(KC):
                        m = PE.do(lambda e, k=k, tt=tt, s=s, bank=bank: e.matmul(
                            bank[:, s * D:(s + 1) * D], src[:, k, tt * P:(tt + 1) * P], w_qkv[:, k, 2 * D:3 * D],
                            start=(k == 0), stop=(k == KC - 1)), "v" if (s, k) == (1, KC - 1) else None)
                DVE.wait(m, v_free[0])
                got = DVE.do(lambda e, half=half, bank=bank: e.tensor_tensor(
                    v_out[0][:, 2 * half:2 * half + 2, :, 0:HD], bank.rearrange("p (s h d) -> p s h d", s=2, d=HD),
                    b_v.rearrange("p (h d) -> p h d", d=HD).unsqueeze(1).broadcast_to([P, 2, H, HD]), ALU.add), "v_add")
                ring_v.give(n, got)
            last["v_add"], last["v"] = got, m
            for _ in following:
                pass
            if b + 1 < B:
                turn(b + 1)
            xT_free[b % 2] = m
            SP.wait(got)
            v_free[0] = stored_v[b] = SP.dma(v_dram[b].rearrange("(t p) n -> p t n", p=P), v_out[0].rearrange("p t h d -> p t (h d)"),
                                                 "v_store")

        parts_done, lows_done, last = {}, {}, {}

        w_sb = weights[:, :].rearrange("p (e w) -> p e w", e=E)

        def load_weights(e_, m):
            w_loaded[e_, m] = ACTE.dma(
                w_sb[:, e_, m * EW // 2:(m + 1) * EW // 2].rearrange("p (c n) -> p c n", c=(KC, FC)[m]),
                t[("L0_ffn_w1", "L0_ffn_w2")[m]][e_].rearrange("(c p) n -> p c n", p=P), f"w_in{m}{e_}")

        w_loaded = {}

        def magnitude(e_, m):
            DVE.wait(w_loaded[e_, m])
            return DVE.do(lambda e: e.tensor_reduce(tops[:, m, e_:e_ + 1], w_sb[:, e_, m * EW // 2:(m + 1) * EW // 2],
                                                    AX.X, ALU.max, apply_absolute_value=True), "tops")

        matrices = [(e_, m) for e_ in [*range(E - LATE, E), *range(E - LATE)] for m in range(2)]
        EARLY = B
        STEPS_A_CHUNK = 8
        opening = iter(())
        whole(normalise(0))
        turn(0)
        DVE.wait(wqkv_loaded)
        bias_scaled = DVE.do(lambda e: e.tensor_scalar(b_qk[:, 0:KC], b_qk[:, 0:KC], SCALE, None, ALU.mult), "bias")
        v_ones = [DVE.do(lambda e, v=v: e.memset(v[:, :, :, HD:2 * HD], 1.0), "v_ones") for v in v_out][-1]
        for s in range(4):
            ones_set = DVE.do(lambda e, s=s: e.memset(k_st[s][STACK:P, :, :], 1.0), "ones_set")
        for tt in range(TT):
            POOL.do(lambda e, tt=tt: e.memset(b2_pad[tt], 0.0), "set")
        is_set = POOL.do(lambda e: e.memset(cw_pad, 0.0), "set")
        SP.wait(is_set)
        for tt in range(TT):
            b2_loaded = SP.dma(b2_pad[tt][32 * tt:32 * tt + E, :], t["L0_ffn_b2"], "b2_in")
        m = DVE.do(lambda e: e.memset(rows[:, :, :], 0.0), "spare")
        SP.wait(m)
        spare_rows = SP.dma(rows_dram[N:N + P, :], rows[:, 0, :], "spare_rows")
        SP.wait(spare_rows)
        spare_acc = SP.dma(acc_dram[N:N + P, :], rows[:, 0, 0:D], "spare_acc")

        for b in range(B):
            if b + 2 < B:
                load_x(b + 2)
            if b < EARLY:
                load_weights(*matrices[b])
            if b == 4:
                opening = open_attention()
            project(b)
            if 1 < b < 5:
                load_unit(b - 2)
            if b < EARLY:
                tops_done = magnitude(*matrices[b])
                if b == 2 * LATE - 1:
                    lent_free = tops_done
        for _ in opening:
            pass
        banks_read = (xT_ready[B - 1], last["qk_32"], last["v_add"])
        a1_free = (last["v"], last["v_add"], last["qk_low"], *part_free, *v_free)

        S_TOP, S_SCALE, S_TMP, S_UNDO = stat[:, 0:8], stat[:, 8:12], stat[:, 16:24], stat[:, 24:28]
        UNDO_1, UNDO_2 = stat[:, 28:29], stat[:, 29:30]
        SCALE_W = [S_SCALE[:, 0:1], S_SCALE[:, 1:2]]
        SCALE_X, SCALE_H = S_SCALE[:, 2:3], S_SCALE[:, 3:4]

        def find_scales(tops_done):
            DVE.wait(vectors, tops_done)
            m = DVE.do(lambda e: e.tensor_reduce(S_TMP[:, 0:2], tops, AX.X, ALU.max), "scale")
            DVE.do(lambda e: e.tensor_reduce(S_TMP[:, 2:3], gamma, AX.X, ALU.max, apply_absolute_value=True), "scale")
            DVE.do(lambda e: e.tensor_reduce(S_TMP[:, 3:4], beta, AX.X, ALU.max, apply_absolute_value=True), "scale")
            m = DVE.do(lambda e: e.tensor_reduce(S_TMP[:, 4:5], b1_sb, AX.XY, ALU.max, apply_absolute_value=True), "scale")
            POOL.wait(m)
            m = POOL.do(lambda e: e.partition_all_reduce(S_TOP[:, 0:5], S_TMP[:, 0:5], P, bass.bass_isa.ReduceOp.max), "scale_all")
            DVE.wait(m)
            root = math.ceil(math.sqrt(D))
            m = DVE.do(lambda e: e.scalar_tensor_tensor(S_TOP[:, 2:3], S_TOP[:, 2:3], float(root), S_TOP[:, 3:4],
                                                        ALU.mult, ALU.add), "scale")
            DVE.wait(m)
            m = DVE.do(lambda e: e.scalar_tensor_tensor(S_TOP[:, 3:4], S_TOP[:, 2:3], float(D), S_TOP[:, 0:1],
                                                        ALU.mult, ALU.mult), "scale")
            DVE.wait(m)
            m = DVE.do(lambda e: e.tensor_tensor(S_TOP[:, 3:4], S_TOP[:, 3:4], S_TOP[:, 4:5], ALU.add), "scale")
            DVE.wait(m)
            m = DVE.do(lambda e: e.tensor_scalar(S_TMP[:, 0:4].bitcast(I32), S_TOP[:, 0:4].bitcast(I32), 23, None,
                                                 ALU.logical_shift_right), "scale")
            DVE.wait(m)
            m = DVE.do(lambda e: e.tensor_scalar(S_TMP[:, 0:4].bitcast(I32), S_TMP[:, 0:4].bitcast(I32), 80.0, 200.0,
                                                 ALU.max, ALU.min), "scale")
            DVE.wait(m)
            m = DVE.do(lambda e: e.tensor_scalar(S_TMP[:, 4:8].bitcast(I32), S_TMP[:, 0:4].bitcast(I32), -1.0,
                                                 float(127 * 2 + 14), ALU.mult, ALU.add), "scale")
            m2 = DVE.do(lambda e: e.tensor_scalar(S_TMP[:, 0:4].bitcast(I32), S_TMP[:, 0:4].bitcast(I32), -14.0, None,
                                                  ALU.add), "scale")
            DVE.wait(m, m2)
            DVE.do(lambda e: e.tensor_scalar(S_SCALE.bitcast(I32), S_TMP[:, 4:8].bitcast(I32), 23, None,
                                             ALU.logical_shift_left), "scale")
            m = DVE.do(lambda e: e.tensor_scalar(S_UNDO.bitcast(I32), S_TMP[:, 0:4].bitcast(I32), 23, None,
                                                 ALU.logical_shift_left), "scale")
            DVE.wait(m)
            DVE.do(lambda e: e.tensor_tensor(UNDO_1, S_UNDO[:, 0:1], S_UNDO[:, 2:3], ALU.mult), "scale")
            scales = DVE.do(lambda e: e.tensor_tensor(UNDO_2, S_UNDO[:, 1:2], S_UNDO[:, 3:4], ALU.mult), "scale")
            return scales

        def meet():
            marks = [(s, s.count) for s in pool.values() if s.count]
            for lane in LANES:
                lane.wait(*marks)
        ring_p = Ring([banks[:, n, :] for n in range(4, 7)], banks_read)
        ring_o = Ring([banks[:, 7, :]])

        def load_v(u):
            b, g = divmod(u, NG)
            own = slice(g * HG * 2 * HD, (g + 1) * HG * 2 * HD)
            SP.wait(vone_free[u % 2], stored_v[b])
            v_ready[u] = SP.dma(v_one[u % 2].rearrange("p t h d -> p t (h d)"),
                                v_dram[b].rearrange("(t p) n -> p t n", p=P)[:, :, own], f"v_in{u % 2}")

        def exponentials(u, h, pair):
            q, k = q_st[u % 4], k_st[u % 4]
            ROWS = STACK + MAXROWS
            if h == 0:
                PE.wait(top_loaded[u], ones_set)

            def block(h, out_, kt):
                return PE.do(lambda e: e.matmul(out_, k[0:ROWS, h, kt * P:kt * P + P], q[0:ROWS, h, kt * P:T],
                                                start=True, stop=True), "scores_T")

            slot = 2 * (pair % 3) + h % 2
            if h % 2 == 0:
                ACTE.wait(*pair_free[pair % 3], lent_free)
            for at, chunks in ((0, ((0, 0),)), (T, ((3, 0), (1, P)))):
                n, bank = ring_p.take(PE)
                for kt, to in chunks:
                    m = block(h, bank[:, to:to + T - kt * P], kt)
                ACTE.wait(m)
                m = ACTE.do(lambda e, at=at, bank=bank: e.activation(p_T[:, slot, at:at + T], bank, ACT.Exp), "exp")
                ring_p.give(n, m)
                yield
            if h % 2:
                n, bank = ring_p.take(PE)
                block(h - 1, bank[:, 0:2 * P], 2)
                st_free[u % 4] = m = block(h, bank[:, 2 * P:T], 2)
                ACTE.wait(m)
                m = ACTE.do(lambda e, bank=bank: e.activation(p_T[:, slot - 1:slot + 1, 2 * T:PT_LEN],
                                                              bank.rearrange("p (h c) -> p h c", h=2), ACT.Exp), "exp")
                ring_p.give(n, m)
                POOL.wait(m)
                both = p_T[:, slot - 1:slot + 1, :]
                for area, pattern in ((both[:, :, 0:P], [[0, 2], [1, P]]),
                                      (both[:, :, T:T + 2 * P], [[0, 2], [0, 2], [1, P]]),
                                      (both[:, :, 2 * T:2 * T + P], [[0, 2], [1, P]])):
                    m = POOL.do(lambda e, area=area, pattern=pattern: e.affine_select(
                        out=area, in_=area, compare_op=ALU.is_ge, fill=0.0, base=0, pattern=pattern,
                        channel_multiplier=-1), "masked")
                pair_ready[pair] = m
                yield

        def weigh(u):
            yield from rest(REST_P)
            b, g = divmod(u, NG)
            vv = v_one[u % 2]
            n, bank = ring_o.take(PE)
            PE.wait(v_ready[u], pair_ready[2 * u], pair_ready[2 * u + 1])
            for kt in range(TT):
                for h in range(HG):
                    slot = 2 * ((2 * u + h // 2) % 3) + h % 2
                    a, w = PT_AT[kt], T - kt * P
                    m = PE.do(lambda e, h=h, kt=kt, slot=slot, a=a, w=w: e.matmul(
                        bank[32 * h:32 * h + 32, kt * P:T], vv[:, kt, h, :], p_T[:, slot, a:a + w],
                        start=(kt == 0), stop=(kt == TT - 1), tile_position=(0, 32 * h)),
                        "weighed" if (kt, h) == (TT - 1, HG - 1) else None)
                if kt < TT - 1:
                    yield
            vone_free[u % 2] = m
            for pair in (2 * u, 2 * u + 1):
                pair_free[pair % 3] = (m,)
            ACTE.wait(m, o_turned[0])
            m = ACTE.do(lambda e: e.copy(o_T, bank), "o_T")
            ring_o.give(n, m)
            copied[u] = m

        copied, divided = {}, {}

        def divide(u):
            b, g = divmod(u, NG)
            while u not in copied:
                yield
            PE.wait(copied[u])
            n, bank = ring_s.take(PE)
            for qt in range(TT):
                m = PE.do(lambda e, qt=qt: e.transpose(bank[:, qt * P:qt * P + P], o_T[:, qt * P:qt * P + P], ident),
                          "o_turned" if qt == TT - 1 else None)
            o_turned[0] = m
            yield
            sums = bank.rearrange("p (t h d) -> p t h d", t=TT, h=HG)
            DVE.wait(m, o_rows_free[0], recip_free[0])
            m = DVE.do(lambda e: e.reciprocal(recip, sums[:, :, :, HD]), "divide")
            DVE.wait(m)
            m = DVE.do(lambda e: e.tensor_tensor(
                o_rows[:, :, g * HG * HD:(g + 1) * HG * HD].rearrange("p t (h d) -> p t h d", h=HG),
                sums[:, :, :, 0:HD], recip.unsqueeze(3).broadcast_to([P, TT, HG, HD]), ALU.mult), "divide")
            recip_free[0] = divided[u] = m
            ring_s.give(n, m)

        o_rows_free, recip_free = [None], [None]
        x_again, x2_free = {}, [None]
        rows_free, turned_free, z_free, cw_free = [spare_acc], [None], [None], [None]

        def load_again(b):
            SP.wait(x2_free[0])
            x_again[b] = SP.dma(x2, t["L0_attn_x"][b].rearrange("(t p) d -> p t d", p=P), "x_again")

        def over_tiles(vec):
            return vec.unsqueeze(1).broadcast_to([P, TT, vec.shape[1]])

        def column(c, n):
            return c.unsqueeze(2).broadcast_to([P, TT, n])

        def turn_rows(src, ready, name):
            PE.wait(ready)
            ACTE.wait(turned_free[0])
            for k in range(KC):
                n, bank = ring_s.take(PE)
                for tt in range(TT):
                    m = PE.do(lambda e, k=k, tt=tt, bank=bank: e.transpose(
                        bank[:, tt * P:(tt + 1) * P], src[:, tt, k * P:(k + 1) * P], ident), name if tt == TT - 1 else None)
                ACTE.wait(m)
                out = ACTE.do(lambda e, k=k, bank=bank: e.copy(turned[:, k, :], bank), "turned")
                ring_s.give(n, out)
                yield
            yield from rest(REST_TURN)
            return m, out

        def finish(b):
            POOL.wait(x_again[b])
            with_bias = POOL.do(lambda e: e.tensor_tensor(x2, x2, over_tiles(b_out), ALU.add), "with_bias")
            while (b + 1) * NG - 1 not in divided:
                yield
            o_rows_free[0], out = yield from turn_rows(o_rows, divided[(b + 1) * NG - 1], "rows_turned")
            PE.wait(out)
            for half in range(2):
                n, bank = ring_s.take(PE)
                for s in range(2):
                    tt = 2 * half + s
                    for k in range(KC):
                        m = PE.do(lambda e, k=k, tt=tt, s=s, bank=bank: e.matmul(
                            bank[:, s * D:(s + 1) * D], turned[:, k, tt * P:(tt + 1) * P], w_out[:, k, :],
                            start=(k == 0), stop=(k == KC - 1)), "w_out" if (s, k) == (1, KC - 1) else None)
                    if (half, s) == (1, 1):
                        turned_free[0] = m
                    yield
                DVE.wait(m, with_bias)
                got = DVE.do(lambda e, half=half, bank=bank: e.tensor_tensor(
                    x2[:, 2 * half:2 * half + 2, :], bank.rearrange("p (s d) -> p s d", s=2),
                    x2[:, 2 * half:2 * half + 2, :], ALU.add), "x2")
                ring_s.give(n, got)
            yield
            DVE.wait(got)
            for tt in range(TT):
                m = DVE.do(lambda e, tt=tt: e.bn_stats(moments[:, tt, :], x2[:, tt, :]), "norms")
                yield
            DVE.wait(m)
            for tt in range(TT):
                m = DVE.do(lambda e, tt=tt: e.bn_aggr(mean_var[:, tt, :], moments[:, tt, :]), "norms")
            yield
            (s1, s2), (y1, y2) = (newton[0][:, 0, :], newton[0][:, 1, :]), (newton[1][:, 0, :], newton[1][:, 1, :])
            DVE.wait(m)
            m = DVE.do(lambda e: e.tensor_scalar(s1, mean_var[:, :, 1], EPS, None, ALU.add), "norms")
            yield
            DVE.wait(m)
            m = DVE.do(lambda e: e.scalar_tensor_tensor(s2, s1, EPS, mean_var[:, :, 1], ALU.mult, ALU.add), "norms")
            yield
            m = yield from rsqrt(m, newton, "norms")
            yield
            DVE.wait(m)
            m = DVE.do(lambda e: e.scalar_tensor_tensor(shift, mean_var[:, :, 0], -1.0, y1, ALU.mult, ALU.mult), "norms")
            ACTE.wait(m, z_free[0])
            for tt in range(TT):
                z_done = ACTE.do(lambda e, tt=tt: e.activation(
                    z[:, tt, :], x2[:, tt, :], ACT.Identity, bias=shift[:, tt:tt + 1], scale=y1[:, tt:tt + 1]), "z")
            m = DVE.do(lambda e: e.tensor_tensor(rstd_z, s1, y1, ALU.mult), "norms")
            yield
            DVE.wait(m)
            m = DVE.do(lambda e: e.tensor_tensor(rstd_z, rstd_z, y2, ALU.mult), "norms")
            yield from rest(4)
            DVE.wait(z_done, m, *rows_free)
            for tt in range(TT):
                m = DVE.do(lambda e, tt=tt: e.scalar_tensor_tensor(
                    rows[:, tt, 0:D], z[:, tt, :], rstd_z[:, tt:tt + 1], gamma, ALU.mult, ALU.mult), "norms")
                yield
            POOL.wait(m)
            normed = POOL.do(lambda e: e.tensor_tensor(rows[:, :, 0:D], rows[:, :, 0:D], over_tiles(beta), ALU.add), "beta")
            yield
            m = POOL.do(lambda e: e.tensor_tensor(z, z, x2, ALU.add), "residual")
            x2_free[0] = residual = m
            if b + 1 < B:
                load_again(b + 1)
            yield
            yield from rest(REST_BETA)
            tiles = slice(b * TT, (b + 1) * TT)
            _, out = yield from turn_rows(rows, normed, "gate_turned")
            PE.wait(out)
            n, bank = ring_s.take(PE)
            for tt in range(TT):
                for k in range(KC):
                    m = PE.do(lambda e, k=k, tt=tt, bank=bank: e.matmul(
                        bank[:, tt * E:(tt + 1) * E], turned[:, k, tt * P:(tt + 1) * P], gate_w[:, k, :],
                        start=(k == 0), stop=(k == KC - 1)), "gate" if (tt, k) == (TT - 1, KC - 1) else None)
            turned_free[0] = m
            yield
            DVE.wait(m)
            m = DVE.do(lambda e, bank=bank: e.tensor_copy(logit, bank[:, 0:TT * E].rearrange("p (t e) -> p t e", t=TT)), "choose")
            ring_s.give(n, m)
            step = [m]

            def then(emit):
                DVE.wait(step[0])
                step[0] = DVE.do(emit, "choose")

            first, second, order, gap, one, w1 = col
            pick1, pick2 = choice[:, tiles, 0, :], choice[:, tiles, 1, :]
            for top_, src, pick in ((first, logit, pick1), (second, g2, pick2)):
                then(lambda e, top_=top_, src=src: e.tensor_reduce(top_, src, AX.X, ALU.max))
                yield
                then(lambda e, top_=top_, src=src: e.tensor_tensor(g1, src, column(top_, E), ALU.is_ge))
                yield
                then(lambda e: e.tensor_tensor(g1, g1, over_tiles(prefer), ALU.mult))
                yield
                then(lambda e: e.tensor_reduce(order, g1, AX.X, ALU.max))
                yield
                then(lambda e, pick=pick: e.tensor_tensor(pick, g1, column(order, E), ALU.is_equal))
                yield
                if pick is pick1:
                    then(lambda e: e.scalar_tensor_tensor(g2, pick1, -3.0e38, logit, ALU.mult, ALU.add))
                    yield
            then(lambda e: e.tensor_tensor(gap, second, first, ALU.subtract))
            yield
            ACTE.wait(step[0])
            step[0] = ACTE.do(lambda e: e.activation(gap, gap, ACT.Exp), "gate_exp")
            yield from rest(3)
            then(lambda e: e.tensor_scalar(one, gap, 1.0, None, ALU.add))
            yield
            then(lambda e: e.reciprocal(w1, one))
            yield
            then(lambda e: e.tensor_tensor(gap, gap, w1, ALU.mult))
            yield
            then(lambda e: e.tensor_tensor(g1, pick1, column(w1, E), ALU.mult))
            yield
            then(lambda e: e.tensor_tensor(g2, pick2, column(gap, E), ALU.mult))
            yield
            DVE.wait(cw_free[0])
            then(lambda e: e.tensor_tensor(rows[:, :, D:ROW], g1, g2, ALU.add))
            yield
            then(lambda e: e.tensor_tensor(cw_pad[:, :, 0:E], g1, g2, ALU.add))
            yield
            SP.wait(step[0], normed)
            m = SP.dma(rows_dram[b * T:(b + 1) * T, :].rearrange("(t p) d -> p t d", p=P), rows, "rows_out")
            rows_free[:] = [m, out]
            yield
            PE.wait(step[0])
            n, bank = ring_s.take(PE)
            m = PE.do(lambda e, bank=bank: e.transpose(bank[:, 0:P], cw_pad.rearrange("p t e -> p (t e)"), ident), "cw_turned")
            cw_free[0] = m
            ACTE.wait(m)
            m = ACTE.do(lambda e, bank=bank: e.copy(cw_T, bank[:, 0:P]), "cw_T")
            ring_s.give(n, m)
            yield
            PE.wait(m, b2_loaded)
            DVE.wait(residual)
            for half in range(2):
                n, bank = ring_s.take(PE)
                for s in range(2):
                    m = PE.do(lambda e, s=s, bank=bank, tt=2 * half + s: e.matmul(
                        bank[:, s * D:(s + 1) * D], cw_T, b2_pad[tt], start=True, stop=True), "b2")
                yield
                DVE.wait(m)
                got = DVE.do(lambda e, half=half, bank=bank: e.tensor_tensor(
                    z[:, 2 * half:2 * half + 2, :], bank.rearrange("p (s d) -> p s d", s=2),
                    z[:, 2 * half:2 * half + 2, :], ALU.add), "base")
                ring_s.give(n, got)
            SP.wait(got)
            z_free[0] = SP.dma(acc_dram[b * T:(b + 1) * T, :].rearrange("(t p) d -> p t d", p=P), z, "acc_out")

        HALF = EW // 4
        w_16 = weights[:, :].bitcast(F16).rearrange("p (e m k s w) -> p e m k s w", e=E, m=2, k=2, s=2)
        split_free = [None, None]

        def split_weights(e_, m_, k_, high, low):
            src = w_sb[:, e_, m_ * EW // 2 + k_ * HALF:m_ * EW // 2 + (k_ + 1) * HALF]
            ACTE.wait(scales, *split_free)
            m = ACTE.do(lambda e: e.activation(src, src, ACT.Copy, scale=SCALE_W[m_]), "w_scaled")
            yield
            ACTE.wait(m)
            m = ACTE.do(lambda e: e.copy(high, src), "w_high")
            yield
            POOL.wait(m)
            m = POOL.do(lambda e: e.tensor_tensor(low, src, high, ALU.subtract), "w_low")
            yield from rest(REST_SPLIT)
            DVE.wait(m)
            DVE.do(lambda e: e.tensor_copy(w_16[:, e_, m_, k_, 0, :], high), "w_split")
            m = DVE.do(lambda e: e.tensor_copy(w_16[:, e_, m_, k_, 1, :], low), "w_split")
            split_free[:] = [m, m]

        splits = [(e_, m_, k_) for e_ in range(E - LATE) for m_ in range(2) for k_ in range(2)]

        load_again(0)
        scales = None
        tops_line, weigh_line, divide_line, finish_line, split_line = [], [], [], [], []
        lines = (tops_line, weigh_line, divide_line, finish_line, split_line)

        def advance():
            for line in lines:
                if line and next(line[0], "done") == "done":
                    line.pop(0)

        for i in range(UNITS + 1):
            if i < UNITS:
                load_v(i)
            if i + 3 < UNITS:
                load_unit(i + 3)
            if i + 1 < UNITS:
                tops_line.append(place_maxima(i + 1))
            for h in range(HG):
                both = [maxima(i + 2, h) if i + 2 < UNITS else iter(()), exponentials(i, h, 2 * i + h // 2) if i < UNITS else iter(())]
                for _ in range(3):
                    for part in both:
                        next(part, None)
                        advance()
                if h == 0 and i > 0:
                    weigh_line.append(weigh(i - 1))
                if h == 1 and i > 0:
                    divide_line.append(divide(i - 1))
                    if i % NG == 0:
                        finish_line.append(finish(i // NG - 1))
                if h == 2 and i + EARLY < len(matrices):
                    if matrices[i + EARLY][0] in MIDDLE:
                        ACTE.wait(*a1_free)
                    load_weights(*matrices[i + EARLY])
                if h == 3 and 0 < i <= len(matrices) - EARLY:
                    tops_done = magnitude(*matrices[i - 1 + EARLY])
                    if i == len(matrices) - EARLY:
                        scales = find_scales(tops_done)
                if h == 1 and i > len(matrices) - EARLY and splits:
                    split_line.append(split_weights(*splits.pop(0), w_high, w_low))
        while splits:
            split_line.append(split_weights(*splits.pop(0), w_high, w_low))
        while any(lines):
            advance()
        meet()
        for late in matrices[:2 * LATE]:
            load_weights(*late)
        a3 = Area(arena, HEAD, WORDS)
        NE = NT * E
        chosen = a3.take(NE // 2, BF16)
        totals = a3.take(NE, i=NT, e=E)
        before = a3.take(NE, i=NT, e=E)
        ones_i = a3.take(NT)
        counts = a3.take(E)
        tiles_e, ends = a3.take(E), a3.take(E)
        base = a3.take(E)
        by_choice = a3.take(NT * TOPK * E, i=NT, k=TOPK, e=E)
        slot = a3.take(NT * TOPK)
        slot_row, slot_col = a3.take(NT * TOPK), a3.take(NT * TOPK)
        slot_int = a3.take(NT * TOPK, I32)
        in_row = a3.take(NT * TOPK * P // 2, BF16, n=NT * TOPK, q=P)
        in_col = a3.take(NT * TOPK * SC, BF16, n=NT * TOPK, v=2, c=SC)
        ended = a3.take(TILES * E, j=TILES, e=E)
        tile_f = a3.take(TILES)
        found = a3.take(2 * SC, v=2, c=SC)
        real = a3.take(SC)
        spare = a3.take(1)
        temp = Area(arena, a3.at, WORDS)
        w_high_late, w_low_late = temp.take(EW // 8, F16), temp.take(EW // 8, F16)

        step = [None]

        def then3(emit):
            DVE.wait(step[0])
            step[0] = DVE.do(emit, "route")

        then3(lambda e: e.tensor_tensor(chosen.rearrange("p (i e) -> p i e", i=NT), choice[:, :, 0, :], choice[:, :, 1, :], ALU.add))
        then3(lambda e: e.memset(ones_i, 1.0))
        PE.wait(step[0])
        PE.do(lambda e: e.matmul(banks[:, 0, 0:NE], upper_b, chosen, start=True, stop=True))
        m = PE.do(lambda e: e.matmul(banks[:, 1, 0:NE], ones_b, chosen, start=True, stop=True), "counted")
        DVE.wait(m)
        tile_pairs = banks[:, 1, 0:NE].rearrange("p (i e) -> p i e", i=NT)
        for e_ in range(E):
            then3(lambda e, e_=e_: e.tensor_tensor_scan(totals[:, :, e_], ones_i, tile_pairs[:, :, e_], 0.0, ALU.mult, ALU.add))
        then3(lambda e: e.tensor_copy(counts, totals[:, NT - 1, :]))
        then3(lambda e: e.tensor_tensor(totals, totals, tile_pairs, ALU.subtract))
        then3(lambda e: e.tensor_tensor(before, totals, banks[:, 0, 0:NE].rearrange("p (i e) -> p i e", i=NT), ALU.add))
        then3(lambda e: e.tensor_scalar(base.bitcast(I32), counts, float(TILE - 1), None, ALU.add))
        then3(lambda e: e.tensor_scalar(base.bitcast(I32), base.bitcast(I32), TILE.bit_length() - 1, None, ALU.logical_shift_right))
        then3(lambda e: e.tensor_copy(tiles_e, base.bitcast(I32)))
        then3(lambda e: e.tensor_tensor_scan(ends, ones_i[:, 0:E], tiles_e, 0.0, ALU.mult, ALU.add))
        then3(lambda e: e.tensor_tensor(base, ends, tiles_e, ALU.subtract))
        then3(lambda e: e.tensor_scalar(base, base, float(TILE), None, ALU.mult))
        then3(lambda e: e.tensor_tensor(before, before, base.unsqueeze(1).broadcast_to([P, NT, E]), ALU.add))
        then3(lambda e: e.tensor_tensor(by_choice[:, :, 0, :], choice[:, :, 0, :], before, ALU.mult))
        then3(lambda e: e.tensor_tensor(by_choice[:, :, 1, :], choice[:, :, 1, :], before, ALU.mult))
        then3(lambda e: e.tensor_reduce(slot, by_choice.rearrange("p i k e -> p (i k) e"), AX.X, ALU.add))
        then3(lambda e: e.tensor_copy(slot_int, slot))
        then3(lambda e: e.tensor_scalar(slot_int, slot_int, 7, None, ALU.logical_shift_right))
        then3(lambda e: e.tensor_copy(slot_col, slot_int))
        then3(lambda e: e.scalar_tensor_tensor(slot_row, slot_col, float(-P), slot, ALU.mult, ALU.add))
        DVE.wait(step[0])
        for n in range(NT * TOPK):
            DVE.do(lambda e, n=n: e.tensor_scalar(in_row[:, n, :], iota_row, slot_row[:, n:n + 1], None, ALU.is_equal), "in_col")
            DVE.do(lambda e, n=n: e.tensor_scalar(in_col[:, n, 0, :], iota_row[:, 0:SC], slot_col[:, n:n + 1],
                                                  float(n // TOPK + 1), ALU.is_equal, ALU.mult), "in_col")
            col_ready = DVE.do(lambda e, n=n: e.tensor_scalar(in_col[:, n, 1, :], iota_row[:, 0:SC], slot_col[:, n:n + 1],
                                                              iota_part, ALU.is_equal, ALU.mult), "in_col")
            PE.wait(col_ready)
            m = PE.do(lambda e, n=n: e.matmul(banks[:, 2, 0:2 * SC], in_row[:, n, :], in_col[:, n].rearrange("p v c -> p (v c)"),
                                              start=(n == 0), stop=(n == NT * TOPK - 1)), "table" if n == NT * TOPK - 1 else None)
        then3(lambda e: e.tensor_tensor(ended, iota_row[:, 0:TILES].unsqueeze(2).broadcast_to([P, TILES, E]),
                                        ends.unsqueeze(1).broadcast_to([P, TILES, E]), ALU.is_ge))
        then3(lambda e: e.tensor_reduce(tile_f, ended, AX.X, ALU.add))
        then3(lambda e: e.tensor_scalar(tile_f, tile_f, float(E - 1), None, ALU.min))
        then3(lambda e: e.tensor_copy(tile_of, tile_f))
        tiles_known = step[0]
        then3(lambda e: e.tensor_tensor(hot, iota_row[:, 0:E].unsqueeze(1).broadcast_to([P, TILES, E]),
                                        tile_f.unsqueeze(2).broadcast_to([P, TILES, E]), ALU.is_equal))
        then3(lambda e: e.tensor_scalar(hot, hot, UNDO_2, None, ALU.mult))
        DVE.wait(m)
        then3(lambda e: e.tensor_copy(found, banks[:, 2, 0:2 * SC].rearrange("p (v c) -> p v c", v=2)))
        then3(lambda e: e.tensor_scalar(real, found[:, 0, :], 0.0, None, ALU.is_gt))
        then3(lambda e: e.scalar_tensor_tensor(found[:, 1, :], found[:, 0, :], float(P), found[:, 1, :], ALU.mult, ALU.add))
        then3(lambda e: e.tensor_scalar(spare, iota_part, float(N + P), None, ALU.add))
        then3(lambda e: e.tensor_scalar(found[:, 1, :], found[:, 1, :], spare, None, ALU.subtract))
        then3(lambda e: e.tensor_tensor(found[:, 1, :], found[:, 1, :], real, ALU.mult))
        then3(lambda e: e.tensor_scalar(spare, iota_part, float(N), None, ALU.add))
        then3(lambda e: e.tensor_scalar(found[:, 1, :], found[:, 1, :], spare, None, ALU.add))
        then3(lambda e: e.tensor_copy(slot_token, found[:, 1, :]))
        table_ready = step[0]

        split_free[:] = [None, None]
        for e_, m_ in matrices[:2 * LATE]:
            ACTE.wait(w_loaded[e_, m_])
            for k_ in range(2):
                for _ in split_weights(e_, m_, k_, w_high_late, w_low_late):
                    pass

        meet()
        a4 = Area(arena, HEAD, WORDS)
        gathered = [a4.take(TC * ROW, c=TC, d=ROW) for _ in range(3)]
        xt_high = [a4.take(KC * TILE // 2, F16, k=KC, s=TILE) for _ in range(2)]
        xt_low = [a4.take(KC * TILE // 2, F16, k=KC, s=TILE) for _ in range(2)]
        w1_now = [a4.take(EW // 2, F16, k=KC, s=2, w=F) for _ in range(2)]
        w2_now = [a4.take(EW // 2, F16, k=2, s=2, c=FC // 2, n=D) for _ in range(2)]
        b1_now = [a4.take(FC) for _ in range(2)]
        h_32 = [a4.take(2 * TILE, c=2, s=TILE) for _ in range(2)]
        h_high = [a4.take(FC * TILE // 2, F16, c=FC, s=TILE) for _ in range(1)]
        h_low = [a4.take(FC * TILE // 2, F16, c=FC, s=TILE) for _ in range(1)]
        y = [a4.take(TC * D, c=TC, d=D) for _ in range(2)]
        share = a4.take(TC * E, c=TC, e=E)
        weight = [a4.take(TC) for _ in range(2)]
        ring_x = Ring([banks[:, 0, :]])
        ring_h = Ring([banks[:, n, :] for n in range(1, 6)])
        ring_y = Ring([banks[:, n, :] for n in range(6, 8)])

        gathered_free = [()] * 3
        gather_done, x_split, staged_1, staged_2, staged_b = {}, {}, {}, {}, {}
        xt_free, w1_free, w2_free, b1_free, y_free = [None] * 2, [None] * 2, [None] * 2, [None] * 2, [None] * 2
        h32_free, h_free = [None] * 2, [None]
        h_ready, added, weight_ready = {}, {}, {}
        h_count = 0

        def gather(j):
            s = j % 3
            POOL.wait(*gathered_free[s])
            for c in range(TC):
                gather_done[j] = POOL.indirect(f"gathered{s}", gathered[s][:, c, :], None, rows_dram[:, :],
                                               bass.IndirectOffsetOnAxis(slot_token[:, TC * j + c:TC * j + c + 1], 0))

        def stage_expert(j):
            s = j % 2
            DVE.wait(w1_free[s], w2_free[s], b1_free[s])

            box = []
            DVE.do(lambda e: box.append(e.value_load(tile_of[0:1, j:j + 1], min_val=0, max_val=E - 1)))
            flat = weights[:, :].bitcast(F16)
            staged_1[j] = DVE.do(lambda e: e.tensor_copy(w1_now[s].rearrange("p k s w -> p (k s w)"),
                                                         flat[:, bass.ds(box[0] * (2 * EW), EW)]), "staged")
            staged_b[j] = DVE.do(lambda e: e.tensor_copy(b1_now[s], b1_sb.rearrange("p e c -> p (e c)")[:, bass.ds(box[0] * FC, FC)]), "staged")
            staged_2[j] = DVE.do(lambda e: e.tensor_copy(w2_now[s].rearrange("p k s c n -> p (k s c n)"),
                                                         flat[:, bass.ds(box[0] * (2 * EW) + EW, EW)]), "staged")

        def turn_tokens(j):
            g = gathered[j % 3]
            PE.wait(gather_done[j])
            n, bank = ring_x.take(PE)
            for k in range(KC):
                for c in range(TC):
                    m = PE.do(lambda e, k=k, c=c: e.transpose(bank[:, k * TILE + c * P:k * TILE + (c + 1) * P],
                                                              g[:, c, k * P:(k + 1) * P], ident), "x_turned")
            turned_mark = m
            s = j % 2
            both = bank.rearrange("p (k s) -> p k s", k=KC)
            ACTE.wait(m, xt_free[s])
            m = ACTE.do(lambda e: e.activation(xt_high[s], both, ACT.Copy, scale=SCALE_X), "xt_high")
            DVE.wait(m)
            x_split[j] = DVE.do(lambda e: e.scalar_tensor_tensor(xt_low[s], both, SCALE_X, xt_high[s], ALU.mult, ALU.subtract), "xt_low")
            ring_x.give(n, x_split[j])
            DVE.wait(gather_done[j], y_weighted.get(j - 2))
            m = DVE.do(lambda e: e.tensor_tensor(share, g[:, :, D:ROW], hot[:, j:j + 1, :].broadcast_to([P, TC, E]), ALU.mult), "share")
            DVE.wait(m)
            weight_ready[j] = DVE.do(lambda e: e.tensor_reduce(weight[s], share, AX.X, ALU.add), "share")
            gathered_free[j % 3] = (turned_mark, m)

        y_weighted = {}

        def hidden(j):
            nonlocal h_count
            s = j % 2
            w1, xh, xl = w1_now[s], xt_high[s], xt_low[s]
            PE.wait(staged_1[j], x_split[j])
            for c2 in range(FC // 2):
                n, bank = ring_h.take(PE)
                for c in range(2):
                    f = (2 * c2 + c) * P
                    terms = [(k, wp, xp) for k in range(KC) for wp, xp in ((0, xh), (0, xl), (1, xh))]
                    for i, (k, wp, xp) in enumerate(terms):
                        m = PE.do(lambda e, k=k, wp=wp, xp=xp, f=f, c=c, i=i, bank=bank: e.matmul(
                            bank[:, c * TILE:(c + 1) * TILE], w1[:, k, wp, f:f + P], xp[:, k, :],
                            start=(i == 0), stop=(i == len(terms) - 1)), "hidden" if i == len(terms) - 1 else None)
                r = h_count % 2
                h_count += 1
                ACTE.wait(m, h32_free[r], staged_b[j])
                for c in range(2):
                    m2 = ACTE.do(lambda e, c=c, c2=c2, r=r, bank=bank: e.activation(
                        h_32[r][:, c, :], bank[:, c * TILE:(c + 1) * TILE], ACT.Gelu,
                        bias=b1_now[s][:, 2 * c2 + c:2 * c2 + c + 1], scale=UNDO_1), "gelu")
                ring_h.give(n, m2)
                DVE.wait(m2, h_free[0])
                m3 = DVE.do(lambda e, c2=c2, r=r: e.tensor_scalar(h_high[0][:, 2 * c2:2 * c2 + 2, :], h_32[r], SCALE_H, None,
                                                                  ALU.mult), "h_high")
                DVE.wait(m3)
                h_ready[j, c2] = h32_free[r] = DVE.do(lambda e, c2=c2, r=r: e.scalar_tensor_tensor(
                    h_low[0][:, 2 * c2:2 * c2 + 2, :], h_32[r], SCALE_H, h_high[0][:, 2 * c2:2 * c2 + 2, :], ALU.mult, ALU.subtract), "h_low")
            w1_free[s] = xt_free[s] = m
            b1_free[s] = m2

        def expert_out(j):
            s = j % 2
            w2 = w2_now[s]
            n, bank = ring_y.take(PE)
            PE.wait(staged_2[j])
            for c in range(TC):
                for f in range(FC):
                    PE.wait(h_ready[j, f // 2])
                    for i, (hp, wp) in enumerate(((h_high[0], 0), (h_high[0], 1), (h_low[0], 0))):
                        last = (f, i) == (FC - 1, 2)
                        m = PE.do(lambda e, f=f, c=c, i=i, hp=hp, wp=wp, last=last: e.matmul(
                            bank[:, c * D:(c + 1) * D], hp[:, f, c * P:(c + 1) * P],
                            w2[:, f // (FC // 2), wp, f % (FC // 2), :], start=(f == 0 and i == 0), stop=last),
                            "expert_out" if last else None)
            h_free[0] = w2_free[s] = m
            DVE.wait(m, y_free[s], weight_ready[j])
            for c in range(TC):
                m = DVE.do(lambda e, c=c: e.tensor_scalar(y[s][:, c, :], bank[:, c * D:(c + 1) * D], weight[s][:, c:c + 1], None,
                                                          ALU.mult), "y")
            ring_y.give(n, m)
            y_weighted[j] = m
            POOL.wait(m, added.get(j - 1))
            for c in range(TC):
                if c:
                    POOL.wait(added[j])
                added[j] = POOL.indirect("added", acc_dram[:, :], bass.IndirectOffsetOnAxis(slot_token[:, TC * j + c:TC * j + c + 1], 0),
                                         y[s][:, c, :], None, compute_op=ALU.add)
            y_free[s] = added[j]

        for j in range(2):
            gather(j)
        stage_expert(0)
        turn_tokens(0)
        hidden(0)
        for j in range(TILES):
            if j + 2 < TILES:
                gather(j + 2)
            if j + 1 < TILES:
                stage_expert(j + 1)
                turn_tokens(j + 1)
            expert_out(j)
            if j + 1 < TILES:
                hidden(j + 1)

        SP.wait(added[TILES - 1])
        done = SP.dma(t["out"].rearrange("b t d -> (b t) d"), acc_dram[0:N, :], "out")
        SP.wait(done)
        block = ctx.enter_context(nc.Block())
        for lane, where in zip(LANES, (block.tensor, block.scalar, block.vector, block.gpsimd, block.sync)):
            where(lambda engine, lane=lane: lane.play(engine))


_INS = ["L0_attn_x", "L0_attn_W_qkv", "L0_attn_b_qkv", "L0_attn_W_out", "L0_attn_b_out", "L0_ffn_gate_w",
        "L0_ffn_w1", "L0_ffn_b1", "L0_ffn_w2", "L0_ffn_b2", "L0_ffn_gamma", "L0_ffn_beta"]


def kernel(**inputs):
    import numpy as np
    from concourse import bacc
    from concourse.bass_utils import run_bass_kernel_spmd

    nc = bacc.Bacc("TRN2", target_bir_lowering=False, num_devices=1)
    arrays, tensors = {}, {}
    for name in _INS:
        a = np.ascontiguousarray(inputs[name])
        arrays[f"in_{name}"] = a
        tensors[name] = nc.dram_tensor(f"in_{name}", a.shape, mybir.dt.from_np(a.dtype), kind="ExternalInput").ap()
    shape = inputs["L0_attn_x"].shape
    tensors["out"] = nc.dram_tensor("out", shape, F32, kind="ExternalOutput").ap()
    build(nc, tensors)
    got = run_bass_kernel_spmd(nc, [arrays], core_ids=[0])
    return got.results[0]["out"]
```

```python
import math
from contextlib import ExitStack
from itertools import chain

import concourse.bass as bass
import concourse.mybir as mybir

ALU = mybir.AluOpType
ACT = mybir.ActivationFunctionType
AX = mybir.AxisListType
F32 = mybir.dt.float32
F16 = mybir.dt.float16
BF16 = mybir.dt.bfloat16
I32 = mybir.dt.int32

P = 128
NEG = -1.0e30
EPS = 1e-5


class Signal:

    def __init__(self, sem):
        self.sem, self.count = sem, 0

    def after(self, step):
        self.count += step
        return self, self.count


class Lane:

    def __init__(self, signals):
        self.items, self.signals, self.seen = [], signals, {}

    def do(self, emit, name=None):
        if name is None:
            self.items.append(emit)
            return None
        mark = self.signals(name).after(1)
        self.items.append(lambda e: emit(e).then_inc(mark[0].sem, 1))
        return mark

    def dma(self, out, in_, name, **how):
        mark = self.signals(name).after(16)
        self.items.append(lambda e: e.dma_start(out, in_, **how).then_inc(mark[0].sem, 16))
        return mark

    def indirect(self, name, *what, **how):
        mark = self.signals(name).after(16)
        self.items.append(lambda e: e.indirect_dma_start(*what, **how).then_inc(mark[0].sem, 16))
        return mark

    def wait(self, *marks):
        for mark in marks:
            if mark is None or self.seen.get(mark[0], 0) >= mark[1]:
                continue
            self.seen[mark[0]] = mark[1]
            self.items.append(lambda e, mark=mark: e.wait_ge(mark[0].sem, mark[1]))

    def play(self, engine):
        for item in self.items:
            item(engine)


class Ring:

    def __init__(self, buffers, free=()):
        self.buffers, self.free, self.next = buffers, [free] * len(buffers), 0

    def take(self, lane):
        n = self.next % len(self.buffers)
        self.next += 1
        assert self.free[n] is not None
        lane.wait(*self.free[n])
        self.free[n] = None
        return n, self.buffers[n]

    def give(self, n, *marks):
        self.free[n] = marks


def whole(steps):
    while True:
        try:
            next(steps)
        except StopIteration as end:
            return end.value


def build(nc, t):
    B, T, D = t["L0_attn_x"].shape
    E, _, F = t["L0_ffn_w1"].shape
    HD = 16
    H = D // HD
    SCALE = HD ** -0.5
    KC = D // P
    FC = F // P
    TT = T // P
    NT = B * TT
    N = B * T
    HG = 4
    NG = H // HG
    TOPK = 2
    TILE = 256
    TC = TILE // P
    TILES = N * TOPK // TILE + E - 1
    SC = TILES * TC
    LOCAL = N // P
    assert N <= 4096
    ROW = D + E
    PARTS = 3
    STACK = PARTS * (PARTS + 1) // 2 * HD
    MAXROWS = 3
    EW = 2 * KC * F

    ctx = ExitStack()
    with ctx:
        pool = {}

        def signals(name):
            if name not in pool:
                pool[name] = Signal(ctx.enter_context(nc.semaphore(name)))
            return pool[name]

        PE, ACTE, DVE, POOL, SP = (Lane(signals) for _ in range(5))
        LANES = (PE, ACTE, DVE, POOL, SP)

        def dram(name, shape, dt):
            return nc.dram_tensor(name, shape, dt).ap()

        qk_dram = dram("qk_parts", (2, B, H, PARTS, HD, T), BF16)
        v_dram = dram("v_rows", (B, T, 2 * D), F32)
        rows_dram = dram("token_rows", (N + P, ROW), F32)
        acc_dram = dram("result_rows", (N + P, D), F32)

        weights = ctx.enter_context(nc.sbuf_tensor("weights", [P, E * EW], F32))
        WORDS = 20440
        arena = ctx.enter_context(nc.sbuf_tensor("arena", [P, WORDS], F32))
        banks = ctx.enter_context(nc.psum_tensor("banks", [P, 8, 512], F32))

        class Area:

            def __init__(self, base, start, end):
                self.base, self.at, self.end = base, start, end

            def take(self, words, dt=F32, **dims):
                a, self.at = self.at, self.at + words
                assert self.at <= self.end, (self.at, self.end)
                v = self.base[:, a:a + words]
                if dt != F32:
                    v = v.bitcast(dt)
                if dims:
                    names = list(dims)
                    v = v.rearrange(f"p ({' '.join(names)}) -> p {' '.join(names)}",
                                    **{k: dims[k] for k in names[1:]})
                return v

        keep = Area(arena, 0, 3000)
        ident = keep.take(P)
        ident_b = keep.take(P // 2, BF16)
        mask_b = keep.take(P // 2, BF16)
        upper_b = keep.take(P // 2, BF16)
        ones_b = keep.take(P // 2, BF16)
        iota_part = keep.take(1)
        prefer = keep.take(E)
        gamma = keep.take(D)
        beta = keep.take(D)
        b_out = keep.take(D)
        w_out = keep.take(KC * D, k=KC, n=D)
        gate_w = keep.take(KC * E, k=KC, e=E)
        iota_16 = keep.take((E * LOCAL + P) // 2, F16)
        codes = keep.take(NT)
        table = keep.take(E * LOCAL, e=E, c=LOCAL)
        running = keep.take(E)
        b1_sb = keep.take(E * FC, e=E, c=FC)
        stat = keep.take(32)
        tops = keep.take(2 * E, m=2, e=E)
        KEPT = keep.at
        hot = keep.take(TILES * E, j=TILES, e=E)
        tile_of = keep.take(TILES, I32)
        slot_token = keep.take(SC, I32)

        HEAD = keep.at
        c_zero = POOL.do(lambda e: e.memset(arena[:, 0:2 * P], 0.0), "const")
        c_ones = POOL.do(lambda e: e.memset(ones_b, 1.0), "const")
        c_upper = POOL.do(lambda e: e.memset(upper_b, 1.0), "const")
        POOL.wait(c_zero, c_ones, c_upper)
        POOL.do(lambda e: e.affine_select(out=ident, in_=ident, compare_op=ALU.not_equal, fill=1.0,
                                          base=0, pattern=[[-1, P]], channel_multiplier=1), "const")
        POOL.do(lambda e: e.affine_select(out=ident_b, in_=ident_b, compare_op=ALU.not_equal, fill=1.0,
                                          base=0, pattern=[[-1, P]], channel_multiplier=1), "const")
        POOL.do(lambda e: e.affine_select(out=mask_b, in_=mask_b, compare_op=ALU.is_ge, fill=NEG,
                                          base=0, pattern=[[-1, P]], channel_multiplier=1), "const")
        POOL.do(lambda e: e.affine_select(out=upper_b, in_=upper_b, compare_op=ALU.is_gt, fill=0.0,
                                          base=0, pattern=[[1, P]], channel_multiplier=-1), "const")
        POOL.do(lambda e: e.iota(b_out[:, 0:P].bitcast(I32), [[1, P]], base=0, channel_multiplier=0), "const")
        POOL.do(lambda e: e.iota(b_out[:, P:P + 1].bitcast(I32), [[0, 1]], base=0, channel_multiplier=1), "const")
        POOL.do(lambda e: e.iota(b_out[:, P + 1:P + 1 + E].bitcast(I32), [[-1, E]], base=E, channel_multiplier=0), "const")
        POOL.do(lambda e: e.iota(b_out[:, 2 * P - NT:2 * P].bitcast(I32), [[P, NT]], base=-N // 2, channel_multiplier=1), "const")
        consts_pool = POOL.do(lambda e: e.iota(w_out[:, 0, :].bitcast(I32), [[1, D]], base=-E * LOCAL, channel_multiplier=0), "const")
        DVE.wait(consts_pool)
        DVE.do(lambda e: e.tensor_copy(iota_part, b_out[:, P:P + 1].bitcast(I32)), "numbers")
        DVE.do(lambda e: e.tensor_copy(iota_16[:, 0:D], w_out[:, 0, :].bitcast(I32)), "numbers")
        DVE.do(lambda e: e.tensor_copy(iota_16[:, E * LOCAL:], b_out[:, 0:P].bitcast(I32)), "numbers")
        DVE.do(lambda e: e.tensor_copy(codes[:, 0:NT // 2], b_out[:, 2 * P - NT:2 * P - NT // 2].bitcast(I32)), "numbers")
        DVE.do(lambda e: e.tensor_scalar(codes[:, NT // 2:NT], b_out[:, 2 * P - NT // 2:2 * P].bitcast(I32), 1.0, None, ALU.add), "numbers")
        DVE.do(lambda e: e.memset(table, 0.0), "numbers")
        DVE.do(lambda e: e.memset(running, 0.0), "numbers")
        numbers = DVE.do(lambda e: e.tensor_copy(prefer, b_out[:, P + 1:P + 1 + E].bitcast(I32)), "numbers")

        def rows_of(vector):
            return vector.partition_broadcast(P)

        def rsqrt(ready, scratch, name):
            s, y, u = scratch
            DVE.wait(ready)
            m = DVE.do(lambda e: e.tensor_scalar(y.bitcast(I32), s.bitcast(I32), 1, None,
                                                 ALU.logical_shift_right), name)
            yield
            DVE.wait(m)
            m = DVE.do(lambda e: e.tensor_scalar(y.bitcast(I32), y.bitcast(I32), -1.0, float(0x5F3759DF),
                                                 ALU.mult, ALU.add), name)
            for _ in range(3):
                yield
                DVE.wait(m)
                m = DVE.do(lambda e: e.scalar_tensor_tensor(u, y, -0.5, y, ALU.mult, ALU.mult), name)
                yield
                DVE.wait(m)
                m = DVE.do(lambda e: e.tensor_tensor(u, u, s, ALU.mult), name)
                yield
                DVE.wait(m)
                m = DVE.do(lambda e: e.scalar_tensor_tensor(y, u, 1.5, y, ALU.add, ALU.mult), name)
            return m

        stored_qk, stored_v = {}, {}
        LATE = 2
        a2 = Area(arena, KEPT, WORDS)
        lent = Area(weights, (E - LATE) * EW, E * EW)
        q_st = [a2.take(HG * T // 2, BF16, h=HG, t=T) for _ in range(4)]
        k_st = [a2.take(HG * T // 2, BF16, h=HG, t=T) for _ in range(4)]
        v_one = [a2.take(TT * HG * 2 * HD, t=TT, h=HG, d=2 * HD) for _ in range(2)]
        PT_AT, PT_LEN = (0, 640, 1024, 512), TT * (TT + 1) // 2 * P
        p_T = lent.take(6 * PT_LEN, h=6, c=PT_LEN)
        o_T = a2.take(T)
        o_rows = a2.take(TT * D, t=TT, d=D)
        turned = a2.take(KC * T, k=KC, t=T)
        x2 = a2.take(TT * D, t=TT, d=D)
        z = a2.take(TT * D, t=TT, d=D)
        rows = a2.take(TT * ROW, t=TT, d=ROW)
        b2_pad = [a2.take(D) for tt in range(TT)]
        w_high, w_low = a2.take(EW // 8, F16), a2.take(EW // 8, F16)
        top = [a2.take(HG * TT, h=HG, t=TT) for _ in range(2)]
        top_rest = a2.take(HG * TT, h=HG, t=TT)
        top_part = a2.take(MAXROWS * HG * TT // 2, BF16, s=MAXROWS, h=HG, t=TT)
        top_T = a2.take(P // 2, BF16)
        recip = a2.take(TT * HG, t=TT, h=HG)
        moments = a2.take(TT * 6, t=TT, s=6)
        mean_var = a2.take(TT * 2, t=TT, s=2)
        newton = [a2.take(2 * TT, n=2, t=TT) for _ in range(3)]
        shift, rstd_z = a2.take(TT), a2.take(TT)
        logit = a2.take(TT * E, t=TT, e=E)
        g1, g2 = a2.take(TT * E, t=TT, e=E), a2.take(TT * E, t=TT, e=E)
        col = [a2.take(TT) for _ in range(6)]
        choice = a2.take(TT * TOPK * E, t=TT, k=TOPK, e=E)
        orders = a2.take(TT * TOPK, t=TT, k=TOPK)
        chosen = a2.take(TT * E // 2, BF16, t=TT, e=E)
        before = a2.take(TT * E, t=TT, e=E)
        by_choice = a2.take(TT * TOPK * E, t=TT, k=TOPK, e=E)
        rank, rank_int, chunk_f, slot_row, slot_col = (a2.take(TT * TOPK, dt, t=TT, k=TOPK) for dt in (F32, I32, F32, F32, F32))
        in_row = [a2.take(P // 2, F16) for _ in range(TOPK)]
        in_col = [a2.take(E * LOCAL // 2, F16) for _ in range(TOPK)]
        cw_pad = a2.take(TT * 32, t=TT, e=32)
        cw_T = a2.take(P); assert a2.at<=WORDS

        UNITS = B * NG
        qk_loaded, top_loaded, v_ready = {}, {}, {}
        st_free, vone_free = [None] * 4, [None] * 2
        pair_free = [()] * 3
        pair_ready = {}
        o_turned = [None]

        def load_unit(u):
            b, g = divmod(u, NG)
            s = u % 4
            SP.wait(st_free[s], stored_qk[b, g // 2], stored_qk[b, KC + g // 2])
            row = 0
            for count in range(1, PARTS + 1):
                here = slice(row, row + count * HD)
                row += count * HD
                for stack, which, first in ((q_st[s], 0, 0), (k_st[s], 1, PARTS - count)):
                    m = SP.dma(stack[here, :, :], qk_dram[which, b, g * HG:(g + 1) * HG, first:first + count, :, :]
                               .rearrange("h s d t -> (s d) h t"), f"qk_in{s}")
                yield
            qk_loaded[u] = m

        ring_s = Ring([banks[:, n, :] for n in range(4)])

        def maxima(u, h):
            q, k, out = q_st[u % 4], k_st[u % 4], top[u % 2]
            if h == 0:
                PE.wait(qk_loaded[u])
                DVE.wait(top_split.get(u - 2))

            def block(bank, at, h, qt):
                keys = (qt + 1) * P
                PE.do(lambda e: e.matmul(bank[:, at:at + keys], q[0:STACK, h, qt * P:qt * P + P],
                                         k[0:STACK, h, 0:keys], start=True, stop=False))
                return PE.do(lambda e: e.matmul(bank[:, at + keys - P:at + keys], ident_b, mask_b,
                                                start=False, stop=True), "scores")

            def reduce(out_, in_, mark):
                DVE.wait(mark)
                return DVE.do(lambda e: e.tensor_reduce(out_, in_, AX.X, ALU.max, negate=True), "maxima")

            n, bank = ring_s.take(PE)
            m = block(bank, 0, h, 3)
            ring_s.give(n, reduce(out[:, h, 3:4], bank, m))
            yield
            n, bank = ring_s.take(PE)
            block(bank, 0, h, 0)
            m = block(bank, P, h, 2)
            reduce(out[:, h, 0:1], bank[:, 0:P], m)
            ring_s.give(n, reduce(out[:, h, 2:3], bank[:, P:T], m))
            yield
            if h % 2:
                n, bank = ring_s.take(PE)
                block(bank, 0, h - 1, 1)
                m = block(bank, 2 * P, h, 1)
                got = reduce(out[:, h - 1:h + 1, 1], bank.rearrange("p (h k) -> p h k", h=2), m)
                ring_s.give(n, got)
                top_done[u] = got
                yield

        top_done, top_split, top_turned = {}, {}, {}
        REST_TOP, REST_SPLIT, REST_BETA, REST_TURN, REST_P = 9, 12, 13, 5, 2
        REST_LATE, REST_COUNT, REST_TABLE, LOAD_FROM = 7, 5, 7, 4

        def rest(steps):
            for _ in range(steps):
                yield

        def place_maxima(u):
            src = top[u % 2]
            DVE.wait(top_done[u], top_turned.get(u - 1))
            m = DVE.do(lambda e: e.tensor_copy(top_part[:, 0], src), "top")
            yield
            DVE.wait(m)
            m = DVE.do(lambda e: e.tensor_tensor(top_rest, src, top_part[:, 0], ALU.subtract), "top")
            yield
            DVE.wait(m)
            m = DVE.do(lambda e: e.tensor_copy(top_part[:, 1], top_rest), "top")
            yield
            DVE.wait(m)
            top_split[u] = DVE.do(lambda e: e.tensor_tensor(top_part[:, 2], top_rest, top_part[:, 1], ALU.subtract), "top")
            yield from rest(REST_TOP)
            PE.wait(top_split[u])
            n, bank = ring_s.take(PE)
            rows_ = MAXROWS * HG * TT
            m = PE.do(lambda e: e.transpose(bank.bitcast(BF16)[0:rows_, 0:P],
                                            top_part.rearrange("p s h t -> p (s h t)"), ident_b), "top_turned")
            top_turned[u] = m
            ACTE.wait(m, top_loaded.get(u - 1))
            m = ACTE.do(lambda e: e.copy(top_T[0:rows_, :], bank.bitcast(BF16)[0:rows_, 0:P]), "top_T")
            ring_s.give(n, m)
            SP.wait(m)
            for s in range(MAXROWS):
                m = SP.dma(q_st[u % 4][STACK + s:STACK + s + 1, :, :].rearrange("o h (t c) -> o (h t) c", c=P),
                           top_T[s * HG * TT:(s + 1) * HG * TT, :], "top_in")
            top_loaded[u] = m

        def open_attention():
            for u in range(2):
                for h in range(HG):
                    yield from maxima(u, h)
            yield from place_maxima(0)

        MIDDLE = range(2, E - LATE)
        a1 = Area(weights, MIDDLE.start * EW, MIDDLE.stop * EW)
        x_in = [a1.take(TT * D, t=TT, d=D) for _ in range(2)]
        x_norm = [a1.take(TT * D, t=TT, d=D) for _ in range(2)]
        x_T = [a1.take(KC * T, k=KC, t=T) for _ in range(2)]
        w_qkv = a1.take(KC * 3 * D, k=KC, n=3 * D)
        b_qk = a1.take(2 * KC)
        b_v = a1.take(D)
        qk_32 = [a1.take(T) for _ in range(2)]
        qk_rest = [a1.take(T) for _ in range(2)]
        qk_part = [a1.take(3 * T // 2, BF16, s=3, t=T) for _ in range(4)]
        v_out = [a1.take(TT * H * 2 * HD, t=TT, h=H, d=2 * HD) for _ in range(1)]
        moments_1 = a1.take(TT * 6, t=TT, s=6)
        mean_var_1 = a1.take(TT * 2, t=TT, s=2)
        newton_1 = [a1.take(TT) for _ in range(3)]

        ring_T = ring_v = Ring([banks[:, 4, :], banks[:, 7, :]])
        ring_qk = Ring([banks[:, n, :] for n in range(5, 7)])

        x_free = [None, None]
        norm_free = [None, None]
        xT_free = [None, None]
        part_free = [None] * 4
        v_free = [None]
        x_loaded, x_ready, xT_ready = {}, {}, {}

        wqkv_loaded = None

        def load_x(b):
            ACTE.wait(x_free[b % 2])
            x_loaded[b] = ACTE.dma(x_in[b % 2], t["L0_attn_x"][b].rearrange("(t p) d -> p t d", p=P), f"x_in{b % 2}")

        load_x(0)
        SP.dma(w_qkv, t["L0_attn_W_qkv"].rearrange("(k p) n -> p k n", p=P), "w_qkv")
        bias = t["L0_attn_b_qkv"]
        SP.dma(b_qk, bias[0:2 * D].rearrange("(c p) -> p c", p=P), "w_qkv", allow_slow_non_contiguous=True)
        wqkv_loaded = SP.dma(b_v, rows_of(bias[2 * D:3 * D]), "w_qkv")
        load_x(1)
        SP.wait(numbers)
        SP.dma(gamma, rows_of(t["L0_ffn_gamma"]), "vectors")
        SP.dma(beta, rows_of(t["L0_ffn_beta"]), "vectors")
        SP.dma(b_out, rows_of(t["L0_attn_b_out"]), "vectors")
        SP.dma(w_out, t["L0_attn_W_out"].rearrange("(k p) n -> p k n", p=P), "vectors")
        SP.dma(gate_w, t["L0_ffn_gate_w"].rearrange("(k p) e -> p k e", p=P), "vectors")
        vectors = SP.dma(b1_sb, t["L0_ffn_b1"].rearrange("e (c p) -> p e c", p=P), "vectors",
                         allow_slow_non_contiguous=True)


        def normalise(b):
            src, dst = x_in[b % 2], x_norm[b % 2]
            DVE.wait(x_loaded[b], norm_free[b % 2])
            for tt in range(TT):
                m = DVE.do(lambda e, tt=tt: e.bn_stats(moments_1[:, tt, :], src[:, tt, :]), "norm")
                yield
            DVE.wait(m)
            for tt in range(TT):
                m = DVE.do(lambda e, tt=tt: e.bn_aggr(mean_var_1[:, tt, :], moments_1[:, tt, :]), "norm")
            yield
            DVE.wait(m)
            m = DVE.do(lambda e: e.tensor_scalar(newton_1[0], mean_var_1[:, :, 1], EPS, None, ALU.add), "norm")
            yield
            m = yield from rsqrt(m, newton_1, "norm")
            yield
            DVE.wait(m)
            for tt in range(TT):
                m = DVE.do(lambda e, tt=tt: e.tensor_scalar(dst[:, tt, :], src[:, tt, :], mean_var_1[:, tt, 0:1],
                                                            newton_1[1][:, tt:tt + 1], ALU.subtract, ALU.mult), "norm")
                yield
            x_free[b % 2] = x_ready[b] = m

        def turn(b):
            PE.wait(x_ready[b], consts_pool)
            ACTE.wait(xT_free[b % 2])
            src, dst = x_norm[b % 2], x_T[b % 2]
            for k in range(KC):
                n, bank = ring_T.take(PE)
                for tt in range(TT):
                    m = PE.do(lambda e, k=k, tt=tt, bank=bank: e.transpose(
                        bank[:, tt * P:(tt + 1) * P], src[:, tt, k * P:(k + 1) * P], ident), "turned" if tt == TT - 1 else None)
                ACTE.wait(m)
                out = ACTE.do(lambda e, k=k, bank=bank: e.copy(dst[:, k, :], bank), "xT")
                ring_T.give(n, out)
            norm_free[b % 2] = m
            xT_ready[b] = out

        chunk = 0

        def project(b):
            nonlocal chunk
            following = normalise(b + 1) if b + 1 < B else iter(())
            src = x_T[b % 2]
            PE.wait(xT_ready[b], wqkv_loaded)
            ACTE.wait(bias_scaled)
            for c in range(2 * KC):
                n, bank = ring_qk.take(PE)
                for k in range(KC):
                    m = PE.do(lambda e, k=k, c=c, bank=bank: e.matmul(
                        bank, w_qkv[:, k, c * P:(c + 1) * P], src[:, k, :], start=(k == 0), stop=(k == KC - 1)),
                        "qk" if k == KC - 1 else None)
                i, j = chunk % 2, chunk % 4
                chunk += 1
                full, rest, part = qk_32[i], qk_rest[i], qk_part[j]
                ACTE.wait(m, parts_done.get(chunk - 2), part_free[j])
                got = ACTE.do(lambda e, c=c, bank=bank, full=full: e.activation(
                    full, bank, ACT.Identity, bias=b_qk[:, c:c + 1], scale=SCALE if c < KC else 1.0), "qk_32")
                ring_qk.give(n, got)
                last["qk_32"] = got
                ACTE.wait(got)
                high = ACTE.do(lambda e, full=full, part=part: e.copy(part[:, 0, :], full), "qk_high")
                for _ in range(STEPS_A_CHUNK):
                    next(following, None)
                    next(opening, None)
                DVE.wait(high, lows_done.get(chunk - 2))
                m = DVE.do(lambda e, full=full, rest=rest, part=part: e.tensor_tensor(
                    rest, full, part[:, 0, :], ALU.subtract), "qk_rest")
                parts_done[chunk] = m
                DVE.wait(m)
                mid = DVE.do(lambda e, rest=rest, part=part: e.tensor_copy(part[:, 1, :], rest), "qk_mid")
                POOL.wait(mid)
                low = POOL.do(lambda e, rest=rest, part=part: e.tensor_tensor(
                    part[:, 2, :], rest, part[:, 1, :], ALU.subtract), "qk_low")
                lows_done[chunk] = last["qk_low"] = low
                SP.wait(low)
                which, first = c // KC, (c % KC) * (P // HD)
                for s in range(PARTS):
                    part_free[j] = SP.dma(
                        qk_dram[which, b, first:first + P // HD, s if which == 0 else PARTS - 1 - s, :, :],
                        part[:, s, :], f"qk_store{j}")
                stored_qk[b, c] = part_free[j]
            for half in range(2):
                n, bank = ring_v.take(PE)
                for s in range(2):
                    tt = half * 2 + s
                    for k in range(KC):
                        m = PE.do(lambda e, k=k, tt=tt, s=s, bank=bank: e.matmul(
                            bank[:, s * D:(s + 1) * D], src[:, k, tt * P:(tt + 1) * P], w_qkv[:, k, 2 * D:3 * D],
                            start=(k == 0), stop=(k == KC - 1)), "v" if (s, k) == (1, KC - 1) else None)
                DVE.wait(m, v_free[0])
                got = DVE.do(lambda e, half=half, bank=bank: e.tensor_tensor(
                    v_out[0][:, 2 * half:2 * half + 2, :, 0:HD], bank.rearrange("p (s h d) -> p s h d", s=2, d=HD),
                    b_v.rearrange("p (h d) -> p h d", d=HD).unsqueeze(1).broadcast_to([P, 2, H, HD]), ALU.add), "v_add")
                ring_v.give(n, got)
            last["v_add"], last["v"] = got, m
            for _ in following:
                pass
            if b + 1 < B:
                turn(b + 1)
            xT_free[b % 2] = m
            SP.wait(got)
            v_free[0] = stored_v[b] = SP.dma(v_dram[b].rearrange("(t p) n -> p t n", p=P), v_out[0].rearrange("p t h d -> p t (h d)"),
                                                 "v_store")

        parts_done, lows_done, last = {}, {}, {}

        w_sb = weights[:, :].rearrange("p (e w) -> p e w", e=E)

        def load_weights(e_, m):
            w_loaded[e_, m] = ACTE.dma(
                w_sb[:, e_, m * EW // 2:(m + 1) * EW // 2].rearrange("p (c n) -> p c n", c=(KC, FC)[m]),
                t[("L0_ffn_w1", "L0_ffn_w2")[m]][e_].rearrange("(c p) n -> p c n", p=P), f"w_in{m}{e_}")

        w_loaded = {}

        def magnitude(e_, m):
            DVE.wait(w_loaded[e_, m])
            return DVE.do(lambda e: e.tensor_reduce(tops[:, m, e_:e_ + 1], w_sb[:, e_, m * EW // 2:(m + 1) * EW // 2],
                                                    AX.X, ALU.max, apply_absolute_value=True), "tops")

        matrices = [(e_, m) for e_ in [*range(E - LATE, E), *range(E - LATE)] for m in range(2)]
        EARLY = B
        STEPS_A_CHUNK = 8
        opening = iter(())
        whole(normalise(0))
        turn(0)
        DVE.wait(wqkv_loaded)
        bias_scaled = DVE.do(lambda e: e.tensor_scalar(b_qk[:, 0:KC], b_qk[:, 0:KC], SCALE, None, ALU.mult), "bias")
        DVE.do(lambda e: e.memset(v_out[0][:, :, :, HD:2 * HD], 1.0), "v_ones")
        for s in range(4):
            ones_set = DVE.do(lambda e, s=s: e.memset(k_st[s][STACK:P, :, :], 1.0), "ones_set")
        for tt in range(TT):
            POOL.do(lambda e, tt=tt: e.memset(b2_pad[tt], 0.0), "set")
        is_set = POOL.do(lambda e: e.memset(cw_pad, 0.0), "set")
        SP.wait(is_set)
        for tt in range(TT):
            b2_loaded = SP.dma(b2_pad[tt][32 * tt:32 * tt + E, :], t["L0_ffn_b2"], "b2_in")
        m = DVE.do(lambda e: e.memset(rows[:, :, :], 0.0), "spare")
        SP.wait(m)
        spare_rows = SP.dma(rows_dram[N:N + P, :], rows[:, 0, :], "spare_rows")
        SP.wait(spare_rows)
        spare_acc = SP.dma(acc_dram[N:N + P, :], rows[:, 0, 0:D], "spare_acc")

        FIRST_UNIT, OPEN = 2, 6
        for b in range(B):
            if b + 2 < B:
                load_x(b + 2)
            if b < EARLY:
                load_weights(*matrices[b])
            if b == OPEN:
                opening = open_attention()
            project(b)
            if FIRST_UNIT <= b < FIRST_UNIT + 3:
                whole(load_unit(b - FIRST_UNIT))
            if b < EARLY:
                tops_done = magnitude(*matrices[b])
                if b == 2 * LATE - 1:
                    lent_free = tops_done
        for _ in opening:
            pass
        banks_read = (xT_ready[B - 1], last["qk_32"], last["v_add"])
        a1_free = (last["v"], last["v_add"], last["qk_low"], *part_free, *v_free)

        S_TOP, S_SCALE, S_TMP, S_UNDO = stat[:, 0:8], stat[:, 8:12], stat[:, 16:24], stat[:, 24:28]
        UNDO_1, UNDO_2 = stat[:, 28:29], stat[:, 29:30]
        SCALE_W = [S_SCALE[:, 0:1], S_SCALE[:, 1:2]]
        SCALE_X, SCALE_H = S_SCALE[:, 2:3], S_SCALE[:, 3:4]

        def find_scales(tops_done):
            DVE.wait(vectors, tops_done)
            m = DVE.do(lambda e: e.tensor_reduce(S_TMP[:, 0:2], tops, AX.X, ALU.max), "scale")
            DVE.do(lambda e: e.tensor_reduce(S_TMP[:, 2:3], gamma, AX.X, ALU.max, apply_absolute_value=True), "scale")
            DVE.do(lambda e: e.tensor_reduce(S_TMP[:, 3:4], beta, AX.X, ALU.max, apply_absolute_value=True), "scale")
            m = DVE.do(lambda e: e.tensor_reduce(S_TMP[:, 4:5], b1_sb, AX.XY, ALU.max, apply_absolute_value=True), "scale")
            POOL.wait(m)
            m = POOL.do(lambda e: e.partition_all_reduce(S_TOP[:, 0:5], S_TMP[:, 0:5], P, bass.bass_isa.ReduceOp.max), "scale_all")
            DVE.wait(m)
            root = math.ceil(math.sqrt(D))
            m = DVE.do(lambda e: e.scalar_tensor_tensor(S_TOP[:, 2:3], S_TOP[:, 2:3], float(root), S_TOP[:, 3:4],
                                                        ALU.mult, ALU.add), "scale")
            DVE.wait(m)
            m = DVE.do(lambda e: e.scalar_tensor_tensor(S_TOP[:, 3:4], S_TOP[:, 2:3], float(D), S_TOP[:, 0:1],
                                                        ALU.mult, ALU.mult), "scale")
            DVE.wait(m)
            m = DVE.do(lambda e: e.tensor_tensor(S_TOP[:, 3:4], S_TOP[:, 3:4], S_TOP[:, 4:5], ALU.add), "scale")
            DVE.wait(m)
            m = DVE.do(lambda e: e.tensor_scalar(S_TMP[:, 0:4].bitcast(I32), S_TOP[:, 0:4].bitcast(I32), 23, None,
                                                 ALU.logical_shift_right), "scale")
            DVE.wait(m)
            m = DVE.do(lambda e: e.tensor_scalar(S_TMP[:, 0:4].bitcast(I32), S_TMP[:, 0:4].bitcast(I32), 80.0, 200.0,
                                                 ALU.max, ALU.min), "scale")
            DVE.wait(m)
            m = DVE.do(lambda e: e.tensor_scalar(S_TMP[:, 4:8].bitcast(I32), S_TMP[:, 0:4].bitcast(I32), -1.0,
                                                 float(127 * 2 + 14), ALU.mult, ALU.add), "scale")
            m2 = DVE.do(lambda e: e.tensor_scalar(S_TMP[:, 0:4].bitcast(I32), S_TMP[:, 0:4].bitcast(I32), -14.0, None,
                                                  ALU.add), "scale")
            DVE.wait(m, m2)
            DVE.do(lambda e: e.tensor_scalar(S_SCALE.bitcast(I32), S_TMP[:, 4:8].bitcast(I32), 23, None,
                                             ALU.logical_shift_left), "scale")
            m = DVE.do(lambda e: e.tensor_scalar(S_UNDO.bitcast(I32), S_TMP[:, 0:4].bitcast(I32), 23, None,
                                                 ALU.logical_shift_left), "scale")
            DVE.wait(m)
            DVE.do(lambda e: e.tensor_tensor(UNDO_1, S_UNDO[:, 0:1], S_UNDO[:, 2:3], ALU.mult), "scale")
            scales = DVE.do(lambda e: e.tensor_tensor(UNDO_2, S_UNDO[:, 1:2], S_UNDO[:, 3:4], ALU.mult), "scale")
            return scales

        def meet():
            marks = [(s, s.count) for s in pool.values() if s.count]
            for lane in LANES:
                lane.wait(*marks)
        ring_p = Ring([banks[:, n, :] for n in range(4, 7)], banks_read)
        ring_o = Ring([banks[:, 7, :]])

        def load_v(u):
            b, g = divmod(u, NG)
            own = slice(g * HG * 2 * HD, (g + 1) * HG * 2 * HD)
            SP.wait(vone_free[u % 2], stored_v[b])
            v_ready[u] = SP.dma(v_one[u % 2].rearrange("p t h d -> p t (h d)"),
                                v_dram[b].rearrange("(t p) n -> p t n", p=P)[:, :, own], f"v_in{u % 2}")

        def exponentials(u, h, pair):
            q, k = q_st[u % 4], k_st[u % 4]
            ROWS = STACK + MAXROWS
            if h == 0:
                PE.wait(top_loaded[u], ones_set)

            def block(h, out_, kt):
                return PE.do(lambda e: e.matmul(out_, k[0:ROWS, h, kt * P:kt * P + P], q[0:ROWS, h, kt * P:T],
                                                start=True, stop=True), "scores_T")

            slot = 2 * (pair % 3) + h % 2
            if h % 2 == 0:
                ACTE.wait(*pair_free[pair % 3], lent_free)
            for at, chunks in ((0, ((0, 0),)), (T, ((3, 0), (1, P)))):
                n, bank = ring_p.take(PE)
                for kt, to in chunks:
                    m = block(h, bank[:, to:to + T - kt * P], kt)
                ACTE.wait(m)
                m = ACTE.do(lambda e, at=at, bank=bank: e.activation(p_T[:, slot, at:at + T], bank, ACT.Exp), "exp")
                ring_p.give(n, m)
                yield
            if h % 2:
                n, bank = ring_p.take(PE)
                block(h - 1, bank[:, 0:2 * P], 2)
                st_free[u % 4] = m = block(h, bank[:, 2 * P:T], 2)
                ACTE.wait(m)
                m = ACTE.do(lambda e, bank=bank: e.activation(p_T[:, slot - 1:slot + 1, 2 * T:PT_LEN],
                                                              bank.rearrange("p (h c) -> p h c", h=2), ACT.Exp), "exp")
                ring_p.give(n, m)
                POOL.wait(m)
                both = p_T[:, slot - 1:slot + 1, :]
                for area, pattern in ((both[:, :, 0:P], [[0, 2], [1, P]]),
                                      (both[:, :, T:T + 2 * P], [[0, 2], [0, 2], [1, P]]),
                                      (both[:, :, 2 * T:2 * T + P], [[0, 2], [1, P]])):
                    m = POOL.do(lambda e, area=area, pattern=pattern: e.affine_select(
                        out=area, in_=area, compare_op=ALU.is_ge, fill=0.0, base=0, pattern=pattern,
                        channel_multiplier=-1), "masked")
                pair_ready[pair] = m
                yield

        def weigh(u):
            yield from rest(REST_P)
            b, g = divmod(u, NG)
            vv = v_one[u % 2]
            n, bank = ring_o.take(PE)
            PE.wait(v_ready[u], pair_ready[2 * u], pair_ready[2 * u + 1])
            for kt in range(TT):
                for h in range(HG):
                    slot = 2 * ((2 * u + h // 2) % 3) + h % 2
                    a, w = PT_AT[kt], T - kt * P
                    m = PE.do(lambda e, h=h, kt=kt, slot=slot, a=a, w=w: e.matmul(
                        bank[32 * h:32 * h + 32, kt * P:T], vv[:, kt, h, :], p_T[:, slot, a:a + w],
                        start=(kt == 0), stop=(kt == TT - 1), tile_position=(0, 32 * h)),
                        "weighed" if (kt, h) == (TT - 1, HG - 1) else None)
                if kt < TT - 1:
                    yield
            vone_free[u % 2] = m
            for pair in (2 * u, 2 * u + 1):
                pair_free[pair % 3] = (m,)
            ACTE.wait(m, o_turned[0])
            m = ACTE.do(lambda e: e.copy(o_T, bank), "o_T")
            ring_o.give(n, m)
            copied[u] = m

        copied, divided = {}, {}

        def divide(u):
            b, g = divmod(u, NG)
            while u not in copied:
                yield
            PE.wait(copied[u])
            n, bank = ring_s.take(PE)
            for qt in range(TT):
                m = PE.do(lambda e, qt=qt: e.transpose(bank[:, qt * P:qt * P + P], o_T[:, qt * P:qt * P + P], ident),
                          "o_turned" if qt == TT - 1 else None)
            o_turned[0] = m
            yield
            sums = bank.rearrange("p (t h d) -> p t h d", t=TT, h=HG)
            DVE.wait(m, o_rows_free[0], recip_free[0])
            m = DVE.do(lambda e: e.reciprocal(recip, sums[:, :, :, HD]), "divide")
            DVE.wait(m)
            m = DVE.do(lambda e: e.tensor_tensor(
                o_rows[:, :, g * HG * HD:(g + 1) * HG * HD].rearrange("p t (h d) -> p t h d", h=HG),
                sums[:, :, :, 0:HD], recip.unsqueeze(3).broadcast_to([P, TT, HG, HD]), ALU.mult), "divide")
            recip_free[0] = divided[u] = m
            ring_s.give(n, m)

        o_rows_free, recip_free = [None], [None]
        x_again, x2_free = {}, [None]
        rows_free, turned_free, z_free, cw_free = [spare_acc], [None], [None], [None]

        def load_again(b):
            SP.wait(x2_free[0])
            x_again[b] = SP.dma(x2, t["L0_attn_x"][b].rearrange("(t p) d -> p t d", p=P), "x_again")

        def over_tiles(vec):
            return vec.unsqueeze(1).broadcast_to([P, TT, vec.shape[1]])

        def column(c, n):
            return c.unsqueeze(2).broadcast_to([P, TT, n])

        def turn_rows(src, ready, name):
            PE.wait(ready)
            ACTE.wait(turned_free[0])
            for k in range(KC):
                n, bank = ring_s.take(PE)
                for tt in range(TT):
                    m = PE.do(lambda e, k=k, tt=tt, bank=bank: e.transpose(
                        bank[:, tt * P:(tt + 1) * P], src[:, tt, k * P:(k + 1) * P], ident), name if tt == TT - 1 else None)
                ACTE.wait(m)
                out = ACTE.do(lambda e, k=k, bank=bank: e.copy(turned[:, k, :], bank), "turned")
                ring_s.give(n, out)
                yield
            yield from rest(REST_TURN)
            return m, out

        def finish(b):
            POOL.wait(x_again[b])
            with_bias = POOL.do(lambda e: e.tensor_tensor(x2, x2, over_tiles(b_out), ALU.add), "with_bias")
            while (b + 1) * NG - 1 not in divided:
                yield
            o_rows_free[0], out = yield from turn_rows(o_rows, divided[(b + 1) * NG - 1], "rows_turned")
            PE.wait(out)
            for half in range(2):
                n, bank = ring_s.take(PE)
                for s in range(2):
                    tt = 2 * half + s
                    for k in range(KC):
                        m = PE.do(lambda e, k=k, tt=tt, s=s, bank=bank: e.matmul(
                            bank[:, s * D:(s + 1) * D], turned[:, k, tt * P:(tt + 1) * P], w_out[:, k, :],
                            start=(k == 0), stop=(k == KC - 1)), "w_out" if (s, k) == (1, KC - 1) else None)
                    if (half, s) == (1, 1):
                        turned_free[0] = m
                    yield
                DVE.wait(m, with_bias)
                got = DVE.do(lambda e, half=half, bank=bank: e.tensor_tensor(
                    x2[:, 2 * half:2 * half + 2, :], bank.rearrange("p (s d) -> p s d", s=2),
                    x2[:, 2 * half:2 * half + 2, :], ALU.add), "x2")
                ring_s.give(n, got)
            yield
            DVE.wait(got)
            for tt in range(TT):
                m = DVE.do(lambda e, tt=tt: e.bn_stats(moments[:, tt, :], x2[:, tt, :]), "norms")
                yield
            DVE.wait(m)
            for tt in range(TT):
                m = DVE.do(lambda e, tt=tt: e.bn_aggr(mean_var[:, tt, :], moments[:, tt, :]), "norms")
            yield
            (s1, s2), (y1, y2) = (newton[0][:, 0, :], newton[0][:, 1, :]), (newton[1][:, 0, :], newton[1][:, 1, :])
            DVE.wait(m)
            m = DVE.do(lambda e: e.tensor_scalar(s1, mean_var[:, :, 1], EPS, None, ALU.add), "norms")
            yield
            DVE.wait(m)
            m = DVE.do(lambda e: e.scalar_tensor_tensor(s2, s1, EPS, mean_var[:, :, 1], ALU.mult, ALU.add), "norms")
            yield
            m = yield from rsqrt(m, newton, "norms")
            yield
            DVE.wait(m)
            m = DVE.do(lambda e: e.scalar_tensor_tensor(shift, mean_var[:, :, 0], -1.0, y1, ALU.mult, ALU.mult), "norms")
            ACTE.wait(m, z_free[0])
            for tt in range(TT):
                z_done = ACTE.do(lambda e, tt=tt: e.activation(
                    z[:, tt, :], x2[:, tt, :], ACT.Identity, bias=shift[:, tt:tt + 1], scale=y1[:, tt:tt + 1]), "z")
            m = DVE.do(lambda e: e.tensor_tensor(rstd_z, s1, y1, ALU.mult), "norms")
            yield
            DVE.wait(m)
            m = DVE.do(lambda e: e.tensor_tensor(rstd_z, rstd_z, y2, ALU.mult), "norms")
            yield from rest(4)
            DVE.wait(z_done, m, *rows_free)
            for tt in range(TT):
                m = DVE.do(lambda e, tt=tt: e.scalar_tensor_tensor(
                    rows[:, tt, 0:D], z[:, tt, :], rstd_z[:, tt:tt + 1], gamma, ALU.mult, ALU.mult), "norms")
                yield
            lane = POOL if b + 1 < B else DVE
            lane.wait(m)
            normed = lane.do(lambda e: e.tensor_tensor(rows[:, :, 0:D], rows[:, :, 0:D], over_tiles(beta), ALU.add), "beta" if lane is POOL else "beta_last")
            yield
            POOL.wait(m)
            m = POOL.do(lambda e: e.tensor_tensor(z, z, x2, ALU.add), "residual")
            x2_free[0] = residual = m
            yield from rest(REST_BETA)
            _, out = yield from turn_rows(rows, normed, "gate_turned")
            PE.wait(out)
            n, bank = ring_s.take(PE)
            for tt in range(TT):
                for k in range(KC):
                    m = PE.do(lambda e, k=k, tt=tt, bank=bank: e.matmul(
                        bank[:, tt * E:(tt + 1) * E], turned[:, k, tt * P:(tt + 1) * P], gate_w[:, k, :],
                        start=(k == 0), stop=(k == KC - 1)), "gate" if (tt, k) == (TT - 1, KC - 1) else None)
            turned_free[0] = m
            if b + 1 < B:
                load_again(b + 1)
            yield
            DVE.wait(m)
            m = DVE.do(lambda e, bank=bank: e.tensor_copy(logit, bank[:, 0:TT * E].rearrange("p (t e) -> p t e", t=TT)), "choose")
            ring_s.give(n, m)
            step = [m]

            def then(emit):
                DVE.wait(step[0])
                step[0] = DVE.do(emit, "choose")

            first, second, gap, one, w1 = col[0:5]
            pick1, pick2 = choice[:, :, 0, :], choice[:, :, 1, :]
            DVE.wait(*routed[b - 1])
            for k, top_, src, pick in ((0, first, logit, pick1), (1, second, g2, pick2)):
                order = orders[:, :, k]
                then(lambda e, top_=top_, src=src: e.tensor_reduce(top_, src, AX.X, ALU.max))
                yield
                then(lambda e, top_=top_, src=src: e.tensor_tensor(g1, src, column(top_, E), ALU.is_ge))
                yield
                then(lambda e: e.tensor_tensor(g1, g1, over_tiles(prefer), ALU.mult))
                yield
                then(lambda e, order=order: e.tensor_reduce(order, g1, AX.X, ALU.max))
                yield
                then(lambda e, pick=pick, order=order: e.tensor_tensor(pick, g1, column(order, E), ALU.is_equal))
                yield
                if pick is pick1:
                    then(lambda e: e.scalar_tensor_tensor(g2, pick1, -3.0e38, logit, ALU.mult, ALU.add))
                    yield
            picked[b] = step[0]
            route_line.append(route(b))
            then(lambda e: e.tensor_tensor(gap, second, first, ALU.subtract))
            yield
            ACTE.wait(step[0])
            step[0] = ACTE.do(lambda e: e.activation(gap, gap, ACT.Exp), "gate_exp")
            yield from rest(3)
            then(lambda e: e.tensor_scalar(one, gap, 1.0, None, ALU.add))
            yield
            then(lambda e: e.reciprocal(w1, one))
            yield
            then(lambda e: e.tensor_tensor(gap, gap, w1, ALU.mult))
            yield
            then(lambda e: e.tensor_tensor(g1, pick1, column(w1, E), ALU.mult))
            yield
            then(lambda e: e.tensor_tensor(g2, pick2, column(gap, E), ALU.mult))
            yield
            DVE.wait(cw_free[0])
            then(lambda e: e.tensor_tensor(rows[:, :, D:ROW], g1, g2, ALU.add))
            yield
            then(lambda e: e.tensor_tensor(cw_pad[:, :, 0:E], g1, g2, ALU.add))
            yield
            yield from rest(REST_COUNT)
            SP.wait(step[0], normed)
            m = SP.dma(rows_dram[b * T:(b + 1) * T, :].rearrange("(t p) d -> p t d", p=P), rows, "rows_out")
            rows_free[:] = [m, out]
            PE.wait(step[0])
            n, bank = ring_s.take(PE)
            m = PE.do(lambda e, bank=bank: e.transpose(bank[:, 0:P], cw_pad.rearrange("p t e -> p (t e)"), ident), "cw_turned")
            cw_free[0] = m
            ACTE.wait(m)
            m = ACTE.do(lambda e, bank=bank: e.copy(cw_T, bank[:, 0:P]), "cw_T")
            ring_s.give(n, m)
            yield
            PE.wait(m, b2_loaded)
            DVE.wait(residual)
            for half in range(2):
                n, bank = ring_s.take(PE)
                for s in range(2):
                    m = PE.do(lambda e, s=s, bank=bank, tt=2 * half + s: e.matmul(
                        bank[:, s * D:(s + 1) * D], cw_T, b2_pad[tt], start=True, stop=True), "b2")
                yield
                DVE.wait(m)
                got = DVE.do(lambda e, half=half, bank=bank: e.tensor_tensor(
                    z[:, 2 * half:2 * half + 2, :], bank.rearrange("p (s d) -> p s d", s=2),
                    z[:, 2 * half:2 * half + 2, :], ALU.add), "base")
                ring_s.give(n, got)
            yield from rest(REST_COUNT)
            SP.wait(got)
            z_free[0] = SP.dma(acc_dram[b * T:(b + 1) * T, :].rearrange("(t p) d -> p t d", p=P), z, "acc_out")

        picked, routed = {}, {-1: ()}
        running_done = [numbers]

        def route(b):
            step = [picked[b]]

            def then(emit):
                DVE.wait(step[0])
                step[0] = DVE.do(emit, "route")

            DVE.wait(counted.get(b - 1))
            then(lambda e: e.tensor_tensor(chosen, choice[:, :, 0, :], choice[:, :, 1, :], ALU.add))
            yield from rest(REST_COUNT)
            PE.wait(step[0])
            n, bank = ring_s.take(PE)
            for tt in range(TT + 1):
                terms = [(ones_b, s) for s in range(tt)] + ([(upper_b, tt)] if tt < TT else [])
                for i, (which, s) in enumerate(terms):
                    m = PE.do(lambda e, tt=tt, which=which, s=s, i=i, bank=bank, count=len(terms): e.matmul(
                        bank[:, tt * E:(tt + 1) * E], which, chosen[:, s, :], start=(i == 0), stop=(i == count - 1)),
                        "counted" if (tt, s) == (TT, TT - 1) else None)
            counted[b] = m
            yield
            DVE.wait(m, running_done[0])
            then(lambda e, bank=bank: e.tensor_tensor(before, bank[:, 0:TT * E].rearrange("p (t e) -> p t e", e=E),
                                                      over_tiles(running), ALU.add))
            then(lambda e, bank=bank: e.tensor_tensor(running, running, bank[:, TT * E:(TT + 1) * E], ALU.add))
            ring_s.give(n, step[0])
            running_done[0] = counts_done[b] = step[0]
            yield
            then(lambda e: e.tensor_tensor(by_choice, choice, before.unsqueeze(2).broadcast_to([P, TT, TOPK, E]), ALU.mult))
            yield
            then(lambda e: e.tensor_reduce(rank, by_choice, AX.X, ALU.add))
            yield
            then(lambda e: e.tensor_copy(rank_int, rank))
            yield
            then(lambda e: e.tensor_scalar(rank_int, rank_int, P.bit_length() - 1, None, ALU.logical_shift_right))
            yield
            then(lambda e: e.tensor_copy(chunk_f, rank_int))
            yield
            then(lambda e: e.scalar_tensor_tensor(slot_row, chunk_f, float(-P), rank, ALU.mult, ALU.add))
            then(lambda e: e.scalar_tensor_tensor(slot_col, orders, float(-LOCAL), chunk_f, ALU.mult, ALU.add))
            routed[b] = (step[0],)
            slots_known = step[0]
            for tt in range(TT):
                yield
                DVE.wait(slots_known, in_table[0])
                for k in range(TOPK):
                    DVE.do(lambda e, tt=tt, k=k: e.tensor_scalar(
                        in_row[k], iota_16[:, E * LOCAL:], slot_row[:, tt, k:k + 1],
                        codes[:, b * TT + tt:b * TT + tt + 1], ALU.is_equal, ALU.mult), "one_hot")
                    m = DVE.do(lambda e, tt=tt, k=k: e.tensor_scalar(
                        in_col[k], iota_16[:, 0:E * LOCAL], slot_col[:, tt, k:k + 1], None, ALU.is_equal), "one_hot")
                yield from rest(REST_TABLE)
                PE.wait(m)
                n, bank = ring_s.take(PE)
                for k in range(TOPK):
                    m = PE.do(lambda e, k=k, bank=bank: e.matmul(bank[:, 0:E * LOCAL], in_row[k], in_col[k],
                                                                 start=(k == 0), stop=(k == TOPK - 1)), "table")
                in_table[0] = m
                yield
                DVE.wait(m, table_done[0])
                table_done[0] = DVE.do(lambda e, bank=bank: e.tensor_tensor(
                    table.rearrange("p e c -> p (e c)"), table.rearrange("p e c -> p (e c)"), bank[:, 0:E * LOCAL],
                    ALU.add), "in_table")
                ring_s.give(n, table_done[0])
            routed[b] = (slots_known, table_done[0])
            tables_done[b] = table_done[0]

        counts_done, tables_done = {}, {}
        counted, in_table, table_done = {}, [None], [None]
        route_line = []

        HALF = EW // 4
        w_16 = weights[:, :].bitcast(F16).rearrange("p (e m k s w) -> p e m k s w", e=E, m=2, k=2, s=2)
        split_free = [None, None]

        def split_weights(e_, m_, k_, high, low, LANE, pause):
            src = w_sb[:, e_, m_ * EW // 2 + k_ * HALF:m_ * EW // 2 + (k_ + 1) * HALF]
            ACTE.wait(scales, w_loaded[e_, m_])
            m = ACTE.do(lambda e: e.activation(src, src, ACT.Copy, scale=SCALE_W[m_]), "w_scaled")
            yield
            ACTE.wait(m, *split_free)
            m = ACTE.do(lambda e: e.copy(high, src), "w_high")
            yield
            if LANE is DVE:
                yield from rest(pause)
            LANE.wait(m)
            m = LANE.do(lambda e: e.tensor_tensor(low, src, high, ALU.subtract), "w_low" if LANE is POOL else "w_low_late")
            yield from rest(pause)
            DVE.wait(m)
            DVE.do(lambda e: e.tensor_copy(w_16[:, e_, m_, k_, 0, :], high), "w_split")
            m = DVE.do(lambda e: e.tensor_copy(w_16[:, e_, m_, k_, 1, :], low), "w_split")
            split_free[:] = [m, m]

        splits = [(e_, m_, k_) for e_ in range(E - LATE) for m_ in range(2) for k_ in range(2)]

        load_again(0)
        scales = None
        tops_line, load_line, weigh_line, divide_line, finish_line, split_line, place_line = ([] for _ in range(7))
        lines = (tops_line, load_line, weigh_line, divide_line, finish_line, route_line, place_line, split_line)

        def advance():
            for line in lines:
                if line and next(line[0], "done") == "done":
                    line.pop(0)

        for i in range(UNITS + 1):
            if i < UNITS:
                load_v(i)
            if i + 3 < UNITS:
                load_line.append(chain(rest(LOAD_FROM), load_unit(i + 3)))
            if i + 1 < UNITS:
                tops_line.append(place_maxima(i + 1))
            for h in range(HG):
                both = [maxima(i + 2, h) if i + 2 < UNITS else iter(()),
                        exponentials(i, h, 2 * i + h // 2) if i < UNITS else iter(())]
                for _ in range(3):
                    for part in both:
                        next(part, None)
                        advance()
                if h == 0 and i > 0:
                    weigh_line.append(weigh(i - 1))
                if h == 1 and i > 0:
                    divide_line.append(divide(i - 1))
                    if i % NG == 0:
                        finish_line.append(finish(i // NG - 1))
                if h == 2 and i + EARLY < len(matrices):
                    if matrices[i + EARLY][0] in MIDDLE:
                        ACTE.wait(*a1_free)
                    load_weights(*matrices[i + EARLY])
                if h == 3 and 0 < i <= len(matrices) - EARLY:
                    tops_done = magnitude(*matrices[i - 1 + EARLY])
                    if i == len(matrices) - EARLY:
                        scales = find_scales(tops_done)
                if h == 1 and i > len(matrices) - EARLY and splits:
                    split_line.append(split_weights(*splits.pop(0), w_high, w_low, POOL, REST_SPLIT))
        while splits:
            split_line.append(split_weights(*splits.pop(0), w_high, w_low, POOL, REST_SPLIT))
        ACTE.wait(*pair_free[0], *pair_free[1], *pair_free[2])
        for late in matrices[:2 * LATE]:
            load_weights(*late)
            for k_ in range(2):
                split_line.append(split_weights(*late, k_, w_high, w_low, DVE, REST_LATE))
        tiles_step = [None]

        def then3(emit):
            DVE.wait(tiles_step[0])
            tiles_step[0] = DVE.do(emit, "tiles")

        a3 = Area(arena, HEAD, HEAD + q_st[0].shape[1] * T // 2)
        tiles_int, first_chunk = a3.take(E, I32), a3.take(E, I32)
        tiles_e, ends, starts, ones_e = (a3.take(E) for _ in range(4))
        ended = a3.take(TILES * E, j=TILES, e=E)
        tile_f = a3.take(TILES)
        code = a3.take(SC + LOCAL)
        real, positive = a3.take(SC), a3.take(SC)
        spare, spare_code = a3.take(1), a3.take(1)

        def place_tiles():
            while B - 1 not in counts_done:
                yield
            DVE.wait(counts_done[B - 1], *st_free)
            then3(lambda e: e.memset(ones_e, 1.0))
            yield
            then3(lambda e: e.tensor_scalar(tiles_int, running, float(TILE - 1), None, ALU.add))
            yield
            then3(lambda e: e.tensor_scalar(tiles_int, tiles_int, TILE.bit_length() - 1, None, ALU.logical_shift_right))
            yield
            then3(lambda e: e.tensor_copy(tiles_e, tiles_int))
            yield
            then3(lambda e: e.tensor_tensor_scan(ends, ones_e, tiles_e, 0.0, ALU.mult, ALU.add))
            yield
            then3(lambda e: e.tensor_tensor(starts, ends, tiles_e, ALU.subtract))
            yield
            then3(lambda e: e.tensor_scalar(first_chunk, starts, float(TC), None, ALU.mult))
            yield
            then3(lambda e: e.tensor_tensor(ended, iota_16[:, E * LOCAL:E * LOCAL + TILES].unsqueeze(2).broadcast_to([P, TILES, E]),
                                            ends.unsqueeze(1).broadcast_to([P, TILES, E]), ALU.is_ge))
            yield
            then3(lambda e: e.tensor_reduce(tile_f, ended, AX.X, ALU.add))
            yield
            then3(lambda e: e.tensor_scalar(tile_f, tile_f, float(E - 1), None, ALU.min))
            yield
            then3(lambda e: e.tensor_copy(tile_of, tile_f))
            yield
            then3(lambda e: e.tensor_tensor(hot, iota_16[:, E * LOCAL:E * LOCAL + E].unsqueeze(1).broadcast_to([P, TILES, E]),
                                            tile_f.unsqueeze(2).broadcast_to([P, TILES, E]), ALU.is_equal))
            yield
            then3(lambda e: e.tensor_scalar(hot, hot, UNDO_2, None, ALU.mult))
            yield
            then3(lambda e: e.memset(code, 0.0))
            yield
            first = []
            DVE.wait(tiles_step[0])
            for e_ in range(E):
                DVE.do(lambda e, e_=e_: first.append(e.value_load(first_chunk[0:1, e_:e_ + 1], min_val=0, max_val=SC)))
                yield
            while B - 1 not in tables_done:
                yield
            DVE.wait(tables_done[B - 1])
            for e_ in range(E):
                then3(lambda e, e_=e_: e.tensor_copy(code[:, bass.ds(first[e_], LOCAL)], table[:, e_, :]))
                yield
            found = code[:, 0:SC]
            then3(lambda e: e.tensor_scalar(positive, found, 0.0, None, ALU.is_gt))
            yield
            then3(lambda e: e.tensor_scalar(real, found, 0.0, None, ALU.not_equal))
            yield
            then3(lambda e: e.tensor_tensor(found, found, positive, ALU.subtract))
            yield
            then3(lambda e: e.tensor_scalar(spare_code, iota_part, float(N // 2), None, ALU.add))
            yield
            then3(lambda e: e.tensor_scalar(spare, iota_part, float(N), None, ALU.add))
            yield
            then3(lambda e: e.tensor_scalar(found, found, spare_code, None, ALU.subtract))
            yield
            then3(lambda e: e.tensor_tensor(found, found, real, ALU.mult))
            yield
            then3(lambda e: e.tensor_scalar(found, found, spare, None, ALU.add))
            yield
            then3(lambda e: e.tensor_copy(slot_token, found))
            yield

        place_line.append(place_tiles())
        while any(lines):
            advance()

        meet()
        a4 = Area(arena, HEAD, WORDS)
        gathered = [a4.take(TC * ROW, c=TC, d=ROW) for _ in range(3)]
        xt_high = [a4.take(KC * TILE // 2, F16, k=KC, s=TILE) for _ in range(2)]
        xt_low = [a4.take(KC * TILE // 2, F16, k=KC, s=TILE) for _ in range(2)]
        w1_now = [a4.take(EW // 2, F16, k=KC, s=2, w=F) for _ in range(2)]
        w2_now = [a4.take(EW // 2, F16, k=2, s=2, c=FC // 2, n=D) for _ in range(2)]
        b1_now = [a4.take(FC) for _ in range(2)]
        h_32 = [a4.take(2 * TILE, c=2, s=TILE) for _ in range(2)]
        h_high = [a4.take(FC * TILE // 2, F16, c=FC, s=TILE) for _ in range(1)]
        h_low = [a4.take(FC * TILE // 2, F16, c=FC, s=TILE) for _ in range(1)]
        y = [a4.take(TC * D, c=TC, d=D) for _ in range(2)]
        share = a4.take(TC * E, c=TC, e=E)
        weight = [a4.take(TC) for _ in range(2)]
        ring_x = Ring([banks[:, 0, :]])
        ring_h = Ring([banks[:, n, :] for n in range(1, 6)])
        ring_y = Ring([banks[:, n, :] for n in range(6, 8)])

        gathered_free = [()] * 3
        gather_done, x_split, staged_1, staged_2, staged_b = {}, {}, {}, {}, {}
        xt_free, w1_free, w2_free, b1_free, y_free = [None] * 2, [None] * 2, [None] * 2, [None] * 2, [None] * 2
        h32_free, h_free = [None] * 2, [None]
        h_ready, added, weight_ready = {}, {}, {}
        h_count = 0

        def gather(j):
            s = j % 3
            POOL.wait(*gathered_free[s])
            for c in range(TC):
                gather_done[j] = POOL.indirect(f"gathered{s}", gathered[s][:, c, :], None, rows_dram[:, :],
                                               bass.IndirectOffsetOnAxis(slot_token[:, TC * j + c:TC * j + c + 1], 0))

        def stage_expert(j):
            s = j % 2
            DVE.wait(w1_free[s], w2_free[s], b1_free[s])

            box = []
            DVE.do(lambda e: box.append(e.value_load(tile_of[0:1, j:j + 1], min_val=0, max_val=E - 1)))
            flat = weights[:, :].bitcast(F16)
            staged_1[j] = DVE.do(lambda e: e.tensor_copy(w1_now[s].rearrange("p k s w -> p (k s w)"),
                                                         flat[:, bass.ds(box[0] * (2 * EW), EW)]), "staged")
            staged_b[j] = DVE.do(lambda e: e.tensor_copy(b1_now[s], b1_sb.rearrange("p e c -> p (e c)")[:, bass.ds(box[0] * FC, FC)]), "staged")
            staged_2[j] = DVE.do(lambda e: e.tensor_copy(w2_now[s].rearrange("p k s c n -> p (k s c n)"),
                                                         flat[:, bass.ds(box[0] * (2 * EW) + EW, EW)]), "staged")

        def turn_tokens(j):
            g = gathered[j % 3]
            PE.wait(gather_done[j])
            n, bank = ring_x.take(PE)
            for k in range(KC):
                for c in range(TC):
                    m = PE.do(lambda e, k=k, c=c: e.transpose(bank[:, k * TILE + c * P:k * TILE + (c + 1) * P],
                                                              g[:, c, k * P:(k + 1) * P], ident), "x_turned")
            turned_mark = m
            s = j % 2
            both = bank.rearrange("p (k s) -> p k s", k=KC)
            ACTE.wait(m, xt_free[s])
            m = ACTE.do(lambda e: e.activation(xt_high[s], both, ACT.Copy, scale=SCALE_X), "xt_high")
            DVE.wait(m)
            x_split[j] = DVE.do(lambda e: e.scalar_tensor_tensor(xt_low[s], both, SCALE_X, xt_high[s], ALU.mult, ALU.subtract), "xt_low")
            ring_x.give(n, x_split[j])
            DVE.wait(gather_done[j], y_weighted.get(j - 2))
            m = DVE.do(lambda e: e.tensor_tensor(share, g[:, :, D:ROW], hot[:, j:j + 1, :].broadcast_to([P, TC, E]), ALU.mult), "share")
            DVE.wait(m)
            weight_ready[j] = DVE.do(lambda e: e.tensor_reduce(weight[s], share, AX.X, ALU.add), "share")
            gathered_free[j % 3] = (turned_mark, m)

        y_weighted = {}

        def hidden(j):
            nonlocal h_count
            s = j % 2
            w1, xh, xl = w1_now[s], xt_high[s], xt_low[s]
            PE.wait(staged_1[j], x_split[j])
            for c2 in range(FC // 2):
                n, bank = ring_h.take(PE)
                for c in range(2):
                    f = (2 * c2 + c) * P
                    terms = [(k, wp, xp) for k in range(KC) for wp, xp in ((0, xh), (0, xl), (1, xh))]
                    for i, (k, wp, xp) in enumerate(terms):
                        m = PE.do(lambda e, k=k, wp=wp, xp=xp, f=f, c=c, i=i, bank=bank: e.matmul(
                            bank[:, c * TILE:(c + 1) * TILE], w1[:, k, wp, f:f + P], xp[:, k, :],
                            start=(i == 0), stop=(i == len(terms) - 1)), "hidden" if i == len(terms) - 1 else None)
                r = h_count % 2
                h_count += 1
                ACTE.wait(m, h32_free[r], staged_b[j])
                for c in range(2):
                    m2 = ACTE.do(lambda e, c=c, c2=c2, r=r, bank=bank: e.activation(
                        h_32[r][:, c, :], bank[:, c * TILE:(c + 1) * TILE], ACT.Gelu,
                        bias=b1_now[s][:, 2 * c2 + c:2 * c2 + c + 1], scale=UNDO_1), "gelu")
                ring_h.give(n, m2)
                DVE.wait(m2, h_free[0])
                m3 = DVE.do(lambda e, c2=c2, r=r: e.tensor_scalar(h_high[0][:, 2 * c2:2 * c2 + 2, :], h_32[r], SCALE_H, None,
                                                                  ALU.mult), "h_high")
                DVE.wait(m3)
                h_ready[j, c2] = h32_free[r] = DVE.do(lambda e, c2=c2, r=r: e.scalar_tensor_tensor(
                    h_low[0][:, 2 * c2:2 * c2 + 2, :], h_32[r], SCALE_H, h_high[0][:, 2 * c2:2 * c2 + 2, :], ALU.mult, ALU.subtract), "h_low")
            w1_free[s] = xt_free[s] = m
            b1_free[s] = m2

        def expert_out(j):
            s = j % 2
            w2 = w2_now[s]
            n, bank = ring_y.take(PE)
            PE.wait(staged_2[j])
            for c in range(TC):
                for f in range(FC):
                    PE.wait(h_ready[j, f // 2])
                    for i, (hp, wp) in enumerate(((h_high[0], 0), (h_high[0], 1), (h_low[0], 0))):
                        last = (f, i) == (FC - 1, 2)
                        m = PE.do(lambda e, f=f, c=c, i=i, hp=hp, wp=wp, last=last: e.matmul(
                            bank[:, c * D:(c + 1) * D], hp[:, f, c * P:(c + 1) * P],
                            w2[:, f // (FC // 2), wp, f % (FC // 2), :], start=(f == 0 and i == 0), stop=last),
                            "expert_out" if last else None)
            h_free[0] = w2_free[s] = m
            DVE.wait(m, y_free[s], weight_ready[j])
            for c in range(TC):
                m = DVE.do(lambda e, c=c: e.tensor_scalar(y[s][:, c, :], bank[:, c * D:(c + 1) * D], weight[s][:, c:c + 1], None,
                                                          ALU.mult), "y")
            ring_y.give(n, m)
            y_weighted[j] = m
            POOL.wait(m, added.get(j - 1))
            for c in range(TC):
                if c:
                    POOL.wait(added[j])
                added[j] = POOL.indirect("added", acc_dram[:, :], bass.IndirectOffsetOnAxis(slot_token[:, TC * j + c:TC * j + c + 1], 0),
                                         y[s][:, c, :], None, compute_op=ALU.add)
            y_free[s] = added[j]

        for j in range(2):
            gather(j)
        stage_expert(0)
        turn_tokens(0)
        hidden(0)
        for j in range(TILES):
            if j + 2 < TILES:
                gather(j + 2)
            if j + 1 < TILES:
                stage_expert(j + 1)
                turn_tokens(j + 1)
            expert_out(j)
            if j + 1 < TILES:
                hidden(j + 1)

        SP.wait(added[TILES - 1])
        done = SP.dma(t["out"].rearrange("b t d -> (b t) d"), acc_dram[0:N, :], "out")
        SP.wait(done)
        block = ctx.enter_context(nc.Block())
        for lane, where in zip(LANES, (block.tensor, block.scalar, block.vector, block.gpsimd, block.sync)):
            where(lambda engine, lane=lane: lane.play(engine))


_INS = ["L0_attn_x", "L0_attn_W_qkv", "L0_attn_b_qkv", "L0_attn_W_out", "L0_attn_b_out", "L0_ffn_gate_w",
        "L0_ffn_w1", "L0_ffn_b1", "L0_ffn_w2", "L0_ffn_b2", "L0_ffn_gamma", "L0_ffn_beta"]


def kernel(**inputs):
    import numpy as np
    from concourse import bacc
    from concourse.bass_utils import run_bass_kernel_spmd

    nc = bacc.Bacc("TRN2", target_bir_lowering=False, num_devices=1)
    arrays, tensors = {}, {}
    for name in _INS:
        a = np.ascontiguousarray(inputs[name])
        arrays[f"in_{name}"] = a
        tensors[name] = nc.dram_tensor(f"in_{name}", a.shape, mybir.dt.from_np(a.dtype), kind="ExternalInput").ap()
    shape = inputs["L0_attn_x"].shape
    tensors["out"] = nc.dram_tensor("out", shape, F32, kind="ExternalOutput").ap()
    build(nc, tensors)
    got = run_bass_kernel_spmd(nc, [arrays], core_ids=[0])
    return got.results[0]["out"]
```
